# Optimizing a Trainium2 kernel written in Bass

```python
import numpy as np
import jax
import jax.numpy as jnp

def _softmax(x, axis=-1):
    return jax.nn.softmax(x, axis=axis)

def _gelu(x):
    return jax.nn.gelu(x, approximate=True)

def _silu(x):
    return jax.nn.silu(x)

def _sigmoid(x):
    return jax.nn.sigmoid(x)

def _layernorm(x, axis=-1, eps=1e-05):
    m = jnp.mean(x, axis=axis, keepdims=True)
    v = jnp.var(x, axis=axis, keepdims=True)
    return (x - m) / jnp.sqrt(v + eps)

def _scatter_add(tgt, idx, src, axis=0):
    return tgt.at[idx].add(src)

def _segment_sum(src, seg, n):
    return jax.ops.segment_sum(src, seg, n)
kernel_name = 'mk_early_fusion_d2_tok_img1024_r4_0b6a85'

def setup_inputs(seed: int=0):
    np.random.seed(seed)
    _w = jnp.asarray

    def _rec_inputs():
        import jax
        import jax.numpy as jnp
        _rk = jax.random.key(seed)
        x = jax.random.uniform(jax.random.fold_in(_rk, 1), (16, 3, 256, 256), jnp.float32, 0.0, 1)
        txt = 2.40575 + 1.24603 * jax.random.normal(jax.random.fold_in(_rk, 2), (16, 77, 256), jnp.float32)
        return (x, txt)
    x, txt = _rec_inputs()

    def _L0_tok_setup():
        import jax, jax.numpy as jnp
        import numpy as np
        _GRAY_W = (0.2989, 0.587, 0.114)
        key = jax.random.key(seed)
        x = jax.random.uniform(key, (32, 3, 256, 256), dtype=jnp.float32)
        sx = jnp.array([[-3.0, 0.0, 3.0], [-10.0, 0.0, 10.0], [-3.0, 0.0, 3.0]], dtype=jnp.float32)
        scharr = jnp.stack([sx, sx.T])[:, None, :, :]
        return {'x': x, 'scharr': scharr}
    _L0_tok_all = _L0_tok_setup()
    _L0_tok_in = {k: v for k, v in _L0_tok_all.items() if k in ('scharr',)}
    del _L0_tok_all

    def _L0_attn_setup():
        import math
        import jax, jax.numpy as jnp
        import numpy as np
        D_MODEL = 256
        N_HEADS = 16
        D_K = D_MODEL // N_HEADS
        D_C = 64
        B, S = (2, 512)
        key = jax.random.key(seed)
        ks = jax.random.split(key, 7)
        sd = lambda fan_in: 1.0 / math.sqrt(fan_in)
        return {'x': jax.random.normal(ks[0], (B, S, D_MODEL), dtype=jnp.float32), 'W_dq': jax.random.uniform(ks[1], (D_MODEL, D_C), minval=-sd(D_MODEL), maxval=sd(D_MODEL), dtype=jnp.float32), 'W_uq': jax.random.uniform(ks[2], (D_C, N_HEADS * D_K), minval=-sd(D_C), maxval=sd(D_C), dtype=jnp.float32), 'W_dkv': jax.random.uniform(ks[3], (D_MODEL, D_C), minval=-sd(D_MODEL), maxval=sd(D_MODEL), dtype=jnp.float32), 'W_uk': jax.random.uniform(ks[4], (D_C, N_HEADS * D_K), minval=-sd(D_C), maxval=sd(D_C), dtype=jnp.float32), 'W_uv': jax.random.uniform(ks[5], (D_C, N_HEADS * D_K), minval=-sd(D_C), maxval=sd(D_C), dtype=jnp.float32), 'W_o': jax.random.uniform(ks[6], (N_HEADS * D_K, D_MODEL), minval=-sd(N_HEADS * D_K), maxval=sd(N_HEADS * D_K), dtype=jnp.float32)}
    _L0_attn_all = _L0_attn_setup()
    _L0_attn_in = {k: v for k, v in _L0_attn_all.items() if k in ('W_dq', 'W_uq', 'W_dkv', 'W_uk', 'W_uv', 'W_o')}
    del _L0_attn_all

    def _L0_ffn_setup():
        import jax, jax.numpy as jnp
        import numpy as np
        HIDDEN = 256
        FF = 1024
        N_EXPERTS = 8
        CAP_FACTOR = 1.0
        B, S = (4, 512)
        STD = 0.02

        def _gelu(x):
            return x * 0.5 * (1.0 + jax.lax.erf(x / 1.41421))
        key = jax.random.key(seed)
        ks = jax.random.split(key, 6)
        x = jax.random.normal(ks[0], (B, S, HIDDEN), dtype=jnp.float32)
        W_sw = jax.random.normal(ks[1], (HIDDEN, N_EXPERTS), dtype=jnp.float32) * STD
        b_sw = jnp.zeros((N_EXPERTS,), dtype=jnp.float32)
        W1 = jax.random.normal(ks[2], (N_EXPERTS, HIDDEN, FF), dtype=jnp.float32) * STD
        b1 = jnp.zeros((N_EXPERTS, FF), dtype=jnp.float32)
        W2 = jax.random.normal(ks[3], (N_EXPERTS, FF, HIDDEN), dtype=jnp.float32) * STD
        b2 = jnp.zeros((N_EXPERTS, HIDDEN), dtype=jnp.float32)
        return {'x': x, 'W_sw': W_sw, 'b_sw': b_sw, 'W1': W1, 'b1': b1, 'W2': W2, 'b2': b2}
    _L0_ffn_all = _L0_ffn_setup()
    _L0_ffn_in = {k: v for k, v in _L0_ffn_all.items() if k in ('W_sw', 'b_sw', 'W1', 'b1', 'W2', 'b2')}
    del _L0_ffn_all

    def _L1_attn_setup():
        import jax, jax.numpy as jnp
        import numpy as np
        D_MODEL = 256
        N_HEADS = 16
        N_KV = 4
        HD = D_MODEL // N_HEADS
        N_REP = N_HEADS // N_KV
        WINDOW = 128
        SCALE = HD ** (-0.5)
        B, T = (2, 512)

        def _rope(x):
            t = x.shape[2]
            hd = x.shape[-1]
            inv_freq = 1.0 / 10000.0 ** (jnp.arange(0, hd, 2, dtype=jnp.float32) / hd)
            freqs = jnp.arange(t, dtype=jnp.float32)[:, None] * inv_freq[None, :]
            cos = jnp.cos(freqs)[None, None]
            sin = jnp.sin(freqs)[None, None]
            x1, x2 = (x[..., :hd // 2], x[..., hd // 2:])
            return jnp.concatenate([x1 * cos - x2 * sin, x1 * sin + x2 * cos], axis=-1)
        key = jax.random.key(seed)
        ks = jax.random.split(key, 6)
        s = 0.02
        return {'query': jax.random.normal(ks[0], (B, T, D_MODEL), dtype=jnp.float32), 'Wq': jax.random.normal(ks[1], (D_MODEL, D_MODEL), dtype=jnp.float32) * s, 'Wk': jax.random.normal(ks[2], (N_KV * HD, D_MODEL), dtype=jnp.float32) * s, 'Wv': jax.random.normal(ks[3], (N_KV * HD, D_MODEL), dtype=jnp.float32) * s, 'W1': jax.random.normal(ks[4], (4 * D_MODEL, D_MODEL), dtype=jnp.float32) * s, 'W2': jax.random.normal(ks[5], (D_MODEL, 4 * D_MODEL), dtype=jnp.float32) * s}
    _L1_attn_all = _L1_attn_setup()
    _L1_attn_in = {k: v for k, v in _L1_attn_all.items() if k in ('Wq', 'Wk', 'Wv', 'W1', 'W2')}
    del _L1_attn_all

    def _L1_ffn_setup():
        import jax, jax.numpy as jnp
        import numpy as np
        DIM = 256
        NUM_EXPERTS = 6
        TOP_K = 2
        HIDDEN = DIM * 2
        key = jax.random.key(seed)
        ks = jax.random.split(key, 7)
        s_in = 1.0 / np.sqrt(DIM)
        s_h = 1.0 / np.sqrt(HIDDEN)
        x = jax.random.normal(ks[0], (4, 512, DIM), dtype=jnp.float32)
        Wg = jax.random.uniform(ks[1], (DIM, NUM_EXPERTS), jnp.float32, -s_in, s_in)
        bg = jax.random.uniform(ks[2], (NUM_EXPERTS,), jnp.float32, -s_in, s_in)
        W1 = jax.random.uniform(ks[3], (NUM_EXPERTS, DIM, HIDDEN), jnp.float32, -s_in, s_in)
        b1 = jax.random.uniform(ks[4], (NUM_EXPERTS, HIDDEN), jnp.float32, -s_in, s_in)
        W2 = jax.random.uniform(ks[5], (NUM_EXPERTS, HIDDEN, DIM), jnp.float32, -s_h, s_h)
        b2 = jax.random.uniform(ks[6], (NUM_EXPERTS, DIM), jnp.float32, -s_h, s_h)
        return {'x': x, 'Wg': Wg, 'bg': bg, 'W1': W1, 'b1': b1, 'W2': W2, 'b2': b2}
    _L1_ffn_all = _L1_ffn_setup()
    _L1_ffn_in = {k: v for k, v in _L1_ffn_all.items() if k in ('Wg', 'bg', 'W1', 'b1', 'W2', 'b2')}
    del _L1_ffn_all
    return {'x': x, 'txt': txt, 'L0_tok_scharr': _L0_tok_in['scharr'], 'L0_attn_W_dq': _L0_attn_in['W_dq'], 'L0_attn_W_uq': _L0_attn_in['W_uq'], 'L0_attn_W_dkv': _L0_attn_in['W_dkv'], 'L0_attn_W_uk': _L0_attn_in['W_uk'], 'L0_attn_W_uv': _L0_attn_in['W_uv'], 'L0_attn_W_o': _L0_attn_in['W_o'], 'L0_ffn_W_sw': _L0_ffn_in['W_sw'], 'L0_ffn_b_sw': _L0_ffn_in['b_sw'], 'L0_ffn_W1': _L0_ffn_in['W1'], 'L0_ffn_b1': _L0_ffn_in['b1'], 'L0_ffn_W2': _L0_ffn_in['W2'], 'L0_ffn_b2': _L0_ffn_in['b2'], 'L1_attn_Wq': _L1_attn_in['Wq'], 'L1_attn_Wk': _L1_attn_in['Wk'], 'L1_attn_Wv': _L1_attn_in['Wv'], 'L1_attn_W1': _L1_attn_in['W1'], 'L1_attn_W2': _L1_attn_in['W2'], 'L1_ffn_Wg': _L1_ffn_in['Wg'], 'L1_ffn_bg': _L1_ffn_in['bg'], 'L1_ffn_W1': _L1_ffn_in['W1'], 'L1_ffn_b1': _L1_ffn_in['b1'], 'L1_ffn_W2': _L1_ffn_in['W2'], 'L1_ffn_b2': _L1_ffn_in['b2']}

def reference(x, txt, L0_tok_scharr, L0_attn_W_dq, L0_attn_W_uq, L0_attn_W_dkv, L0_attn_W_uk, L0_attn_W_uv, L0_attn_W_o, L0_ffn_W_sw, L0_ffn_b_sw, L0_ffn_W1, L0_ffn_b1, L0_ffn_W2, L0_ffn_b2, L1_attn_Wq, L1_attn_Wk, L1_attn_Wv, L1_attn_W1, L1_attn_W2, L1_ffn_Wg, L1_ffn_bg, L1_ffn_W1, L1_ffn_b1, L1_ffn_W2, L1_ffn_b2):
    import jax
    import jax.numpy as jnp

    def _L0_tok_ref(x, scharr):
        import jax, jax.numpy as jnp
        import numpy as np
        _GRAY_W = (0.2989, 0.587, 0.114)
        w = jnp.asarray(_GRAY_W, dtype=x.dtype)
        gray = jnp.einsum('bchw,c->bhw', x, w)[:, None]
        edges = jax.lax.conv_general_dilated(gray, scharr, window_strides=(1, 1), padding='SAME', dimension_numbers=('NCHW', 'OIHW', 'NCHW'))
        abs_edges = jnp.sqrt(jnp.square(edges))
        edge = abs_edges.sum(axis=1) / 2
        return edge

    def _L0_attn_ref(x, W_dq, W_uq, W_dkv, W_uk, W_uv, W_o):
        import math
        import jax, jax.numpy as jnp
        import numpy as np
        D_MODEL = 256
        N_HEADS = 16
        D_K = D_MODEL // N_HEADS
        D_C = 64
        B, S = (2, 512)
        Bx, Sx, _ = x.shape
        c_q = x @ W_dq
        Q = (c_q @ W_uq).reshape(Bx, Sx, N_HEADS, D_K)
        c_kv = x @ W_dkv
        K = (c_kv @ W_uk).reshape(Bx, Sx, N_HEADS, D_K)
        V = (c_kv @ W_uv).reshape(Bx, Sx, N_HEADS, D_K)
        scores = jnp.einsum('bqhd,bkhd->bhqk', Q, K) / math.sqrt(D_K)
        causal = jnp.tril(jnp.ones((Sx, Sx), dtype=bool))
        scores = jnp.where(causal, scores, -jnp.inf)
        attn = jax.nn.softmax(scores, axis=-1)
        out = jnp.einsum('bhqk,bkhd->bqhd', attn, V).reshape(Bx, Sx, N_HEADS * D_K)
        return out @ W_o

    def _L0_ffn_ref(x, W_sw, b_sw, W1, b1, W2, b2):
        import jax, jax.numpy as jnp
        import numpy as np
        HIDDEN = 256
        FF = 1024
        N_EXPERTS = 8
        CAP_FACTOR = 1.0
        B, S = (4, 512)
        STD = 0.02

        def _gelu(x):
            return x * 0.5 * (1.0 + jax.lax.erf(x / 1.41421))
        Bb, Ss, D = x.shape
        T = Bb * Ss
        E = W1.shape[0]
        capacity = int(CAP_FACTOR * T / E)
        xf = x.reshape(T, D)
        logits = xf @ W_sw + b_sw
        probs = jax.nn.softmax(logits, axis=-1)
        pmax = jnp.max(probs, axis=-1)
        routes = jnp.argmax(probs, axis=-1)
        factor = pmax / jax.lax.stop_gradient(pmax)
        xs = xf * factor[:, None]
        onehot = jax.nn.one_hot(routes, E, dtype=jnp.int32)
        pos = jnp.cumsum(onehot, axis=0) - 1
        pos_tok = jnp.take_along_axis(pos, routes[:, None], axis=1)[:, 0]
        keep = pos_tok < capacity
        pos_safe = jnp.where(keep, pos_tok, capacity)
        buf = jnp.zeros((E, capacity + 1, D), dtype=xs.dtype)
        buf = buf.at[routes, pos_safe].set(xs)
        buf = buf[:, :capacity]
        h = _gelu(jnp.einsum('ecd,edf->ecf', buf, W1) + b1[:, None, :])
        expert_out = jnp.einsum('ecf,efd->ecd', h, W2) + b2[:, None, :]
        gathered = expert_out[routes, jnp.minimum(pos_tok, capacity - 1)]
        final = jnp.where(keep[:, None], gathered, xs)
        return final.reshape(Bb, Ss, D)

    def _L1_attn_ref(query, Wq, Wk, Wv, W1, W2):
        import jax, jax.numpy as jnp
        import numpy as np
        D_MODEL = 256
        N_HEADS = 16
        N_KV = 4
        HD = D_MODEL // N_HEADS
        N_REP = N_HEADS // N_KV
        WINDOW = 128
        SCALE = HD ** (-0.5)
        B, T = (2, 512)

        def _rope(x):
            t = x.shape[2]
            hd = x.shape[-1]
            inv_freq = 1.0 / 10000.0 ** (jnp.arange(0, hd, 2, dtype=jnp.float32) / hd)
            freqs = jnp.arange(t, dtype=jnp.float32)[:, None] * inv_freq[None, :]
            cos = jnp.cos(freqs)[None, None]
            sin = jnp.sin(freqs)[None, None]
            x1, x2 = (x[..., :hd // 2], x[..., hd // 2:])
            return jnp.concatenate([x1 * cos - x2 * sin, x1 * sin + x2 * cos], axis=-1)
        b, t, _ = query.shape
        q = (query @ Wq.T).reshape(b, t, N_HEADS, HD).transpose(0, 2, 1, 3)
        k = (query @ Wk.T).reshape(b, t, N_KV, HD).transpose(0, 2, 1, 3)
        v = (query @ Wv.T).reshape(b, t, N_KV, HD).transpose(0, 2, 1, 3)
        q = _rope(q)
        k = _rope(k)
        k = jnp.repeat(k, N_REP, axis=1)
        v = jnp.repeat(v, N_REP, axis=1)
        scores = jnp.einsum('bhqd,bhkd->bhqk', q, k) * SCALE
        i = jnp.arange(t)[:, None]
        j = jnp.arange(t)[None, :]
        mask = (j > i) | (j < i - (WINDOW - 1))
        scores = jnp.where(mask[None, None], jnp.float32(-1e+30), scores)
        attn = jax.nn.softmax(scores, axis=-1)
        out = jnp.einsum('bhqk,bhkd->bhqd', attn, v)
        out = out.transpose(0, 2, 1, 3).reshape(b, t, D_MODEL)
        h = out @ W1.T
        h = h * jax.nn.sigmoid(h)
        return h @ W2.T

    def _L1_ffn_ref(x, Wg, bg, W1, b1, W2, b2):
        import jax, jax.numpy as jnp
        import numpy as np
        DIM = 256
        NUM_EXPERTS = 6
        TOP_K = 2
        HIDDEN = DIM * 2
        gate_logits = jnp.einsum('bsd,de->bse', x, Wg) + bg
        topk_w, topk_idx = jax.lax.top_k(gate_logits, TOP_K)
        topk_w = jax.nn.softmax(topk_w, axis=-1)
        combine = jnp.sum(jax.nn.one_hot(topk_idx, NUM_EXPERTS, dtype=x.dtype) * topk_w[..., None], axis=-2)
        h = jnp.einsum('bsd,edh->ebsh', x, W1) + b1[:, None, None, :]
        h = jax.nn.gelu(h, approximate=False)
        y = jnp.einsum('ebsh,ehd->ebsd', h, W2) + b2[:, None, None, :]
        out = jnp.einsum('ebsd,bse->bsd', y, combine)
        return out
    h = _L0_tok_ref(x, L0_tok_scharr)
    h = jnp.concatenate([h, txt], axis=1)
    h = h + _L0_attn_ref(_layernorm(h, axis=-1), L0_attn_W_dq, L0_attn_W_uq, L0_attn_W_dkv, L0_attn_W_uk, L0_attn_W_uv, L0_attn_W_o)
    h = h + _L0_ffn_ref(_layernorm(h, axis=-1), L0_ffn_W_sw, L0_ffn_b_sw, L0_ffn_W1, L0_ffn_b1, L0_ffn_W2, L0_ffn_b2)
    h = h + _L1_attn_ref(_layernorm(h, axis=-1), L1_attn_Wq, L1_attn_Wk, L1_attn_Wv, L1_attn_W1, L1_attn_W2)
    h = h + _L1_ffn_ref(_layernorm(h, axis=-1), L1_ffn_Wg, L1_ffn_bg, L1_ffn_W1, L1_ffn_b1, L1_ffn_W2, L1_ffn_b2)
    return h

_drawn_inputs = setup_inputs


def setup_inputs(seed=0):
    import zlib

    import numpy as np

    out = dict(_drawn_inputs(seed))
    spreads = {'L0_ffn_b_sw': (0.0, 0.1), 'L0_ffn_b1': (0.0, 0.661), 'L0_ffn_b2': (0.0, 0.1)}
    factors = {'L0_attn_W_dq': 4.336,
     'L0_attn_W_uq': 5.608,
     'L0_attn_W_uk': 6.384,
     'L1_attn_Wq': 8.0,
     'L1_attn_Wk': 8.0,
     'L1_attn_Wv': 8.0,
     'L1_attn_W1': 8.0,
     'L1_attn_W2': 8.0,
     'L1_ffn_bg': 45.984,
     'L1_ffn_b1': 64.0,
     'L1_ffn_b2': 58.075,
     'L1_ffn_Wg': 5.257,
     'L1_ffn_W1': 7.707,
     'L1_ffn_W2': 6.515}
    for name, (base, spread) in spreads.items():
        noise = np.random.default_rng([zlib.crc32(name.encode()), seed]).standard_normal(out[name].shape)
        drawn = base * np.exp(spread * noise) if base else spread * noise
        out[name] = jnp.asarray(drawn.astype(out[name].dtype))
    for name, factor in factors.items():
        out[name] = (out[name] * factor).astype(out[name].dtype)
    return out
```

```python
from contextlib import ExitStack

import numpy as np

import concourse.bass as bass
from concourse import mybir

F32 = mybir.dt.float32
F32R = mybir.dt.float32r
BF16 = mybir.dt.bfloat16
I32 = mybir.dt.int32
ALU = mybir.AluOpType
ACT = mybir.ActivationFunctionType
AX = mybir.AxisListType

P = 128
TT = 111
NT = 3
S = TT * NT
SP1 = S + 1
SCALE = 0.25
MASKED = -1e30
EPS = 1e-5


class Ring:

    def __init__(self, banks, units):
        self.banks, self.names, self.who = banks, [u for u, _ in units], [w for _, w in units]
        self.at = {u: k for k, u in enumerate(self.names)}
        self.real = sum(1 for w in self.who if w)
        self.per = {e: sum(e in w for w in self.who) for e in "AD"}
        assert len(units) % banks == 0

    def bank(self, unit):
        return self.at[unit] % self.banks

    def filled(self, rnd, unit):
        return rnd * self.real + sum(1 for w in self.who[: self.at[unit] + 1] if w)

    def drained(self, rnd, k, engine):
        return (rnd + 1) * self.per[engine] + sum(engine in w for w in self.who[: k + 1])

    def before(self, rnd, unit):
        k, back = self.at[unit] - self.banks, 0
        while not self.who[k % len(self.who)]:
            k -= self.banks
        while k < 0:
            k, back = k + len(self.who), back + 1
        return [(e, self.drained(rnd - back, k, e)) for e in self.who[k]]


def flat(ap):
    return ap.rearrange("p a b -> p (a b)")


def credit(eng, sem, n):
    eng.sem_inc(sem, n)


def load_and_cut_image(nc, sb, ps, sem, x, txt, scharr, h):
    B = x.shape[0]
    ROW0 = [0, 110, 128]
    OFF = [-1, 0, 93]
    ROWS = [TT, TT, 256 - 2 * TT]
    taps = sb("taps", [P, 18], F32)
    diag = sb("diag", [P, 3, NT, TT], F32)
    band = sb("band", [P, 6, NT, TT], F32)
    band_hi = sb("band_hi", [P, 6, NT, TT], F32R)
    band_lo = sb("band_lo", [P, 6, NT, TT], F32R)
    img = [sb(f"img{t}", [P, 3, 256], F32) for t in range(NT)]
    red = [sb(f"red{t}", [P, 256], F32) for t in range(NT)]
    redgreen = [sb(f"redgreen{t}", [P, 256], F32) for t in range(NT)]
    gray = [sb(f"gray{t}", [P, 258], F32) for t in range(NT)]
    gray_hi = [sb(f"gray_hi{t}", [P, 258], F32R) for t in range(NT)]
    gray_lo = [sb(f"gray_lo{t}", [P, 258], F32R) for t in range(NT)]
    halves = [sb(f"halves{t}", [TT, 512], F32) for t in range(NT)]
    edge_ps = [ps(f"edge_ps{t}", [P, 512], F32) for t in range(NT)]

    taps_loaded, txt_loaded = sem("taps_loaded"), sem("txt_loaded")
    diag_made, band_step, band_high = sem("diag_made"), sem("band_step"), sem("band_high")
    img_loaded = [sem(f"img_loaded{t}") for t in range(NT)]
    red_scaled, gray_step, gray_made = sem("red_scaled"), sem("gray_step"), sem("gray_made")
    gray_high, gray_low, edges_summed = sem("gray_high"), sem("gray_low"), sem("edges_summed")
    halves_made, edges_added, pads_zeroed = sem("halves_made"), sem("edges_added"), sem("pads_zeroed")

    with nc.Block() as block:

        @block.sync
        def _(sp):
            sp.dma_start(taps[:], scharr.rearrange("o i y x -> (i o y x)").partition_broadcast(P)).then_inc(taps_loaded, 16)
            sp.dma_start(h[ROWS[2]:TT, 2::NT, :], txt.rearrange("b r d -> r b d")).then_inc(txt_loaded, 16)
            with sp.Fori(0, B) as b:
                for t in range(NT):
                    sp.wait_ge(gray_made, NT * b + t + 1)
                    sp.dma_start(img[t][:], x[bass.ds(b, 1), :, ROW0[t]:ROW0[t] + P, :]
                                 .rearrange("b c p w -> p (b c) w")).then_inc(img_loaded[t], 16)
            sp.wait_ge(txt_loaded, 16)

        @block.gpsimd
        def _(pool):
            pool.memset(diag[:], 1.0).then_inc(diag_made, 1)
            pool.wait_ge(diag_made, 1)
            for k in range(3):
                for t in range(NT):
                    pool.affine_select(out=diag[:, k, t, :], in_=diag[:, k, t, :], compare_op=ALU.is_equal,
                                       fill=0.0, base=-(OFF[t] + k), pattern=[[-1, TT]],
                                       channel_multiplier=1).then_inc(diag_made, 1)

        @block.scalar
        def _(act):
            act.wait_ge(band_step, 18)
            act.copy(band_hi[:], band[:]).then_inc(band_high, 1)
            credit(act, halves_made, NT)
            act.wait_ge(pads_zeroed, 2 * NT)
            with act.Fori(0, B) as b:
                def whiten(t):
                    act.wait_ge(img_loaded[t], 16 * b + 16)
                    act.activation(red[t][:], img[t][:, 0, :], ACT.Copy, scale=0.2989).then_inc(red_scaled, 1)

                def high(t):
                    act.wait_ge(gray_made, NT * (b + 1) + t + 1)
                    act.wait_ge(edges_summed, NT * b + t + 1)
                    act.copy(gray_hi[t][:, 1:257], gray[t][:, 1:257]).then_inc(gray_high, 1)

                def halve(t):
                    act.wait_ge(edges_summed, NT * (b + 1) + t + 1)
                    act.wait_ge(edges_added, NT * b + t + 1)
                    act.activation(halves[t][0:ROWS[t], :], edge_ps[t][0:ROWS[t], :], ACT.Abs,
                                   scale=0.5).then_inc(halves_made, 1)

                whiten(0)
                high(0)
                whiten(1)
                high(1)
                halve(0)
                whiten(2)
                high(2)
                halve(1)
                halve(2)

        @block.vector
        def _(dve):
            for t in range(NT):
                dve.memset(gray_hi[t][:].bitcast(F32)[:, 0:258:257], 0.0).then_inc(pads_zeroed, 1)
                dve.memset(gray_lo[t][:].bitcast(F32)[:, 0:258:257], 0.0).then_inc(pads_zeroed, 1)
            dve.wait_ge(taps_loaded, 16)
            dve.wait_ge(diag_made, 10)
            for k in range(3):
                for o in range(2):
                    for dx in range(3):
                        tap = taps[:, 9 * o + 3 * k + dx:9 * o + 3 * k + dx + 1]
                        at = band[:, 3 * o + dx, :, :]
                        if k == 0:
                            dve.tensor_scalar(at, diag[:, k, :, :], tap, None, ALU.mult).then_inc(band_step, 1)
                        else:
                            dve.wait_ge(band_step, 6 * (k - 1) + 3 * o + dx + 1)
                            dve.scalar_tensor_tensor(at, diag[:, k, :, :], tap, at, ALU.mult, ALU.add).then_inc(band_step, 1)
            dve.wait_ge(band_step, 18)
            dve.wait_ge(band_high, 1)
            dve.tensor_tensor(band_lo[:], band[:], band_hi[:].bitcast(F32), ALU.subtract).then_inc(band_step, 1)
            credit(dve, gray_made, NT)
            credit(dve, edges_added, NT)
            with dve.Fori(0, B) as b:
                def mix(t):
                    dve.wait_ge(red_scaled, NT * b + t + 1)
                    dve.scalar_tensor_tensor(redgreen[t][:], img[t][:, 1, :], 0.587, red[t][:],
                                             ALU.mult, ALU.add).then_inc(gray_step, 1)
                    dve.wait_ge(gray_step, NT * b + t + 1)
                    dve.scalar_tensor_tensor(gray[t][:, 1:257], img[t][:, 2, :], 0.114, redgreen[t][:],
                                             ALU.mult, ALU.add).then_inc(gray_made, 1)

                def low(t):
                    dve.wait_ge(gray_high, NT * b + t + 1)
                    dve.tensor_tensor(gray_lo[t][:, 1:257], gray[t][:, 1:257],
                                      gray_hi[t][:, 1:257].bitcast(F32), ALU.subtract).then_inc(gray_low, 1)

                def add(t):
                    dve.wait_ge(halves_made, NT * (b + 1) + t + 1)
                    n = ROWS[t]
                    dve.tensor_tensor(h[0:n, bass.ds(NT * b + t, 1), :].rearrange("p a d -> p (a d)"),
                                      halves[t][0:n, 0:256], halves[t][0:n, 256:512], ALU.add).then_inc(edges_added, 1)

                mix(0)
                low(0)
                mix(1)
                low(1)
                add(0)
                mix(2)
                low(2)
                add(1)
                add(2)

        @block.tensor
        def _(pe):
            pe.wait_ge(band_step, 19)
            pe.wait_ge(pads_zeroed, 2 * NT)
            credit(pe, edges_summed, NT)
            with pe.Fori(0, B) as b:
                for t in range(NT):
                    pe.wait_ge(gray_low, NT * b + t + 1)
                    pe.wait_ge(halves_made, NT * b + t + 1)
                    for o in range(2):
                        n = 0
                        for dx in range(3):
                            for w, g in ((band_hi, gray_hi), (band_lo, gray_hi), (band_hi, gray_lo)):
                                last = pe.matmul(edge_ps[t][0:ROWS[t], 256 * o:256 * o + 256],
                                                 w[:, 3 * o + dx, t, 0:ROWS[t]], g[t][:, dx:dx + 256],
                                                 start=(n == 0), stop=(n == 8))
                                n += 1
                    last.then_inc(edges_summed, 1)


class LayerNorm:

    def __init__(self, sb, sem, tag, h, xn):
        self.h, self.xn = h, xn
        self.stats = sb(f"ln_stats{tag}", [TT, NT, 6], F32)
        self.mean_var = sb(f"ln_mean_var{tag}", [TT, NT, 2], F32)
        self.var_eps = sb(f"ln_var_eps{tag}", [TT, NT], F32)
        self.rstd = sb(f"ln_rstd{tag}", [TT, NT], F32)
        self.minus_half = sb(f"ln_minus_half{tag}", [TT, NT], F32)
        self.aggr_done = sem(f"ln_aggr_done{tag}")
        self.var_ready, self.rstd_ready = sem(f"ln_var_ready{tag}"), sem(f"ln_rstd_ready{tag}")
        self.xn_ready, self.half_set = sem(f"ln_xn_ready{tag}"), sem(f"ln_half_set{tag}")

    def tile(self, n, i):
        return self.h[:, bass.ds(NT * n + i, 1), :].rearrange("p a d -> p (a d)")

    def on_vector_stats(self, dve, started, n):
        dve.wait_ge(started, 1)
        dve.drain()
        for i in range(NT):
            dve.bn_stats(self.stats[:, i, :], self.tile(n, i))
        dve.drain()
        for i in range(NT):
            dve.bn_aggr(self.mean_var[:, i, :], self.stats[:, i, :]).then_inc(self.aggr_done, 1)
        dve.wait_ge(self.aggr_done, NT * n + NT)
        dve.tensor_scalar(self.var_eps[:], self.mean_var[:, :, 1], EPS, None, ALU.add).then_inc(self.var_ready, 1)

    def on_vector_apply(self, dve, n):
        dve.wait_ge(self.rstd_ready, n + 1)
        for i in range(NT):
            last = dve.tensor_scalar(self.xn[:, i, :], self.tile(n, i), self.mean_var[:, i, 0:1],
                                     self.rstd[:, i:i + 1], ALU.subtract, ALU.mult)
            last.then_inc(self.xn_ready, 1)

    def on_pool(self, pool, n):
        pool.wait_ge(self.var_ready, n + 1)
        pool.tensor_tensor(self.rstd[:], self.var_eps[:], self.minus_half[:], ALU.pow).then_inc(self.rstd_ready, 1)


def attention(nc, sb, ps, sem, layer, c, h, ao, B, weights, table=None):
    L = f"_a{layer}"
    H, D = 16, 16
    window = layer == 1
    KV = 4 if window else 16
    SLOTS = 14
    NK = [SP1 - TT * 2, TT * 2, SP1]
    NQ = [SP1, TT * 2, SP1 - TT * 2]
    common = [(f"X{i}", "AD") for i in range(NT)] + ([] if window else [("C", "AD")])
    common += [(f"QK{i}", "D" if window else "AD") for i in range(NT)]
    units = list(common)
    for s in range(SLOTS):
        if 2 <= s < 10:
            units += [(f"TK{s - 2}", "A"), (f"TQ{s - 2}", "D")]
        if 4 <= s < 12:
            units += [(f"S{s - 4}_{k}", "D") for k in range(4)]
        if s >= 6:
            units += [(f"R{s - 6}", "A" if s % 2 else "D")]
    units += [(f"V{i}", "A") for i in range(NT)]
    while len(units) % 3:
        units.append(("unused" + str(len(units)), ""))
    ring = Ring(3, units)

    xn = sb("xn" + L, [TT, NT, 256], F32)
    xt_hi, xt_lo = sb("xt_hi" + L, [P, 2, SP1], F32R), sb("xt_lo" + L, [P, 2, SP1], F32R)
    qpad, kpad = sb("qpad" + L, [TT, NT, H, 64], F32), sb("kpad" + L, [TT, NT, H, 64], F32)
    vaug = sb("vaug" + L, [TT, NT, KV, D + 1], F32)
    q_first = [sb(f"q_first{i}" + L, [P, SP1], F32R) for i in range(4)]
    q_shift = sb("q_shift" + L, [P, 8, SP1], F32R)
    k_t = sb("k_t" + L, [P, 8, SP1], F32R)
    neg_max = [sb(f"neg_max{i}" + L, [TT, NT, 2], F32) for i in range(2)]
    probs = [sb(f"probs{i}" + L, [TT, 3, 448], F32) for i in range(2)]
    rsum = [sb(f"rsum{i}" + L, [TT, NT, 8], F32) for i in range(2)]
    MW = SP1 if window else SP1 - TT * 2
    mask_s = sb("mask_s" + L, [TT, NT if window else 1, MW], BF16)
    mask_t = sb("mask_t" + L, [TT, MW], BF16)
    ln = LayerNorm(sb, sem, L, h, xn)

    if window:
        W3 = 384
        w_raw, w_hi, w_lo = (sb(n + L, [P, 2, W3], d) for n, d in (("w_raw", F32), ("w_hi", F32R), ("w_lo", F32R)))
        cos, sin = sb("cos" + L, [TT, NT, D], F32), sb("sin" + L, [TT, NT, D], F32)
        qk_cos, qk_sin, qk_rot = (sb(n + L, [TT, NT, 20, D], F32) for n in ("qk_cos", "qk_sin", "qk_rot"))
    else:
        c_hi, c_lo = sb("c_hi" + L, [P, SP1], F32R), sb("c_lo" + L, [P, SP1], F32R)
        d_raw, d_hi, d_lo = (sb(n + L, [P, 2, P], d) for n, d in (("d_raw", F32), ("d_hi", F32R), ("d_lo", F32R)))
        w_raw, w_hi, w_lo = (sb(n + L, [P, 768], d) for n, d in (("w_raw", F32), ("w_hi", F32R), ("w_lo", F32R)))

    work = [ps(f"work{i}" + L, [P, 512], F32) for i in range(3)]
    score_t = [ps(f"score_t{i}" + L, [TT, 512], F32) for i in range(3)]
    heads = [ps(f"heads{i}" + L, [TT, NT, 8, D + 1], F32) for i in range(2)]

    w_loaded, w_zeroed, w_high, w_low = (sem(n + L) for n in ("w_loaded", "w_zeroed", "w_high", "w_low"))
    masks_made, cleared, pads_zeroed = sem("masks_made" + L), sem("cleared" + L), sem("pads_zeroed" + L)
    filled = sem("work_filled" + L)
    drained = {"A": sem("act_drained" + L), "D": sem("dve_drained" + L)}
    max_taken, max_high, max_placed = sem("max_taken" + L), sem("max_high" + L), sem("max_placed" + L)
    score_filled, exp_done, av_done = sem("score_filled" + L), sem("exp_done" + L), sem("av_done" + L)
    sums_inverted, heads_done = sem("sums_inverted" + L), sem("heads_done" + L)
    qk_high, rotated = sem("qk_high" + L), sem("rotated" + L)
    pads_made = sem("pads_made" + L)
    rows_zeroed, rows_cleared = sem("rows_zeroed" + L), sem("rows_cleared" + L)

    def couple(u):
        g, r = u // 2, u % 2
        return slice(64 * r, 64 * r + 64), (2 * g, 2 * g + 1), (4 * g + r, 4 * g + 2 + r)

    SCORE_UNITS = [(0, [0, 1]), (1, [0, 1]), (2, [0]), (2, [1])]

    with nc.Block() as block:

        @block.sync
        def _(sp):
            if window:
                wqT, wkT, wvT, rope_cos, rope_sin = weights
                for w, at, n in ((wqT, 0, 256), (wkT, 256, 64), (wvT, 320, 64)):
                    sp.dma_start(w_raw[:, :, at:at + n], w.rearrange("(a p) n -> p a n", p=P)).then_inc(w_loaded, 16)
                sp.dma_start(cos[:], rope_cos).then_inc(w_loaded, 16)
                sp.dma_start(sin[:], rope_sin).then_inc(w_loaded, 16)
            else:
                w_dq, w_dkv, w_uq, w_uk, w_uv = weights
                for w, at in ((w_dq, 0), (w_dkv, 64)):
                    sp.dma_start(d_raw[:, :, at:at + 64], w.rearrange("(a p) n -> p a n", p=P)).then_inc(w_loaded, 16)
                sp.wait_ge(w_zeroed, 1)
                sp.dma_start(w_raw[0:64, 0:256], w_uq).then_inc(w_loaded, 16)
                sp.dma_start(w_raw[64:P, 256:512], w_uk).then_inc(w_loaded, 16)
                sp.dma_start(w_raw[64:P, 512:768], w_uv).then_inc(w_loaded, 16)
                sp.wait_ge(rows_zeroed, 1)
                slots = table.experts * table.capacity
                sp.dma_start(table.x_rows[0:slots, :].rearrange("(t p) d -> p t d", p=TT),
                             table.zeros[:].to_broadcast([TT, slots // TT, 256])).then_inc(rows_cleared, 16)
                sp.wait_ge(rows_cleared, 16)

        @block.gpsimd
        def _(pool):
            pool.memset(ln.minus_half[:], -0.5).then_inc(ln.half_set, 1)
            if not window:
                pool.memset(table.zeros[:], 0.0).then_inc(rows_zeroed, 1)
            pool.memset(mask_s[:], 0.0).then_inc(masks_made, 1)
            pool.memset(mask_t[:], 0.0).then_inc(masks_made, 1)
            pool.wait_ge(masks_made, 2)
            n = 2

            def keep(m, base, cm, step):
                nonlocal n
                pool.wait_ge(masks_made, n)
                pool.affine_select(out=m, in_=m, compare_op=ALU.is_ge, fill=MASKED, base=base,
                                   pattern=[[step, MW]], channel_multiplier=cm).then_inc(masks_made, 1)
                n += 1

            for i in range(NT if window else 1):
                keep(mask_s[:, i, :], TT * i, 1, -1)
                if window:
                    keep(mask_s[:, i, :], 127 - TT * i, -1, 1)
            keep(mask_t[:], 0, -1, 1)
            if window:
                keep(mask_t[:], 127, 1, -1)

            def prepare(n):
                ln.on_pool(pool, n)
                if window:
                    for i in range(NT):
                        pool.wait_ge(drained["D"], ring.drained(n, ring.at[f"QK{i}"], "D"))
                        pool.tensor_tensor(qk_rot[:, i], qk_cos[:, i], qk_sin[:, i], ALU.add).then_inc(rotated, 1)

            prepare(0)
            with pool.Fori(0, B - 1) as b:
                prepare(b + 1)

        masks_total = 2 + (2 * NT + 2 if window else 2)

        @block.tensor
        def _(pe):
            pe.wait_ge(masks_made, masks_total)
            pe.wait_ge(w_low, 1 if window else 2)
            pe.wait_ge(cleared, 1)

            def free(n, unit):
                for e, count in ring.before(n, unit):
                    pe.wait_ge(drained[e], count)
                return work[ring.bank(unit)]

            def three(out, terms, first=True, last=True):
                for k, (s_hi, s_lo, m_hi, m_lo) in enumerate(terms):
                    for j, (s, m) in enumerate(((s_hi, m_hi), (s_lo, m_hi), (s_hi, m_lo))):
                        got = pe.matmul(out, s, m, start=(first and k == 0 and j == 0),
                                        stop=(last and k == len(terms) - 1 and j == 2))
                return got

            def prepare(n):
                pe.wait_ge(ln.xn_ready, NT * n + NT)
                for i in range(NT):
                    out = free(n, f"X{i}")
                    for a in range(2):
                        got = pe.transpose(out[:, TT * a:TT * a + TT], xn[:, i, P * a:P * a + P], c.ident[0:TT, 0:TT])
                    got.then_inc(filled, 1)
                pe.wait_ge(drained["D"], ring.drained(n, ring.at["X2"], "D"))
                if not window:
                    out = free(n, "C")
                    three(out[:, 0:SP1], [(d_hi[:, a, :], d_lo[:, a, :], xt_hi[:, a, :], xt_lo[:, a, :])
                                          for a in range(2)]).then_inc(filled, 1)
                    pe.wait_ge(drained["D"], ring.drained(n, ring.at["C"], "D"))
                for i in range(NT):
                    out = free(n, f"QK{i}")
                    t = slice(TT * i, TT * i + TT)
                    if window:
                        got = three(out[0:TT, 0:320], [(xt_hi[:, a, t], xt_lo[:, a, t], w_hi[:, a, 0:320], w_lo[:, a, 0:320])
                                                       for a in range(2)])
                    else:
                        got = three(out[0:TT, 0:512], [(c_hi[:, t], c_lo[:, t], w_hi[:, 0:512], w_lo[:, 0:512])])
                    got.then_inc(filled, 1)

            def values(n):
                for i in range(NT):
                    out = free(n, f"V{i}")
                    t = slice(TT * i, TT * i + TT)
                    if window:
                        got = three(out[0:TT, 0:64], [(xt_hi[:, a, t], xt_lo[:, a, t], w_hi[:, a, 320:384], w_lo[:, a, 320:384])
                                                      for a in range(2)])
                    else:
                        got = three(out[0:TT, 0:256], [(c_hi[:, t], c_lo[:, t], w_hi[:, 512:768], w_lo[:, 512:768])])
                    got.then_inc(filled, 1)

            def turn(n, unit, pad, p):
                out = free(n, unit)
                for i in range(NT):
                    got = pe.transpose(out[:, TT * i:TT * i + TT],
                                       pad[:, i, 2 * p:2 * p + 2, :].rearrange("p h c -> p (h c)"), c.ident[0:TT, 0:TT])
                got.then_inc(filled, 1)

            def turn_pair(n, p):
                if p == 0:
                    pe.wait_ge(pads_made, NT * n + NT)
                turn(n, f"TK{p}", kpad, p)
                turn(n, f"TQ{p}", qpad, p)

            def first_scores(n, u):
                rows, tiles, _ = couple(u)
                pe.wait_ge(drained["A"], ring.drained(n, ring.at[f"TK{tiles[1]}"], "A"))
                pe.wait_ge(drained["D"], ring.drained(n, ring.at[f"TQ{tiles[1]}"], "D"))
                for k, (i, which) in enumerate(SCORE_UNITS):
                    out = free(n, f"S{u}_{k}")
                    for j, w in enumerate(which):
                        p = tiles[w]
                        at = NK[i] * j
                        pe.matmul(out[0:TT, at:at + NK[i]], q_first[p % 4][rows, TT * i:TT * i + TT],
                                  k_t[rows, p, 0:NK[i]], start=True, stop=False)
                        if window:
                            cols, mask = slice(at, at + NK[i]), mask_s[:, i, 0:NK[i]]
                        else:
                            m = TT if i == 1 else MW
                            cols, mask = slice(at + TT * i, at + TT * i + m), mask_s[:, 0, 0:m]
                        got = pe.matmul(out[0:TT, cols], c.ident_bf[:, :], mask, start=False, stop=True)
                    got.then_inc(filled, 1)

            def turn_shifted(n, p):
                pe.wait_ge(max_placed, 8 * n + 2 * (p // 2) + 2)
                turn(n, f"R{p}", qpad, p)

            def scores(b, u):
                rows, tiles, _ = couple(u)
                if u == 0:
                    for e in "AD":
                        pe.wait_ge(drained[e], ring.drained(b, len(ring.who) - 1, e))
                for k in range(3):
                    pe.wait_ge(exp_done, 24 * b + 3 * u + k + 1)
                    blocks = [(k, 0, 0), (k, 2, SP1)] if k < 2 else [(0, 1, 0), (1, 1, 2 * TT)]
                    for w, j, at in blocks:
                        p = tiles[w]
                        pe.matmul(score_t[k][:, at:at + NQ[j]], k_t[rows, p, TT * j:TT * j + TT],
                                  q_shift[rows, p, TT * j:TT * j + NQ[j]], start=True, stop=False)
                        cols = NQ[j] if window else (TT if j == 1 else MW)
                        got = pe.matmul(score_t[k][:, at:at + cols], c.ident_bf[:, :], mask_t[:, 0:cols],
                                        start=False, stop=True)
                    got.then_inc(score_filled, 1)

            def weigh(b, u):
                pe.wait_ge(exp_done, 24 * b + 3 * u + 6)
                if u % 4 == 0:
                    pe.wait_ge(heads_done, 2 * b + u // 4 + 1)
                for w, head in enumerate(couple(u)[2]):
                    at = {0: (w, 0), 1: (2, 2 * TT * w), 2: (w, SP1)}
                    for i in range(NT):
                        for j in range(i + 1):
                            k, col = at[j]
                            col += TT * (i - j)
                            got = pe.matmul(heads[u // 4][:, i, head % 8, :], probs[u % 2][:, k, col:col + TT],
                                            vaug[:, j, head * KV // H, :], start=(j == 0), stop=(j == i))
                got.then_inc(av_done, 1)

            def slots(b, n):
                for s in range(SLOTS):
                    if b is not None and s < 8:
                        scores(b, s)
                    if n is not None and 2 <= s < 10:
                        turn_pair(n, s - 2)
                    if b is not None and 1 <= s <= 8:
                        weigh(b, s - 1)
                    if n is not None and 4 <= s < 12:
                        first_scores(n, s - 4)
                    if n is not None and s >= 6:
                        turn_shifted(n, s - 6)
                if n is not None:
                    values(n)

            credit(pe, av_done, 2)
            prepare(0)
            slots(None, 0)
            with pe.Fori(0, B - 1) as b:
                prepare(b + 1)
                slots(b, b + 1)
            slots(B - 1, None)

        @block.scalar
        def _(act):
            if window:
                act.wait_ge(w_loaded, 80)
                act.copy(w_hi[:], w_raw[:]).then_inc(w_high, 1)
            else:
                act.wait_ge(w_loaded, 80)
                act.copy(d_hi[:], d_raw[:]).then_inc(w_high, 1)
                act.copy(w_hi[:], w_raw[:]).then_inc(w_high, 1)
            act.wait_ge(cleared, 1)
            credit(act, drained["A"], ring.per["A"])
            credit(act, exp_done, 3)

            def bank(n, unit):
                act.wait_ge(filled, ring.filled(n, unit))
                return work[ring.bank(unit)]

            def prepare(n):
                for i in range(NT):
                    src = bank(n, f"X{i}")
                    act.copy(xt_hi[:, :, TT * i:TT * i + TT], src[:, 0:2 * TT].rearrange("p (a t) -> p a t", a=2))\
                        .then_inc(drained["A"], 1)
                if not window:
                    src = bank(n, "C")
                    act.copy(c_hi[:, 0:S], src[:, 0:S]).then_inc(drained["A"], 1)
                for i in range(NT):
                    if window:
                        act.wait_ge(rotated, NT * n + i + 1)
                        q = qk_rot[:, i, 0:16, :]
                        k = qk_rot[:, i, 16:20, :]
                    else:
                        src = bank(n, f"QK{i}")
                        q = src[0:TT, 0:256].rearrange("p (h d) -> p h d", h=H)
                        k = src[0:TT, 256:512].rearrange("p (h d) -> p h d", h=H)
                    act.copy(qpad[:, i, :, 0:32].rearrange("p h (s d) -> p h s d", s=2).bitcast(F32R),
                             q.unsqueeze(2).to_broadcast([TT, H, 2, D]))
                    if window:
                        for slot in (0, 2):
                            got = act.copy(kpad[:, i, :, slot * D:slot * D + D].rearrange("p (g r) d -> p g r d", g=4)
                                           .bitcast(F32R), k.unsqueeze(2).to_broadcast([TT, 4, 4, D]))
                        got.then_inc(qk_high, 1)
                    else:
                        act.copy(kpad[:, i, :, 0:48].rearrange("p h (s d) -> p h s d", s=3)[:, :, 0:3:2, :].bitcast(F32R),
                                 k.unsqueeze(2).to_broadcast([TT, H, 2, D])).then_inc(drained["A"], 1)

            def turn_pair(n, p):
                src = bank(n, f"TK{p}")
                act.copy(k_t[:, p, 0:S], src[:, 0:S]).then_inc(drained["A"], 1)

            def turn_shifted(n, p):
                src = bank(n, f"R{p}")
                act.copy(q_shift[:, p, 0:S], src[:, 0:S]).then_inc(drained["A"], 1)

            def values(n):
                for i in range(NT):
                    src = bank(n, f"V{i}")
                    act.copy(vaug[:, i, :, 0:D], src[0:TT, 0:KV * D].rearrange("p (g d) -> p g d", d=D))\
                        .then_inc(drained["A"], 1)

            def exps(b, p):
                act.wait_ge(av_done, 8 * b + p + 1)
                for k in range(3):
                    act.wait_ge(score_filled, 24 * b + 3 * p + k + 1)
                    n = 4 * TT + (2 if k < 2 else 0)
                    act.activation(probs[p % 2][:, k, 0:n], score_t[k][:, 0:n], ACT.Exp, scale=SCALE)\
                        .then_inc(exp_done, 1)

            def slots(b, n):
                for s in range(SLOTS):
                    if b is not None and s < 8:
                        exps(b, s)
                    if n is not None and 2 <= s < 10:
                        turn_pair(n, s - 2)
                    if n is not None and s >= 6 and s % 2:
                        turn_shifted(n, s - 6)
                if n is not None:
                    values(n)

            prepare(0)
            slots(None, 0)
            with act.Fori(0, B - 1) as b:
                prepare(b + 1)
                slots(b, b + 1)
            slots(B - 1, None)

        @block.vector
        def _(dve):
            if not window:
                dve.memset(w_raw[:], 0.0).then_inc(w_zeroed, 1)
            for z in (qpad, kpad):
                dve.memset(z[:], 0.0).then_inc(pads_zeroed, 1)
            for z in (xt_hi, xt_lo, *q_first, q_shift, k_t, *(() if window else (c_hi, c_lo))):
                dve.memset(z[:].bitcast(F32), 0.0)
            dve.memset(vaug[:, :, :, D:D + 1], 1.0)
            dve.wait_ge(pads_zeroed, 2)
            dve.memset(kpad[:, :, :, 48:50], 1.0).then_inc(cleared, 1)
            if not window:
                dve.wait_ge(w_high, 1)
                dve.tensor_tensor(d_lo[:], d_raw[:], d_hi[:].bitcast(F32), ALU.subtract).then_inc(w_low, 1)
            dve.wait_ge(w_high, 1 if window else 2)
            dve.tensor_tensor(w_lo[:], w_raw[:], w_hi[:].bitcast(F32), ALU.subtract).then_inc(w_low, 1)
            dve.wait_ge(ln.half_set, 1)
            credit(dve, drained["D"], ring.per["D"])
            credit(dve, heads_done, 2)

            def bank(n, unit):
                dve.wait_ge(filled, ring.filled(n, unit))
                return work[ring.bank(unit)]

            def prepare(n):
                ln.on_vector_stats(dve, c.ready, n)
                ln.on_vector_apply(dve, n)
                for i in range(NT):
                    src = bank(n, f"X{i}")
                    dve.wait_ge(drained["A"], ring.drained(n, ring.at[f"X{i}"], "A"))
                    t = slice(TT * i, TT * i + TT)
                    dve.tensor_tensor(xt_lo[:, :, t], src[:, 0:2 * TT].rearrange("p (a t) -> p a t", a=2),
                                      xt_hi[:, :, t].bitcast(F32), ALU.subtract).then_inc(drained["D"], 1)
                if not window:
                    src = bank(n, "C")
                    dve.wait_ge(drained["A"], ring.drained(n, ring.at["C"], "A"))
                    dve.tensor_tensor(c_lo[:, 0:S], src[:, 0:S], c_hi[:, 0:S].bitcast(F32), ALU.subtract)\
                        .then_inc(drained["D"], 1)
                for i in range(NT):
                    src = bank(n, f"QK{i}")
                    if window:
                        both = src[0:TT, 0:320].rearrange("p (h d) -> p h d", d=D)
                        dve.tensor_tensor(qk_cos[:, i], both, cos[:, i:i + 1, :].to_broadcast([TT, 20, D]), ALU.mult)
                        dve.tensor_tensor(qk_sin[:, i, :, 0:8], both[:, :, 8:16],
                                          sin[:, i:i + 1, 0:8].to_broadcast([TT, 20, 8]), ALU.mult)
                        dve.tensor_tensor(qk_sin[:, i, :, 8:16], both[:, :, 0:8],
                                          sin[:, i:i + 1, 8:16].to_broadcast([TT, 20, 8]), ALU.mult)\
                            .then_inc(drained["D"], 1)
                        dve.wait_ge(qk_high, NT * n + i + 1)
                        q, k = qk_rot[:, i, 0:16, :], qk_rot[:, i, 16:20, :]
                    else:
                        dve.wait_ge(drained["A"], ring.drained(n, ring.at[f"QK{i}"], "A"))
                        q = src[0:TT, 0:256].rearrange("p (h d) -> p h d", h=H)
                        k = src[0:TT, 256:512].rearrange("p (h d) -> p h d", h=H)
                    dve.tensor_tensor(qpad[:, i, :, 32:48], q, qpad[:, i, :, 0:16], ALU.subtract)
                    if window:
                        dve.tensor_tensor(kpad[:, i, :, 16:32].rearrange("p (g r) d -> p g r d", g=4),
                                          k.unsqueeze(2).to_broadcast([TT, 4, 4, D]),
                                          kpad[:, i, :, 0:16].rearrange("p (g r) d -> p g r d", g=4), ALU.subtract)
                    else:
                        dve.tensor_tensor(kpad[:, i, :, 16:32], k, kpad[:, i, :, 0:16], ALU.subtract)\
                            .then_inc(drained["D"], 1)
                    dve.memset(qpad[:, i, :, 48:50], 0.0).then_inc(pads_made, 1)

            def turn_pair(n, p):
                src = bank(n, f"TQ{p}")
                dve.tensor_copy(q_first[p % 4][:, 0:S], src[:, 0:S]).then_inc(drained["D"], 1)

            def maxima(n, u):
                m = neg_max[u % 2]
                for k, (i, which) in enumerate(SCORE_UNITS):
                    src = bank(n, f"S{u}_{k}")
                    w = len(which)
                    dve.tensor_reduce(m[:, i, which[0]:which[0] + w],
                                      src[0:TT, 0:w * NK[i]].rearrange("p (h k) -> p h k", h=w),
                                      AX.X, ALU.max, negate=True).then_inc(drained["D"], 1)
                dve.wait_ge(drained["D"], ring.drained(n, ring.at[f"S{u}_3"], "D"))
                a, z = couple(u)[2]
                dve.tensor_copy(qpad[:, :, a:z + 1:2, 48].bitcast(F32R), m[:]).then_inc(max_high, 1)
                dve.wait_ge(max_high, 8 * n + u + 1)
                dve.tensor_tensor(qpad[:, :, a:z + 1:2, 49], m[:], qpad[:, :, a:z + 1:2, 48], ALU.subtract)\
                    .then_inc(max_placed, 1)

            def turn_shifted(n, p):
                src = bank(n, f"R{p}")
                dve.tensor_copy(q_shift[:, p, 0:S], src[:, 0:S]).then_inc(drained["D"], 1)

            def divide(b, half):
                dve.wait_ge(av_done, 8 * b + 4 * half + 6)
                src = heads[half]
                dve.reciprocal(rsum[half][:], src[:, :, :, D]).then_inc(sums_inverted, 1)
                dve.wait_ge(sums_inverted, 2 * b + half + 1)
                dve.tensor_tensor(ao[:, bass.ds(NT * b, NT), P * half:P * half + P].rearrange("p t (h d) -> p t h d", h=8),
                                  src[:, :, :, 0:D], rsum[half][:].unsqueeze(3).to_broadcast([TT, NT, 8, D]), ALU.mult)\
                    .then_inc(heads_done, 1)

            def slots(b, n):
                for s in range(SLOTS):
                    if n is not None and 2 <= s < 10:
                        turn_pair(n, s - 2)
                    if n is not None and 4 <= s < 12:
                        maxima(n, s - 4)
                    if n is not None and s >= 6 and s % 2 == 0:
                        turn_shifted(n, s - 6)
                    if b is not None and s in (4, 8):
                        divide(b, s // 4 - 1)

            prepare(0)
            slots(None, 0)
            with dve.Fori(0, B - 1) as b:
                prepare(b + 1)
                slots(b, b + 1)
            slots(B - 1, None)


def dispatch(nc, sb, ps, sem, layer, c, h, ao, B, w_out, w_gate, b_gate, table):
    L = f"_d{layer}"
    top2 = layer == 1
    E = table.experts
    out_ring = Ring(3, [(f"A{i}", "AD") for i in range(NT)] + [("Y01", "D"), ("Y2", "D"), ("unused", "")])
    gate_ring = Ring(4, [(f"X{i}", "AD") for i in range(NT)] + [("G", "D"), ("POS", "D")]
                     + [(f"unused{i}", "") for i in range(3)])

    xn = sb("xn" + L, [TT, NT, 256], F32)
    xs = xn if top2 else sb("xs" + L, [TT, NT, 256], F32)
    xt_hi, xt_lo = sb("xt_hi" + L, [P, 2, SP1], F32R), sb("xt_lo" + L, [P, 2, SP1], F32R)
    g_raw, g_hi, g_lo = (sb(n + L, [P, 2, E], d) for n, d in (("g_raw", F32), ("g_hi", F32R), ("g_lo", F32R)))
    if not top2:
        ao_now = sb("ao_now" + L, [TT, NT, 256], F32)
        at_hi, at_lo = sb("at_hi" + L, [P, 2, SP1], F32R), sb("at_lo" + L, [P, 2, SP1], F32R)
        o_raw, o_hi, o_lo = (sb(n + L, [P, 2, 256], d) for n, d in (("o_raw", F32), ("o_hi", F32R), ("o_lo", F32R)))
    bias = sb("bias" + L, [TT, E], F32)
    upto = sb("upto" + L, [TT, TT], F32)
    ones = sb("ones" + L, [TT, TT], F32)
    order = sb("order" + L, [TT, NT, E], F32)
    token = sb("token" + L, [TT, NT], F32)
    logits, masked, equal, ranks, picked = (sb(n + L, [TT, NT, E], F32) for n in ("logits", "masked", "equal", "ranks", "picked"))
    hot = [sb(f"hot{k}" + L, [TT, NT, E], F32) for k in range(2)]
    both = sb("both" + L, [TT, NT, E], F32)
    best = [sb(f"best{k}" + L, [TT, NT], F32) for k in range(2)]
    first = [sb(f"first{k}" + L, [TT, NT], F32) for k in range(2)]
    place = [sb(f"place{k}" + L, [TT, NT], F32) for k in range(2)]
    kept, shift, expo = sb("kept" + L, [TT, NT], F32), sb("shift" + L, [TT, NT, E], F32), sb("expo" + L, [TT, NT, E], F32)
    prob, inverse, factor = (sb(n + L, [TT, NT], F32) for n in ("prob", "inverse", "factor"))
    before = sb("before" + L, [TT, NT + 1, E], F32)
    slot = [sb(f"slot{k}" + L, [TT, NT], I32) for k in range(2)]
    ln = LayerNorm(sb, sem, L, h, xn)
    for ring, name in ((out_ring, "out"), (gate_ring, "gate")):
        ring.tiles = [ps(f"{name}_bank{i}" + L, [P, 512], F32) for i in range(ring.banks)]
        ring.filled_sem = sem(f"{name}_filled" + L)
        ring.drained_sem = {"A": sem(f"{name}_act_drained" + L), "D": sem(f"{name}_dve_drained" + L)}

    def ring_of(unit):
        return out_ring if unit in out_ring.at and not unit.startswith("unused") else gate_ring

    count_ps = ps("count_ps" + L, [TT, 16], F32)

    loaded, w_high, w_low, made, cleared = (sem(n + L) for n in ("loaded", "w_high", "w_low", "made", "cleared"))
    ao_ready, h_added, step = sem("ao_ready" + L), sem("h_added" + L), sem("step" + L)
    logits_ready, exp_done, hot_ready = sem("logits_ready" + L), sem("exp_done" + L), sem("hot_ready" + L)
    slots_ready, scattered, copied = sem("slots_ready" + L), sem("scattered" + L), sem("copied" + L)
    total_ready, tails_ready = sem("total_ready" + L), sem("tails_ready" + L)
    rows_left = sem("rows_left" + L)
    slots_seen = sem("slots_seen" + L)
    plan_step = sem("plan_step" + L)
    K = 2 if top2 else 1
    MADE = 8 if top2 else 5
    if top2:
        ks = sb("ks" + L, [TT, E, B], F32)
        js = sb("js" + L, [TT, E, table.blocks], F32)
    with nc.Block() as block:

        @block.sync
        def _(sp):
            sp.dma_start(g_raw[:], w_gate.rearrange("(a p) n -> p a n", p=P)).then_inc(loaded, 16)
            sp.dma_start(bias[:], b_gate.partition_broadcast(TT)).then_inc(loaded, 16)
            if not top2:
                sp.dma_start(o_raw[:], w_out.rearrange("(a p) n -> p a n", p=P)).then_inc(loaded, 16)
                with sp.Fori(0, B) as b:
                    sp.wait_ge(slots_ready, b + 1)
                    sp.dma_start(table.y_rows[bass.ds(table.own + S * b, S), :].rearrange("(t p) d -> p t d", p=TT),
                                 xs[:]).then_inc(copied, 16)
                sp.wait_ge(copied, 16 * (B + 1))
            else:
                sp.wait_ge(tails_ready, 1)
                sp.wait_ge(scattered, 16 * NT * K * B)
                for e in range(E):
                    at = sp.value_load(table.tails[0:1, e:e + 1], min_val=e * table.region,
                                       max_val=e * table.region + S * B)
                    sp.dma_start(table.x_rows[bass.ds(at, S), :].rearrange("(t p) d -> p t d", p=TT),
                                 table.zeros[:].to_broadcast([TT, NT, 256])).then_inc(copied, 16)
                sp.dma_start(table.x_rows[E * table.region:E * table.region + S, :].rearrange("(t p) d -> p t d", p=TT),
                             table.zeros[:].to_broadcast([TT, NT, 256])).then_inc(copied, 16)
                sp.wait_ge(copied, 16 * (E + 1))

        @block.gpsimd
        def _(pool):
            pool.memset(ln.minus_half[:], -0.5).then_inc(ln.half_set, 1)
            pool.memset(upto[:], 1.0).then_inc(made, 1)
            pool.memset(ones[:], 1.0).then_inc(made, 1)
            pool.iota(order[:], [[0, NT], [-1, E]], base=E, channel_multiplier=0,
                      allow_small_or_imprecise_dtypes=True).then_inc(made, 1)
            pool.iota(token[:], [[TT, NT]], base=table.own, channel_multiplier=1,
                      allow_small_or_imprecise_dtypes=True).then_inc(made, 1)
            pool.wait_ge(made, 4)
            pool.affine_select(out=upto[:], in_=upto[:], compare_op=ALU.is_ge, fill=0.0, base=0,
                               pattern=[[1, TT]], channel_multiplier=-1).then_inc(made, 1)
            if top2:
                pool.iota(ks[:], [[0, E], [S, B]], base=0, channel_multiplier=0,
                          allow_small_or_imprecise_dtypes=True).then_inc(made, 1)
                pool.iota(js[:], [[0, E], [1, table.blocks]], base=0, channel_multiplier=0,
                          allow_small_or_imprecise_dtypes=True).then_inc(made, 1)
                pool.memset(table.zeros[:], 0.0).then_inc(made, 1)

            def send(n):
                pool.wait_ge(slots_ready, n + 1)
                pool.sem_inc(slots_seen, 1)
                for i in range(NT):
                    for k in range(K):
                        pool.indirect_dma_start(table.x_rows, bass.IndirectOffsetOnAxis(ap=slot[k][:, i:i + 1], axis=0),
                                                xs[:, i, :], None).then_inc(scattered, 16)
                pool.wait_ge(scattered, 16 * NT * K * (n + 1))
                pool.sem_inc(rows_left, 1)

            ln.on_pool(pool, 0)
            with pool.Fori(0, B - 1) as b:
                ln.on_pool(pool, b + 1)
                send(b)
            send(B - 1)

        @block.tensor
        def _(pe):
            pe.wait_ge(w_low, 1 if top2 else 2)
            pe.wait_ge(made, MADE)
            pe.wait_ge(cleared, 1)

            def free(n, unit):
                ring = ring_of(unit)
                for e, count in ring.before(n, unit):
                    pe.wait_ge(ring.drained_sem[e], count)
                return ring.tiles[ring.bank(unit)]

            def three(out, terms):
                for k, (s_hi, s_lo, m_hi, m_lo) in enumerate(terms):
                    for j, (s, m) in enumerate(((s_hi, m_hi), (s_lo, m_hi), (s_hi, m_lo))):
                        got = pe.matmul(out, s, m, start=(k == 0 and j == 0), stop=(k == len(terms) - 1 and j == 2))
                return got

            def turn(n, name, src):
                for i in range(NT):
                    out = free(n, f"{name}{i}")
                    for a in range(2):
                        got = pe.transpose(out[:, TT * a:TT * a + TT], src[:, i, P * a:P * a + P], c.ident[0:TT, 0:TT])
                    got.then_inc(ring_of(f"{name}0").filled_sem, 1)

            def out_product(n):
                pe.wait_ge(ao_ready, n + 1)
                turn(n, "A", ao_now)
                pe.wait_ge(out_ring.drained_sem["D"], out_ring.drained(n, out_ring.at["A2"], "D"))
                for unit, tiles in (("Y01", (0, 1)), ("Y2", (2,))):
                    out = free(n, unit)
                    for k, i in enumerate(tiles):
                        t = slice(TT * i, TT * i + TT)
                        got = three(out[0:TT, 256 * k:256 * k + 256],
                                    [(at_hi[:, a, t], at_lo[:, a, t], o_hi[:, a, :], o_lo[:, a, :]) for a in range(2)])
                    got.then_inc(out_ring.filled_sem, 1)

            def gate(n):
                pe.wait_ge(ln.xn_ready, NT * n + NT)
                turn(n, "X", xn)
                pe.wait_ge(gate_ring.drained_sem["D"], gate_ring.drained(n, gate_ring.at["X2"], "D"))
                out = free(n, "G")
                for i in range(NT):
                    t = slice(TT * i, TT * i + TT)
                    got = three(out[0:TT, E * i:E * i + E],
                                [(xt_hi[:, a, t], xt_lo[:, a, t], g_hi[:, a, :], g_lo[:, a, :]) for a in range(2)])
                got.then_inc(gate_ring.filled_sem, 1)

            def rank(n):
                pe.wait_ge(hot_ready, n + 1)
                out = free(n, "POS")
                pe.matmul(out[0:TT, 0:NT * E], upto[:, :], (both if top2 else hot[0])[:].rearrange("p t e -> p (t e)"),
                          start=True, stop=False)
                pe.matmul(out[0:TT, 0:NT * E], ones[:, :], before[:, 0:NT, :].rearrange("p t e -> p (t e)"),
                          start=False, stop=True).then_inc(gate_ring.filled_sem, 1)

            if not top2:
                out_product(0)
            with pe.Fori(0, B - 1) as b:
                gate(b)
                if not top2:
                    out_product(b + 1)
                rank(b)
            gate(B - 1)
            rank(B - 1)
            if top2:
                pe.wait_ge(total_ready, 1)
                pe.matmul(count_ps[:, 0:E], ones[:, :], before[:, NT, :], start=True, stop=True).then_inc(total_ready, 1)

        @block.scalar
        def _(act):
            act.wait_ge(loaded, 32 if top2 else 48)
            act.copy(g_hi[:], g_raw[:]).then_inc(w_high, 1)
            if not top2:
                act.copy(o_hi[:], o_raw[:]).then_inc(w_high, 1)
            act.wait_ge(cleared, 1)
            for ring in (out_ring, gate_ring):
                credit(act, ring.drained_sem["A"], ring.per["A"])

            def high(n, name, to):
                ring = ring_of(f"{name}0")
                for i in range(NT):
                    act.wait_ge(ring.filled_sem, ring.filled(n, f"{name}{i}"))
                    src = ring.tiles[ring.bank(f"{name}{i}")]
                    act.copy(to[:, :, TT * i:TT * i + TT], src[:, 0:2 * TT].rearrange("p (a t) -> p a t", a=2))\
                        .then_inc(ring.drained_sem["A"], 1)

            def power(n):
                act.wait_ge(logits_ready, n + 1)
                act.activation(expo[:], shift[:], ACT.Exp).then_inc(exp_done, 1)

            if not top2:
                high(0, "A", at_hi)
            with act.Fori(0, B - 1) as b:
                high(b, "X", xt_hi)
                if not top2:
                    high(b + 1, "A", at_hi)
                power(b)
            high(B - 1, "X", xt_hi)
            power(B - 1)

        @block.vector
        def _(dve):
            for z in (xt_hi, xt_lo, *(() if top2 else (at_hi, at_lo))):
                dve.memset(z[:].bitcast(F32), 0.0)
            dve.memset(before[:], 0.0).then_inc(cleared, 1)
            dve.wait_ge(w_high, 1)
            dve.tensor_tensor(g_lo[:], g_raw[:], g_hi[:].bitcast(F32), ALU.subtract).then_inc(w_low, 1)
            if not top2:
                dve.wait_ge(w_high, 2)
                dve.tensor_tensor(o_lo[:], o_raw[:], o_hi[:].bitcast(F32), ALU.subtract).then_inc(w_low, 1)
            dve.wait_ge(ln.half_set, 1)
            dve.wait_ge(made, MADE)
            for ring in (out_ring, gate_ring):
                credit(dve, ring.drained_sem["D"], ring.per["D"])
            credit(dve, rows_left, 1)
            if not top2:
                credit(dve, copied, 16)
            STEPS = 26 if top2 else 22
            taken = [0]

            def then(n, ins):
                taken[0] += 1
                ins.then_inc(step, 1)
                dve.wait_ge(step, STEPS * n + taken[0])

            def bank(n, unit):
                ring = ring_of(unit)
                dve.wait_ge(ring.filled_sem, ring.filled(n, unit))
                return ring.tiles[ring.bank(unit)]

            def taken_by_vector(n, unit):
                ring = ring_of(unit)
                dve.wait_ge(ring.drained_sem["D"], ring.drained(n, ring.at[unit], "D"))

            def low(n, name, hi, lo):
                for i in range(NT):
                    src = bank(n, f"{name}{i}")
                    ring = ring_of(f"{name}{i}")
                    dve.wait_ge(ring.drained_sem["A"], ring.drained(n, ring.at[f"{name}{i}"], "A"))
                    t = slice(TT * i, TT * i + TT)
                    dve.tensor_tensor(lo[:, :, t], src[:, 0:2 * TT].rearrange("p (a t) -> p a t", a=2),
                                      hi[:, :, t].bitcast(F32), ALU.subtract).then_inc(ring.drained_sem["D"], 1)

            def take_heads(n):
                dve.tensor_scalar(ao_now[:], ao[:, bass.ds(NT * n, NT), :], 1.0, None, ALU.mult).then_inc(ao_ready, 1)

            def add_product(n):
                low(n, "A", at_hi, at_lo)
                for unit, tiles in (("Y01", (0, 1)), ("Y2", (2,))):
                    src = bank(n, unit)
                    rows = h[:, bass.ds(NT * n + tiles[0], len(tiles)), :]
                    dve.tensor_tensor(rows, rows, src[0:TT, 0:256 * len(tiles)].rearrange("p (t d) -> p t d", d=256),
                                      ALU.add).then_inc(out_ring.drained_sem["D"], 1)

            def choose(n, lg, k):
                wide = lambda t: t[:].unsqueeze(2).to_broadcast([TT, NT, E])
                then(n, dve.tensor_reduce(best[k][:], lg[:], AX.X, ALU.max))
                then(n, dve.tensor_tensor(equal[:], lg[:], wide(best[k]), ALU.is_equal))
                then(n, dve.tensor_tensor(equal[:], equal[:], order[:], ALU.mult))
                then(n, dve.tensor_reduce(first[k][:], equal[:], AX.X, ALU.max))
                then(n, dve.tensor_tensor(hot[k][:], order[:], wide(first[k]), ALU.is_equal))

            def route(n):
                low(n, "X", xt_hi, xt_lo)
                src = bank(n, "G")
                dve.tensor_tensor(logits[:], src[0:TT, 0:NT * E].rearrange("p (t e) -> p t e", e=E),
                                  bias[:].unsqueeze(1).to_broadcast([TT, NT, E]), ALU.add).then_inc(gate_ring.drained_sem["D"], 1)
                taken_by_vector(n, "G")
                choose(n, logits, 0)
                if top2:
                    then(n, dve.scalar_tensor_tensor(masked[:], hot[0][:], -3.0e38, logits[:], ALU.mult, ALU.add))
                    choose(n, masked, 1)
                    then(n, dve.tensor_tensor(both[:], hot[0][:], hot[1][:], ALU.add))
                    now = both
                    dve.tensor_tensor(shift[:, :, 0], best[1][:], best[0][:], ALU.subtract)
                    dve.memset(shift[:, :, 1:E], 0.0).then_inc(logits_ready, 1)
                else:
                    now = hot[0]
                    dve.tensor_tensor(shift[:], logits[:], best[0][:].unsqueeze(2).to_broadcast([TT, NT, E]),
                                      ALU.subtract).then_inc(logits_ready, 1)
                for i in range(NT):
                    ins = dve.tensor_tensor(before[:, i + 1, :], before[:, i, :], now[:, i, :], ALU.add)
                    if i < NT - 1:
                        then(n, ins)
                ins.then_inc(hot_ready, 1)

            def send(n):
                dve.wait_ge(exp_done, n + 1)
                if top2:
                    then(n, dve.tensor_scalar(prob[:], expo[:, :, 0], 1.0, None, ALU.add))
                    then(n, dve.reciprocal(inverse[:], prob[:]))
                    dve.tensor_copy(table.weight[:, 0, bass.ds(NT * n, NT)], inverse[:])
                    dve.tensor_tensor(table.weight[:, 1, bass.ds(NT * n, NT)], inverse[:], expo[:, :, 0], ALU.mult)
                else:
                    then(n, dve.tensor_reduce(inverse[:], expo[:], AX.X, ALU.add))
                    then(n, dve.reciprocal(prob[:], inverse[:]))
                    then(n, dve.reciprocal(inverse[:], prob[:]))
                    then(n, dve.tensor_tensor(factor[:], prob[:], inverse[:], ALU.mult))
                    dve.wait_ge(rows_left, n + 1)
                    dve.wait_ge(copied, 16 * (n + 1))
                    for i in range(NT):
                        dve.tensor_scalar(xs[:, i, :], xn[:, i, :], factor[:, i:i + 1], None, ALU.mult)
                src = bank(n, "POS")
                dve.tensor_copy(ranks[:], src[0:TT, 0:NT * E].rearrange("p (t e) -> p t e", e=E))\
                    .then_inc(gate_ring.drained_sem["D"], 1)
                taken_by_vector(n, "POS")
                then(n, dve.tensor_copy(before[:, 0, :], before[:, NT, :]))
                if top2:
                    dve.wait_ge(rows_left, n + 1)
                for k in range(K):
                    then(n, dve.tensor_tensor(picked[:], hot[k][:], ranks[:], ALU.mult))
                    then(n, dve.tensor_reduce(place[k][:], picked[:], AX.X, ALU.add))
                    if not top2:
                        then(n, dve.tensor_scalar(kept[:], place[k][:], float(table.capacity), None, ALU.is_le))
                    then(n, dve.tensor_scalar(first[k][:], first[k][:], -float(table.region),
                                              float(E * table.region - 1), ALU.mult, ALU.add))
                    then(n, dve.tensor_tensor(place[k][:], place[k][:], first[k][:], ALU.add))
                    if not top2:
                        then(n, dve.tensor_tensor(place[k][:], place[k][:], token[:], ALU.subtract))
                        then(n, dve.tensor_tensor(place[k][:], place[k][:], kept[:], ALU.mult))
                        then(n, dve.tensor_tensor(place[k][:], place[k][:], token[:], ALU.add))
                        then(n, dve.tensor_scalar(token[:], token[:], float(S), None, ALU.add))
                    dve.tensor_copy((table.place if top2 else table.slots)[:, k, bass.ds(NT * n, NT)], place[k][:])
                    ins = dve.tensor_copy(slot[k][:], place[k][:])
                ins.then_inc(slots_ready, 1)
                assert taken[0] <= STEPS, taken
                while taken[0] < STEPS:
                    then(n, dve.memset(kept[:], 0.0))
                taken[0] = 0

            def normalize(n):
                if top2:
                    dve.wait_ge(rows_left, n + 1)
                ln.on_vector_apply(dve, n)

            if not top2:
                take_heads(0)
                add_product(0)
            ln.on_vector_stats(dve, c.ready, 0)
            normalize(0)
            with dve.Fori(0, B - 1) as b:
                if not top2:
                    take_heads(b + 1)
                route(b)
                if not top2:
                    add_product(b + 1)
                ln.on_vector_stats(dve, c.ready, b + 1)
                send(b)
                normalize(b + 1)
            route(B - 1)
            send(B - 1)
            if top2:
                table.plan(dve, before, total_ready, count_ps, ks, js, plan_step, tails_ready)


class Table:

    def __init__(self, nc, sb, name, experts, region, capacity, own, rows, K, tiles, blocks=0):
        self.experts, self.region, self.capacity, self.own, self.blocks = experts, region, capacity, own, blocks
        self.x_rows = nc.dram_tensor(f"{name}_x_rows", [rows, 256], F32, kind="Internal").ap()
        self.y_rows = nc.dram_tensor(f"{name}_y_rows", [blocks * S if blocks else rows, 256], F32, kind="Internal").ap()
        self.slots = sb(f"{name}_slots", [TT, K, tiles], I32)
        self.zeros = sb(f"{name}_zeros", [TT, 1, 256], F32)
        if K == 2:
            self.place = sb(f"{name}_place", [TT, K, tiles], F32)
            self.x_place = sb(f"{name}_x_place", [TT, K, tiles], F32)
            self.beyond = sb(f"{name}_beyond", [TT, K, tiles], F32)
            self.weight = sb(f"{name}_weight", [TT, K, tiles], F32)
            E = experts
            self.count, self.n_blocks, self.upto, self.gap = (
                sb(f"{name}_{n}", [TT, E], F32) for n in ("count", "n_blocks", "upto", "gap"))
            self.over = sb(f"{name}_over", [TT, E, tiles // NT], F32)
            self.past, self.skip = (sb(f"{name}_{n}", [TT, E, blocks], F32) for n in ("past", "skip"))
            self.row_f, self.expert_f = (sb(f"{name}_{n}", [TT, blocks], F32) for n in ("row_f", "expert_f"))
            self.row, self.expert = (sb(f"{name}_{n}", [TT, blocks], I32) for n in ("row", "expert"))
            self.tails = sb(f"{name}_tails", [TT, E], I32)
            self.at = sb(f"{name}_at", [TT, E], F32)

    def plan(self, dve, before, total_ready, count_ps, ks, js, step, tails_ready):
        E, NB = self.experts, self.blocks
        done = [0]

        def then(ins):
            done[0] += 1
            ins.then_inc(step, 1)
            dve.wait_ge(step, done[0])

        dve.sem_inc(total_ready, 1)
        dve.wait_ge(total_ready, 2)
        then(dve.tensor_copy(self.count[:], count_ps[:, 0:E]))
        then(dve.tensor_tensor(self.over[:], self.count[:].unsqueeze(2).to_broadcast(list(self.over.shape)), ks[:], ALU.is_gt))
        then(dve.tensor_reduce(self.n_blocks[:], self.over[:], AX.X, ALU.add))
        then(dve.tensor_scalar(self.gap[:], self.n_blocks[:], -float(S), float(self.region), ALU.mult, ALU.add))
        then(dve.tensor_copy(self.upto[:], self.n_blocks[:]))
        for e in range(1, E):
            then(dve.tensor_tensor(self.upto[:, e:e + 1], self.upto[:, e - 1:e], self.upto[:, e:e + 1], ALU.add))
        wide = lambda t: t[:].unsqueeze(2).to_broadcast([TT, E, NB])
        then(dve.tensor_tensor(self.past[:], js[:], wide(self.upto), ALU.is_ge))
        then(dve.tensor_tensor(self.skip[:], self.past[:], wide(self.gap), ALU.mult))
        then(dve.tensor_reduce(self.expert_f[:], self.past[:].rearrange("p e j -> p j e"), AX.X, ALU.add))
        then(dve.tensor_scalar(self.expert_f[:], self.expert_f[:], float(E - 1), None, ALU.min))
        then(dve.tensor_reduce(self.row_f[:], self.skip[:].rearrange("p e j -> p j e"), AX.X, ALU.add))
        then(dve.scalar_tensor_tensor(self.row_f[:], js[:, 0, :], float(S), self.row_f[:], ALU.mult, ALU.add))
        then(dve.tensor_scalar(self.row_f[:], self.row_f[:], float(E * self.region), None, ALU.min))
        for e in range(E):
            then(dve.tensor_scalar(self.at[:, e:e + 1], self.count[:, e:e + 1], float(e * self.region), None, ALU.add))
        then(dve.tensor_copy(self.x_place[:], self.place[:]))
        for e in range(E - 1):
            then(dve.tensor_scalar(self.beyond[:], self.x_place[:], float((e + 1) * self.region), self.gap[:, e:e + 1],
                                   ALU.is_ge, ALU.mult))
            then(dve.tensor_tensor(self.place[:], self.place[:], self.beyond[:], ALU.subtract))
        dve.tensor_copy(self.slots[:], self.place[:])
        dve.tensor_copy(self.row[:], self.row_f[:])
        dve.tensor_copy(self.expert[:], self.expert_f[:])
        dve.tensor_copy(self.tails[:], self.at[:]).then_inc(tails_ready, 1)


def feed_forward(nc, sb, ps, sem, tag, c, N, HC, loads, func, factor, packed, b2, source, store, h=None):
    L = "_" + tag
    W = HC * 512
    per_load = {"pair": 2, "block": 1, "once": N}[loads]
    RAWS = 2 if loads == "block" else 1
    biased = b2 is not None
    x_now = [sb(f"x_now{i}" + L, [TT, NT, 256], F32) for i in range(2)]
    xt_hi, xt_lo = ([sb(f"{n}{i}" + L, [P, 2, SP1], F32R) for i in range(2)] for n in ("xt_hi", "xt_lo"))
    raw = [sb(f"raw{i}" + L, [P, W + (HC if biased else 0)], F32) for i in range(RAWS)]
    w_hi, w_lo = (sb(n + L, [P, HC, 512], F32R) for n in ("w_hi", "w_lo"))
    g = [sb(f"g{i}" + L, [P, SP1], F32) for i in range(2)]
    g_hi, g_lo = ([sb(f"{n}{i}" + L, [P, SP1], F32R) for i in range(2)] for n in ("g_hi", "g_lo"))
    if biased:
        bias, factors, b2_now = sb("bias" + L, [P, HC], F32), sb("factors" + L, [P, HC], F32), sb("b2_now" + L, [TT, 256], F32)
        y_now = [sb(f"y_now{i}" + L, [TT, NT, 256], F32) for i in range(2)]
    turn_ps = [ps(f"turn_ps{i}" + L, [P, 512], F32) for i in range(2)]
    up_ps = [ps(f"up_ps{i}" + L, [P, 512], F32) for i in range(2)]
    y_ps = [[ps(f"y_ps{i}{k}" + L, [P, 512], F32) for k in range(2)] for i in range(2)]

    raw_loaded = [sem(f"raw_loaded{i}" + L) for i in range(RAWS)]
    x_loaded = [sem(f"x_loaded{i}" + L) for i in range(2)]
    y_stored = [sem(f"y_stored{i}" + L) for i in range(2)]
    b2_loaded, factors_set, pads_zeroed = sem("b2_loaded" + L), sem("factors_set" + L), sem("pads_zeroed" + L)
    w_high, w_low, turned, xt_high, xt_low = (sem(n + L) for n in ("w_high", "w_low", "turned", "xt_high", "xt_low"))
    up_filled, act_done, g_high, g_low = (sem(n + L) for n in ("up_filled", "act_done", "g_high", "g_low"))
    down_done, y_filled, y_taken = sem("down_done" + L), sem("y_filled" + L), sem("y_taken" + L)

    def walk(eng, step):
        def at(n, k, par):
            if loads == "pair":
                step(n, k, par, k, par == 0, par == 1)
            elif loads == "block":
                step(n, k, par, n, True, True)
            else:
                step(n, k, par, 0, isinstance(n, int) and n == 0, False)

        at(0, 0, 0)
        with eng.Fori(0, (N - 3) // 2) as i:
            at(2 * i + 1, i, 1)
            at(2 * i + 2, i + 1, 0)
        for n in range(1 + 2 * ((N - 3) // 2), N):
            at(n, n // 2, n % 2)

    turns_at = {HC - 3: (0, 1), HC - 2: (2,)}

    with nc.Block() as block:

        @block.sync
        def _(sp):
            def load_weights(e, r):
                sp.dma_start(raw[r][:], packed[bass.ds(e, 1), :, 0:W + (HC if biased else 0)]
                             .rearrange("e p w -> p (e w)")).then_inc(raw_loaded[r], 16)

            def expert_of(n):
                return sp.value_load(source.expert[0:1, bass.ds(n, 1)], min_val=0, max_val=source.experts - 1)

            def load_b2(e):
                sp.dma_start(b2_now[:], b2[bass.ds(e, 1), :].rearrange("e d -> (e d)").partition_broadcast(TT))\
                    .then_inc(b2_loaded, 16)

            def put(n, par):
                sp.wait_ge(y_taken, 6 + 2 * n + 2)
                sp.dma_start(source.to(sp, n), y_now[par][:]).then_inc(y_stored[par], 16)

            load_weights(expert_of(0) if loads == "block" else 0, 0)
            for n in range(2):
                sp.dma_start(x_now[n][:], source.rows(sp, n)).then_inc(x_loaded[n], 16)
            if loads == "block":
                load_weights(expert_of(1), 1)
            if biased:
                load_b2(expert_of(0) if loads == "block" else 0)

            def step(n, k, par, load, is_first, is_last):
                fixed = isinstance(n, int)
                if not (fixed and n == 0) and biased:
                    e = expert_of(n) if loads == "block" else load
                    put(n - 1, 1 - par)
                    if is_first:
                        load_b2(e)
                if loads == "pair" and is_first and not (fixed and load + 1 >= N // 2):
                    sp.wait_ge(w_low, HC * (load + 2))
                    load_weights(load + 1, 0)
                if not (fixed and n + 2 >= N):
                    rows = source.rows(sp, n + 2)
                    if loads == "block":
                        e = expert_of(n + 2)
                        sp.wait_ge(w_low, HC * RAWS + HC * (n + 1))
                        load_weights(e, par)
                    sp.wait_ge(turned, 6 + NT * (n + 1))
                    sp.dma_start(x_now[par][:], rows).then_inc(x_loaded[par], 16)

            walk(sp, step)
            if biased:
                put(N - 1, (N - 1) % 2)
                for par in range(2):
                    sp.wait_ge(y_stored[par], 16 + 16 * ((N + 1 - par) // 2))

        @block.gpsimd
        def _(pool):
            if biased:
                pool.memset(factors[:], factor).then_inc(factors_set, 1)
                pool.wait_ge(factors_set, 1)
            credit(pool, w_low, HC * RAWS)

            def cut(load, m, r):
                pool.wait_ge(w_high, HC * load + m + 1)
                if biased:
                    pool.tensor_tensor(bias[:, m:m + 1], raw[r][:, W + m:W + m + 1], factors[:, m:m + 1], ALU.mult)
                pool.tensor_tensor(w_lo[:, m, :], raw[r][:, 512 * m:512 * m + 512], w_hi[:, m, :].bitcast(F32),
                                   ALU.subtract).then_inc(w_low, 1)

            if loads == "block":
                def both(k):
                    for r in range(2):
                        for m in range(HC):
                            cut(2 * k + r, m, r)
                with pool.Fori(0, N // 2) as k:
                    both(k)
                if N % 2:
                    for m in range(HC):
                        cut(N - 1, m, 0)
            elif loads == "pair":
                with pool.Fori(0, N // 2) as load:
                    for m in range(HC):
                        cut(load, m, 0)
            else:
                for m in range(HC):
                    cut(0, m, 0)

        @block.tensor
        def _(pe):
            pe.wait_ge(pads_zeroed, 1)
            credit(pe, turned, 6)

            def turn(n, k, par, tiles):
                for i in tiles:
                    if i == 0:
                        pe.wait_ge(x_loaded[par], 16 * (k + 1))
                    pe.wait_ge(xt_low, NT * n + i + 1)
                    for a in range(2):
                        got = pe.transpose(turn_ps[(par + i) % 2][:, TT * a:TT * a + TT],
                                           x_now[par][:, i, P * a:P * a + P], c.ident[0:TT, 0:TT])
                    got.then_inc(turned, 1)

            def up(n, par, load, m):
                pe.wait_ge(w_low, HC * RAWS + HC * load + m + 1)
                if m == 0:
                    pe.wait_ge(xt_low, 2 + NT * (n + 1))
                pe.wait_ge(act_done, HC * n + m + 1)
                for a in range(2):
                    for j, (w, x) in enumerate(((w_hi, xt_hi), (w_lo, xt_hi), (w_hi, xt_lo))):
                        got = pe.matmul(up_ps[m % 2][:, 0:SP1], w[:, m, P * a:P * a + P], x[par][:, a, :],
                                        start=(a == 0 and j == 0), stop=(a == 1 and j == 2))
                got.then_inc(up_filled, 1)

            def down(n, par, m):
                pe.wait_ge(g_low, 2 + HC * n + m + 1)
                if m == 0:
                    pe.wait_ge(y_taken, 2 * n + 4)
                for i in range(NT):
                    out = y_ps[par][i // 2][0:TT, 256 * (i % 2):256 * (i % 2) + 256]
                    t = slice(TT * i, TT * i + TT)
                    for j, (x, w) in enumerate(((g_hi, w_hi), (g_lo, w_hi), (g_hi, w_lo))):
                        got = pe.matmul(out, x[m % 2][:, t], w[:, m, 256:512], start=(m == 0 and j == 0 and i != 1),
                                        stop=(m == HC - 1 and j == 2), skip_group_check=True)
                got.then_inc(down_done, 1)

            turn(0, 0, 0, range(NT))

            def step(n, k, par, load, is_first, is_last):
                fixed = isinstance(n, int)
                for m in range(HC):
                    up(n, par, load, m)
                    if m > 0:
                        down(n, par, m - 1)
                    elif not (fixed and n == 0):
                        down(n - 1, 1 - par, HC - 1)
                    if not (fixed and n + 1 >= N):
                        turn(n + 1, k + par, 1 - par, turns_at.get(m, ()))

            walk(pe, step)
            down(N - 1, (N - 1) % 2, HC - 1)

        @block.scalar
        def _(act):
            credit(act, act_done, 2)

            def high(n, par, tiles):
                for i in tiles:
                    act.wait_ge(turned, 6 + NT * n + i + 1)
                    act.copy(xt_hi[par][:, :, TT * i:TT * i + TT],
                             turn_ps[(par + i) % 2][:, 0:2 * TT].rearrange("p (a t) -> p a t", a=2)).then_inc(xt_high, 1)

            def activate(n, m):
                act.wait_ge(g_low, HC * n + m + 1)
                act.wait_ge(up_filled, HC * n + m + 1)
                act.activation(g[m % 2][:, 0:SP1], up_ps[m % 2][:, 0:SP1], func, scale=factor,
                               **({"bias": bias[:, m:m + 1]} if biased else {})).then_inc(act_done, 1)

            act.wait_ge(pads_zeroed, 1)

            def cut(m, k, r, last_block):
                if m == 0:
                    act.wait_ge(raw_loaded[r], 16 * (k + 1))
                if last_block is not None:
                    act.wait_ge(down_done, HC * last_block + m + 1)
                act.copy(w_hi[:, m, :], raw[r][:, 512 * m:512 * m + 512]).then_inc(w_high, 1)

            cut(0, 0, 0, None)
            high(0, 0, range(NT))
            for m in range(1, HC):
                cut(m, 0, 0, None)

            def step(n, k, par, load, is_first, is_last):
                fixed = isinstance(n, int)
                for m in range(HC):
                    activate(n, m)
                    if not (fixed and n + 1 >= N):
                        high(n + 1, 1 - par, turns_at.get(m, ()))
                    if m >= 2 and is_last and not (fixed and n + 1 >= N):
                        if loads == "pair":
                            cut(m - 2, load + 1, 0, n)
                        else:
                            cut(m - 2, k + par, 1 - par, n)
                    if m < 2 and is_first and not (fixed and n == 0) and loads != "once":
                        cut(HC - 2 + m, None, 0 if loads == "pair" else par, n - 1)

            walk(act, step)

        @block.vector
        def _(dve):
            for z in (*xt_hi, *xt_lo):
                ins = dve.memset(z[:].bitcast(F32), 0.0)
            ins.then_inc(pads_zeroed, 1)
            credit(dve, xt_low, 2)
            credit(dve, g_low, 2)
            credit(dve, y_taken, 6)
            if biased:
                for par in range(2):
                    credit(dve, y_stored[par], 16)

            def low(n, par, tiles):
                for i in tiles:
                    dve.wait_ge(xt_high, NT * n + i + 1)
                    t = slice(TT * i, TT * i + TT)
                    dve.tensor_tensor(xt_lo[par][:, :, t],
                                      turn_ps[(par + i) % 2][:, 0:2 * TT].rearrange("p (a t) -> p a t", a=2),
                                      xt_hi[par][:, :, t].bitcast(F32), ALU.subtract).then_inc(xt_low, 1)

            def cut(n, m):
                dve.wait_ge(act_done, 2 + HC * n + m + 1)
                dve.tensor_copy(g_hi[m % 2][:], g[m % 2][:]).then_inc(g_high, 1)
                dve.wait_ge(g_high, HC * n + m + 1)
                dve.tensor_tensor(g_lo[m % 2][:], g[m % 2][:], g_hi[m % 2][:].bitcast(F32), ALU.subtract).then_inc(g_low, 1)

            def take(n, k, par, load):
                dve.wait_ge(down_done, HC * (n + 1))
                if biased:
                    dve.wait_ge(b2_loaded, 16 * (load + 1))
                    dve.wait_ge(y_stored[par], 16 * (k + 1))
                for b, tiles in ((0, 2), (1, 1)):
                    src = y_ps[par][b][0:TT, 0:256 * tiles].rearrange("p (t d) -> p t d", d=256)
                    if biased:
                        ins = dve.scalar_tensor_tensor(y_now[par][:, 2 * b:2 * b + tiles, :], src, 1.0 / factor,
                                                       b2_now[:].unsqueeze(1).to_broadcast([TT, tiles, 256]),
                                                       ALU.mult, ALU.add)
                    else:
                        rows = h[:, bass.ds(NT * n + 2 * b, tiles), :]
                        ins = dve.tensor_tensor(rows, rows, src, ALU.add)
                    ins.then_inc(y_taken, 1)

            low(0, 0, range(NT))

            def step(n, k, par, load, is_first, is_last):
                fixed = isinstance(n, int)
                for m in range(HC):
                    cut(n, m)
                    if m == 0 and not (fixed and n == 0):
                        take(n - 1, k - 1 + par, 1 - par, load - 1 if is_first and loads != "once" else load)
                    if not (fixed and n + 1 >= N):
                        low(n + 1, 1 - par, turns_at.get(m, ()))

            walk(dve, step)
            last = N - 1
            take(last, last // 2, last % 2, last // per_load)


class ExpertRows:

    def __init__(self, table):
        self.table, self.experts = table, table.experts
        self.expert = table.expert if table.blocks else None

    def rows(self, sp, n):
        at = S * n
        if self.table.blocks:
            at = sp.value_load(self.table.row[0:1, bass.ds(n, 1)], min_val=0,
                               max_val=self.table.experts * self.table.region)
        return self.table.x_rows[bass.ds(at, S), :].rearrange("(p t) d -> p t d", t=NT)

    def to(self, sp, n):
        return self.table.y_rows[bass.ds(S * n, S), :].rearrange("(p t) d -> p t d", t=NT)


class TokenRows:

    def __init__(self, tokens):
        self.tokens = tokens

    def rows(self, sp, n):
        return self.tokens[:, bass.ds(NT * n, NT), :]


def combine(nc, sb, ps, sem, layer, h, table, B, out=None):
    L = f"_c{layer}"
    K = 2 if layer == 1 else 1
    slot = [sb(f"slot{i}" + L, [TT, NT, K], I32) for i in range(2)]
    y = [[sb(f"y{i}{k}" + L, [TT, NT, 256], F32) for k in range(K)] for i in range(2)]
    part, total = ([sb(f"{n}{i}" + L, [TT, NT, 256], F32) for i in range(2)] for n in ("part", "total"))
    slots_set, gathered, slots_seen = sem("slots_set" + L), [sem(f"gathered{i}" + L) for i in range(2)], sem("slots_seen" + L)
    weight = [sb(f"weight{i}" + L, [TT, K, NT], F32) for i in range(2)]
    weight_set = sem("weight_set" + L)
    step, summed, stored = sem("step" + L), sem("summed" + L), [sem(f"stored{i}" + L) for i in range(2)]

    with nc.Block() as block:

        @block.sync
        def _(sp):
            if K == 2:
                with sp.Fori(0, B // 2) as i:
                    for par in range(2):
                        sp.wait_ge(summed, 2 * i + par + 1 + 2)
                        sp.dma_start(out[bass.ds(2 * i + par, 1)].rearrange("b (t p) d -> p (b t) d", p=TT),
                                     total[par][:]).then_inc(stored[par], 16)
                for par in range(2):
                    sp.wait_ge(stored[par], 16 * (B // 2) + 16)

        @block.gpsimd
        def _(pool):
            with pool.Fori(0, B // 2) as i:
                for par in range(2):
                    pool.wait_ge(slots_set, 2 * i + par + 1)
                    pool.sem_inc(slots_seen, 1)
                    for t in range(NT):
                        for k in range(K):
                            pool.indirect_dma_start(y[par][k][:, t, :], None, table.y_rows,
                                                    bass.IndirectOffsetOnAxis(ap=slot[par][:, t, k:k + 1], axis=0))\
                                .then_inc(gathered[par], 16)

        @block.vector
        def _(dve):
            for par in range(2):
                credit(dve, stored[par], 16)
            credit(dve, summed, 2)

            def point(n, par):
                for k in range(K):
                    ins = dve.tensor_copy(slot[par][:, :, k], table.slots[:, k, bass.ds(NT * n, NT)])
                    if K == 2:
                        dve.tensor_copy(weight[par][:, k], table.weight[:, k, bass.ds(NT * n, NT)]).then_inc(weight_set, 1)
                ins.then_inc(slots_set, 1)

            def add(n, i, par):
                dve.wait_ge(gathered[par], 16 * NT * K * (i + 1))
                rows = h[:, bass.ds(NT * n, NT), :]
                if K == 1:
                    dve.tensor_tensor(rows, rows, y[par][0][:], ALU.add)
                else:
                    w = [weight[par][:, k].unsqueeze(2).to_broadcast([TT, NT, 256]) for k in range(2)]
                    dve.wait_ge(weight_set, 2 * n + 2)
                    dve.wait_ge(summed, n + 2)
                    dve.tensor_tensor(part[0][:], y[par][0][:], w[0], ALU.mult)
                    dve.tensor_tensor(part[1][:], y[par][1][:], w[1], ALU.mult).then_inc(step, 1)
                    dve.wait_ge(step, 2 * n + 1)
                    dve.tensor_tensor(part[0][:], part[0][:], part[1][:], ALU.add).then_inc(step, 1)
                    dve.wait_ge(step, 2 * n + 2)
                    dve.wait_ge(stored[par], 16 * i + 16)
                    dve.tensor_tensor(total[par][:], part[0][:], rows, ALU.add).then_inc(summed, 1)

            point(0, 0)
            point(1, 1)
            with dve.Fori(0, B // 2 - 1) as i:
                for par in range(2):
                    add(2 * i + par, i, par)
                    point(2 * i + par + 2, par)
            for par in range(2):
                add(B - 2 + par, B // 2 - 1, par)


class Constants:

    def __init__(self, sb, sem):
        self.ident, self.ident_bf = sb("ident", [P, P], F32), sb("ident_bf", [TT, TT], BF16)
        self.zeroed, self.made, self.ready = sem("ident_zeroed"), sem("ident_made"), sem("constants_ready")

    def make(self, nc):
        with nc.Block() as block:
            @block.gpsimd
            def _(pool):
                for m in (self.ident, self.ident_bf):
                    pool.memset(m[:], 0.0).then_inc(self.zeroed, 1)
                pool.wait_ge(self.zeroed, 2)
                for m, n in ((self.ident, P), (self.ident_bf, TT)):
                    pool.affine_select(out=m[:], in_=m[:], compare_op=ALU.not_equal, fill=1.0, base=0,
                                       pattern=[[-1, n]], channel_multiplier=1).then_inc(self.made, 1)
                pool.wait_ge(self.made, 2)
                pool.sem_inc(self.ready, 1)


def program(nc, x, txt, scharr, w_dq, w_uq, w_dkv, w_uk, w_uv, w_o, w_sw, b_sw, f_w, f_b1, f_b2,
            wqT, wkT, wvT, rope_cos, rope_sin, m_w, w_g, b_g, e_w, e_b1, e_b2, out):
    with ExitStack() as whole:
        def sem(name):
            return whole.enter_context(nc.semaphore(name))

        def stage(step, *args):
            semaphores = []

            def own_sem(name):
                semaphores.append(nc.alloc_semaphore(name))
                return semaphores[-1]

            with ExitStack() as own:
                step(nc, lambda n, s, d: own.enter_context(nc.sbuf_tensor(n, s, d)),
                     lambda n, s, d: own.enter_context(nc.psum_tensor(n, s, d)), own_sem, *args)
            nc.clear_and_free_semaphores(semaphores)
            nc.all_engine_barrier()

        whole_sb = lambda n, s, d: whole.enter_context(nc.sbuf_tensor(n, s, d))
        B = x.shape[0]
        h = whole_sb("h", [TT, NT * B, 256], F32)
        c = Constants(whole_sb, sem)
        c.make(nc)
        stage(load_and_cut_image, x, txt, scharr, h)
        cap = B * S // f_b1.shape[0]
        own = f_b1.shape[0] * cap
        switch = Table(nc, whole_sb, "switch", f_b1.shape[0], cap, cap, own, own + B * S, 1, NT * B)
        region = (B + 1) * S
        top = Table(nc, whole_sb, "top2", e_b1.shape[0], region, 0, 0, e_b1.shape[0] * region + S, 2, NT * B,
                    blocks=2 * B + e_b1.shape[0] - 1)
        with nc.sbuf_tensor("ao", [TT, NT * B, 256], F32) as ao:
            stage(attention, 0, c, h, ao, B, (w_dq, w_dkv, w_uq, w_uk, w_uv), switch)
            stage(dispatch, 0, c, h, ao, B, w_o, w_sw, b_sw, switch)
        stage(feed_forward, "e0", c, 2 * f_b1.shape[0], 8, "pair", ACT.Gelu, np.sqrt(2.0) / 1.41421, f_w, f_b2,
              ExpertRows(switch), True)
        stage(combine, 0, h, switch, B)
        with nc.sbuf_tensor("ao1", [TT, NT * B, 256], F32) as ao:
            stage(attention, 1, c, h, ao, B, (wqT, wkT, wvT, rope_cos, rope_sin))
            stage(feed_forward, "mlp", c, B, 8, "once", ACT.Silu, 1.0, m_w, None, TokenRows(ao), False, h)
        stage(dispatch, 1, c, h, None, B, None, w_g, b_g, top)
        stage(feed_forward, "e1", c, top.blocks, 4, "block", ACT.Gelu, 1.0, e_w, e_b2, ExpertRows(top), True)
        stage(combine, 1, h, top, B, out)

def pack(w1, w2, b1=None):
    E, D, F = w1.shape
    up = w1.reshape(E, 2, P, F // P, P).transpose(0, 2, 3, 1, 4).reshape(E, P, F // P, 2 * P)
    down = w2.reshape(E, F // P, P, D).transpose(0, 2, 1, 3)
    both = np.concatenate([up, down], axis=3).reshape(E, P, F * 4)
    return both if b1 is None else np.concatenate([both, b1.reshape(E, F // P, P).transpose(0, 2, 1)], axis=2)


def rope_tables():
    half = 8
    inv_freq = (np.float32(1.0) / np.float32(10000.0) ** (np.arange(0, 2 * half, 2, dtype=np.float32) / np.float32(2 * half)))
    freqs = (np.arange(S, dtype=np.float32)[:, None] * inv_freq[None, :].astype(np.float32)).astype(np.float32)
    cos, sin = np.cos(freqs), np.sin(freqs)
    return [np.ascontiguousarray(t.reshape(NT, TT, 2 * half).transpose(1, 0, 2).astype(np.float32))
            for t in (np.concatenate([cos, cos], 1), np.concatenate([-sin, sin], 1))]


def lay_out(v):
    v = {k: np.asarray(a) for k, a in v.items()}
    cos, sin = rope_tables()
    return {
        "x": v["x"], "txt": v["txt"], "scharr": v["L0_tok_scharr"], "w_dq": v["L0_attn_W_dq"],
        "w_uq": v["L0_attn_W_uq"], "w_dkv": v["L0_attn_W_dkv"], "w_uk": v["L0_attn_W_uk"], "w_uv": v["L0_attn_W_uv"],
        "w_o": v["L0_attn_W_o"], "w_sw": v["L0_ffn_W_sw"], "b_sw": v["L0_ffn_b_sw"],
        "f_w": pack(v["L0_ffn_W1"], v["L0_ffn_W2"], v["L0_ffn_b1"]), "f_b1": v["L0_ffn_b1"], "f_b2": v["L0_ffn_b2"],
        "wqT": v["L1_attn_Wq"].T, "wkT": v["L1_attn_Wk"].T, "wvT": v["L1_attn_Wv"].T, "rope_cos": cos, "rope_sin": sin,
        "m_w": pack(v["L1_attn_W1"].T[None], v["L1_attn_W2"].T[None]), "w_g": v["L1_ffn_Wg"], "b_g": v["L1_ffn_bg"],
        "e_w": pack(v["L1_ffn_W1"], v["L1_ffn_W2"], v["L1_ffn_b1"]), "e_b1": v["L1_ffn_b1"], "e_b2": v["L1_ffn_b2"],
    }


_OUTS = [((16, S, 256), 'float32')]


def kernel(**inputs):
    import numpy as _np
    import concourse.bacc as _bacc
    from concourse import mybir as _mybir
    from concourse.bass_utils import run_bass_kernel_spmd as _run

    nc = _bacc.Bacc("TRN2", target_bir_lowering=False, num_devices=1)
    arrays, args = {}, []
    for name, a in lay_out(inputs).items():
        a = _np.ascontiguousarray(a)
        arrays[f"in_{name}_dram"] = a
        args.append(nc.dram_tensor(f"in_{name}_dram", a.shape, _mybir.dt.from_np(a.dtype), kind="ExternalInput").ap())
    for i, (shape, dtype) in enumerate(_OUTS):
        dt = _mybir.dt.from_np(_np.dtype(dtype))
        args.append(nc.dram_tensor(f"out_{i}_dram", shape, dt, kind="ExternalOutput").ap())
    program(nc, *args)
    r = _run(nc, [arrays], core_ids=[0])
    return r.results[0]["out_0_dram"]
```

```python
from contextlib import ExitStack

import numpy as np

import concourse.bass as bass
from concourse import mybir

F32 = mybir.dt.float32
F32R = mybir.dt.float32r
BF16 = mybir.dt.bfloat16
I32 = mybir.dt.int32
ALU = mybir.AluOpType
ACT = mybir.ActivationFunctionType
AX = mybir.AxisListType

P = 128
TT = 111
NT = 3
S = TT * NT
SP1 = S + 1
SCALE = 0.25
MASKED = -1e30
EPS = 1e-5


class Ring:

    def __init__(self, banks, units):
        self.banks, self.names, self.who = banks, [u for u, _ in units], [w for _, w in units]
        self.at = {u: k for k, u in enumerate(self.names)}
        self.real = sum(1 for w in self.who if w)
        self.per = {e: sum(e in w for w in self.who) for e in "AD"}
        assert len(units) % banks == 0

    def bank(self, unit):
        return self.at[unit] % self.banks

    def filled(self, rnd, unit):
        return rnd * self.real + sum(1 for w in self.who[: self.at[unit] + 1] if w)

    def drained(self, rnd, k, engine):
        return (rnd + 1) * self.per[engine] + sum(engine in w for w in self.who[: k + 1])

    def before(self, rnd, unit):
        k, back = self.at[unit] - self.banks, 0
        while not self.who[k % len(self.who)]:
            k -= self.banks
        while k < 0:
            k, back = k + len(self.who), back + 1
        return [(e, self.drained(rnd - back, k, e)) for e in self.who[k]]


def flat(ap):
    return ap.rearrange("p a b -> p (a b)")


def credit(eng, sem, n):
    eng.sem_inc(sem, n)


def load_and_cut_image(nc, sb, ps, sem, x, txt, scharr, h):
    B = x.shape[0]
    ROW0 = [0, 110, 128]
    OFF = [-1, 0, 93]
    ROWS = [TT, TT, 256 - 2 * TT]
    taps = sb("taps", [P, 18], F32)
    diag = sb("diag", [P, 3, NT, TT], F32)
    band = sb("band", [P, 6, NT, TT], F32)
    band_hi = sb("band_hi", [P, 6, NT, TT], F32R)
    band_lo = sb("band_lo", [P, 6, NT, TT], F32R)
    img = [[sb(f"img{i}{t}", [P, 3, 256], F32) for t in range(NT)] for i in range(2)]
    red = [sb(f"red{t}", [P, 256], F32) for t in range(NT)]
    redgreen = [sb(f"redgreen{t}", [P, 256], F32) for t in range(NT)]
    gray = [sb(f"gray{t}", [P, 258], F32) for t in range(NT)]
    gray_hi = [sb(f"gray_hi{t}", [P, 258], F32R) for t in range(NT)]
    gray_lo = [sb(f"gray_lo{t}", [P, 258], F32R) for t in range(NT)]
    halves = [sb(f"halves{t}", [TT, 512], F32) for t in range(NT)]
    edge_ps = [ps(f"edge_ps{t}", [P, 512], F32) for t in range(NT)]

    taps_loaded, txt_loaded = sem("taps_loaded"), sem("txt_loaded")
    diag_made, band_step, band_high = sem("diag_made"), sem("band_step"), sem("band_high")
    img_loaded = [[sem(f"img_loaded{i}{t}") for t in range(NT)] for i in range(2)]
    red_scaled, gray_step, gray_made = sem("red_scaled"), sem("gray_step"), sem("gray_made")
    gray_high, gray_low, edges_summed = sem("gray_high"), sem("gray_low"), sem("edges_summed")
    halves_made, edges_added, pads_zeroed = sem("halves_made"), sem("edges_added"), sem("pads_zeroed")

    def rotate(eng, step):
        step(0, 0, 0)
        with eng.Fori(0, (B - 2) // 2) as k:
            step(2 * k + 1, k, 1)
            step(2 * k + 2, k + 1, 0)
        step(B - 1, B // 2 - 1, 1)
        step(None, None, None)

    with nc.Block() as block:

        @block.sync
        def _(sp):
            sp.dma_start(taps[:], scharr.rearrange("o i y x -> (i o y x)").partition_broadcast(P)).then_inc(taps_loaded, 16)
            sp.dma_start(h[ROWS[2]:TT, 2::NT, :], txt.rearrange("b r d -> r b d")).then_inc(txt_loaded, 16)
            with sp.Fori(0, B // 2) as k:
                for i in range(2):
                    for t in range(NT):
                        sp.wait_ge(gray_made, NT * (2 * k + i) + t + 1)
                        sp.dma_start(img[i][t][:], x[bass.ds(2 * k + i, 1), :, ROW0[t]:ROW0[t] + P, :]
                                     .rearrange("b c p w -> p (b c) w")).then_inc(img_loaded[i][t], 16)
            sp.wait_ge(txt_loaded, 16)

        @block.gpsimd
        def _(pool):
            pool.memset(diag[:], 1.0).then_inc(diag_made, 1)
            pool.wait_ge(diag_made, 1)
            for k in range(3):
                for t in range(NT):
                    pool.affine_select(out=diag[:, k, t, :], in_=diag[:, k, t, :], compare_op=ALU.is_equal,
                                       fill=0.0, base=-(OFF[t] + k), pattern=[[-1, TT]],
                                       channel_multiplier=1).then_inc(diag_made, 1)

        @block.scalar
        def _(act):
            act.wait_ge(band_step, 18)
            act.copy(band_hi[:], band[:]).then_inc(band_high, 1)
            credit(act, halves_made, NT)
            act.wait_ge(pads_zeroed, 2 * NT)
            def image(b, k, i):
                def whiten(t):
                    act.wait_ge(img_loaded[i][t], 16 * k + 16)
                    act.activation(red[t][:], img[i][t][:, 0, :], ACT.Copy, scale=0.2989).then_inc(red_scaled, 1)

                def high(t):
                    act.wait_ge(gray_made, NT * (b + 2) + t + 1)
                    act.wait_ge(edges_summed, NT * b + t + 1)
                    act.copy(gray_hi[t][:, 1:257], gray[t][:, 1:257]).then_inc(gray_high, 1)

                def halve(t):
                    act.wait_ge(edges_summed, NT * (b + 1) + t + 1)
                    act.wait_ge(edges_added, NT * b + t + 1)
                    act.activation(halves[t][0:ROWS[t], :], edge_ps[t][0:ROWS[t], :], ACT.Abs,
                                   scale=0.5).then_inc(halves_made, 1)

                return lambda t: (whiten(t), high(t)), halve

            def step(b, k, i):
                for t in range(NT):
                    if b is not None:
                        image(b, k, i)[0](t)
                    if not (isinstance(b, int) and b == 0):
                        image(B - 1 if b is None else b - 1, None, None)[1](t)

            rotate(act, step)

        @block.vector
        def _(dve):
            for t in range(NT):
                dve.memset(gray_hi[t][:].bitcast(F32)[:, 0:258:257], 0.0).then_inc(pads_zeroed, 1)
                dve.memset(gray_lo[t][:].bitcast(F32)[:, 0:258:257], 0.0).then_inc(pads_zeroed, 1)
            dve.wait_ge(taps_loaded, 16)
            dve.wait_ge(diag_made, 10)
            for k in range(3):
                for o in range(2):
                    for dx in range(3):
                        tap = taps[:, 9 * o + 3 * k + dx:9 * o + 3 * k + dx + 1]
                        at = band[:, 3 * o + dx, :, :]
                        if k == 0:
                            dve.tensor_scalar(at, diag[:, k, :, :], tap, None, ALU.mult).then_inc(band_step, 1)
                        else:
                            dve.wait_ge(band_step, 6 * (k - 1) + 3 * o + dx + 1)
                            dve.scalar_tensor_tensor(at, diag[:, k, :, :], tap, at, ALU.mult, ALU.add).then_inc(band_step, 1)
            dve.wait_ge(band_step, 18)
            dve.wait_ge(band_high, 1)
            dve.tensor_tensor(band_lo[:], band[:], band_hi[:].bitcast(F32), ALU.subtract).then_inc(band_step, 1)
            credit(dve, gray_made, 2 * NT)
            credit(dve, edges_added, NT)
            def image(b, k, i):
                def mix(t):
                    dve.wait_ge(red_scaled, NT * b + t + 1)
                    dve.scalar_tensor_tensor(redgreen[t][:], img[i][t][:, 1, :], 0.587, red[t][:],
                                             ALU.mult, ALU.add).then_inc(gray_step, 1)
                    dve.wait_ge(gray_step, NT * b + t + 1)
                    dve.scalar_tensor_tensor(gray[t][:, 1:257], img[i][t][:, 2, :], 0.114, redgreen[t][:],
                                             ALU.mult, ALU.add).then_inc(gray_made, 1)

                def low(t):
                    dve.wait_ge(gray_high, NT * b + t + 1)
                    dve.tensor_tensor(gray_lo[t][:, 1:257], gray[t][:, 1:257],
                                      gray_hi[t][:, 1:257].bitcast(F32), ALU.subtract).then_inc(gray_low, 1)

                def add(t):
                    dve.wait_ge(halves_made, NT * (b + 1) + t + 1)
                    n = ROWS[t]
                    dve.tensor_tensor(h[0:n, bass.ds(NT * b + t, 1), :].rearrange("p a d -> p (a d)"),
                                      halves[t][0:n, 0:256], halves[t][0:n, 256:512], ALU.add).then_inc(edges_added, 1)

                return lambda t: (mix(t), low(t)), add

            def step(b, k, i):
                for t in range(NT):
                    if b is not None:
                        image(b, k, i)[0](t)
                    if not (isinstance(b, int) and b == 0):
                        image(B - 1 if b is None else b - 1, None, None)[1](t)

            rotate(dve, step)

        @block.tensor
        def _(pe):
            pe.wait_ge(band_step, 19)
            pe.wait_ge(pads_zeroed, 2 * NT)
            credit(pe, edges_summed, NT)
            with pe.Fori(0, B) as b:
                for t in range(NT):
                    pe.wait_ge(gray_low, NT * b + t + 1)
                    pe.wait_ge(halves_made, NT * b + t + 1)
                    for o in range(2):
                        n = 0
                        for dx in range(3):
                            for w, g in ((band_hi, gray_hi), (band_lo, gray_hi), (band_hi, gray_lo)):
                                last = pe.matmul(edge_ps[t][0:ROWS[t], 256 * o:256 * o + 256],
                                                 w[:, 3 * o + dx, t, 0:ROWS[t]], g[t][:, dx:dx + 256],
                                                 start=(n == 0), stop=(n == 8))
                                n += 1
                    last.then_inc(edges_summed, 1)


class LayerNorm:

    def __init__(self, sb, sem, tag, h, xn, tiles=NT):
        self.h, self.xn, self.tiles = h, xn, tiles
        self.stats = sb(f"ln_stats{tag}", [TT, self.tiles, 6], F32)
        self.mean_var = sb(f"ln_mean_var{tag}", [TT, self.tiles, 2], F32)
        self.var_eps = sb(f"ln_var_eps{tag}", [TT, self.tiles], F32)
        self.rstd = sb(f"ln_rstd{tag}", [TT, self.tiles], F32)
        self.minus_half = sb(f"ln_minus_half{tag}", [TT, self.tiles], F32)
        self.aggr_done = sem(f"ln_aggr_done{tag}")
        self.var_ready, self.rstd_ready = sem(f"ln_var_ready{tag}"), sem(f"ln_rstd_ready{tag}")
        self.xn_ready, self.half_set = sem(f"ln_xn_ready{tag}"), sem(f"ln_half_set{tag}")

    def tile(self, n, i):
        return self.h[:, bass.ds(self.tiles * n + i, 1), :].rearrange("p a d -> p (a d)")

    def on_vector_stats(self, dve, started, n):
        dve.wait_ge(started, 1)
        dve.drain()
        for i in range(self.tiles):
            dve.bn_stats(self.stats[:, i, :], self.tile(n, i))
        dve.drain()
        for i in range(self.tiles):
            dve.bn_aggr(self.mean_var[:, i, :], self.stats[:, i, :]).then_inc(self.aggr_done, 1)
        dve.wait_ge(self.aggr_done, self.tiles * n + self.tiles)
        dve.tensor_scalar(self.var_eps[:], self.mean_var[:, :, 1], EPS, None, ALU.add).then_inc(self.var_ready, 1)

    def on_vector_apply(self, dve, n):
        dve.wait_ge(self.rstd_ready, n + 1)
        for i in range(self.tiles):
            last = dve.tensor_scalar(self.xn[:, i, :], self.tile(n, i), self.mean_var[:, i, 0:1],
                                     self.rstd[:, i:i + 1], ALU.subtract, ALU.mult)
            last.then_inc(self.xn_ready, 1)

    def on_pool(self, pool, n):
        pool.wait_ge(self.var_ready, n + 1)
        pool.tensor_tensor(self.rstd[:], self.var_eps[:], self.minus_half[:], ALU.pow).then_inc(self.rstd_ready, 1)


def attention(nc, sb, ps, sem, layer, c, h, ao, B, weights, table=None):
    L = f"_a{layer}"
    H, D = 16, 16
    window = layer == 1
    KV = 4 if window else 16
    SLOTS = 16
    KH = 2 * KV if window else H
    K_TILES = range(0, 8, 2 if window else 1)
    SCORES_AT = [0, 1, 2, 3, 5, 6, 8, 10]
    WEIGH_AT = [1, 2, 3, 4, 6, 7, 9, 11]
    BACK_AT = [3, 5, 8, 12]
    PAIRS_AT = [5, 5, 6, 7, 8, 9, 10, 10]
    FIRST_AT = [6, 7, 8, 9, 10, 11, 12, 13]
    SHIFT_AT = [8, 9, 10, 11, 12, 13, 14, 15]

    def at(slots, s):
        return [k for k, slot in enumerate(slots) if slot == s]

    PADT = TT + 1
    SPAN = 128
    K0 = [0, 0, (2 * TT - SPAN + 1) // 2 * 2 if window else 0]
    NK = [PADT, TT * 2, SP1 - K0[2]]
    NQ = [TT + SPAN - 1 if window else SP1, TT * 2, PADT]
    common = [(f"X{i}", "AD") for i in range(NT)] + ([] if window else [("C", "AD")])
    common += [(f"QK{i}", "D" if window else "AD") for i in range(NT)]
    units = list(common)
    for s in range(SLOTS):
        for u in at(FIRST_AT, s):
            units += [(f"S{u}_{k}", "D") for k in range(4)]
        for p in at(PAIRS_AT, s):
            units += [(f"TK{p}", "A")] * (p in K_TILES) + [(f"TQ{p}", "A")]
        units += [(f"R{p}", "A") for p in at(SHIFT_AT, s)]
    units += [(f"V{i}", "A") for i in range(NT)]
    while len(units) % 3:
        units.append(("unused" + str(len(units)), ""))
    ring = Ring(3, units)

    xn = sb("xn" + L, [TT, NT, 256], F32)
    xt_hi, xt_lo = sb("xt_hi" + L, [P, 2, SP1], F32R), sb("xt_lo" + L, [P, 2, SP1], F32R)
    qpad, kpad = sb("qpad" + L, [TT, NT, H, 64], F32), sb("kpad" + L, [TT, NT, KH, 64], F32)
    vaug = sb("vaug" + L, [TT, NT, KV, 32], F32)
    ident_r = sb("ident_r" + L, [TT, PADT], F32R)
    out_t = [sb(f"out_t{i}" + L, [P, S], F32) for i in range(2)]
    q_first = [sb(f"q_first{i}" + L, [P, SP1], F32R) for i in range(4)]
    q_shift = sb("q_shift" + L, [P, 8, SP1], F32R)
    k_t = sb("k_t" + L, [P, KH, SP1], F32R)
    neg_max = [sb(f"neg_max{i}" + L, [TT, NT, 2], F32) for i in range(2)]
    probs = [sb(f"probs{i}" + L, [TT, 3, 448], F32) for i in range(2)]
    rsum = [sb(f"rsum{i}" + L, [TT, NT, 4], F32) for i in range(2)]
    MW = SP1 if window else PADT
    mask_s = sb("mask_s" + L, [TT, NT if window else 1, MW], BF16)
    mask_t = sb("mask_t" + L, [TT, NQ[0] if window else PADT], BF16)
    ln = LayerNorm(sb, sem, L, h, xn)

    if window:
        ffn_rows, slot = sb("ffn_rows" + L, [TT, NT, 256], F32), sb("slot" + L, [TT, NT], I32)
        slots_set, slots_seen, gathered, rows_added = (sem(n + L) for n in ("slots_set", "slots_seen", "gathered", "rows_added"))
        W3 = 384
        w_raw, w_hi, w_lo = (sb(n + L, [P, 2, W3], d) for n, d in (("w_raw", F32), ("w_hi", F32R), ("w_lo", F32R)))
        cos, sin = sb("cos" + L, [TT, NT, D], F32), sb("sin" + L, [TT, NT, D], F32)
        qk_cos, qk_sin, qk_rot = (sb(n + L, [TT, NT, 20, D], F32) for n in ("qk_cos", "qk_sin", "qk_rot"))
    else:
        c_hi, c_lo = sb("c_hi" + L, [P, SP1], F32R), sb("c_lo" + L, [P, SP1], F32R)
        d_raw, d_hi, d_lo = (sb(n + L, [P, 2, P], d) for n, d in (("d_raw", F32), ("d_hi", F32R), ("d_lo", F32R)))
        w_raw, w_hi, w_lo = (sb(n + L, [P, 768], d) for n, d in (("w_raw", F32), ("w_hi", F32R), ("w_lo", F32R)))

    work = [ps(f"work{i}" + L, [P, 512], F32) for i in range(3)]
    score_t = [ps(f"score_t{i}" + L, [TT, 512], F32) for i in range(3)]
    heads_t = ps("heads_t" + L, [P, 512], F32)
    heads = ps("heads" + L, [TT, NT, 4, 32], F32)

    w_loaded, w_zeroed, w_high, w_low = (sem(n + L) for n in ("w_loaded", "w_zeroed", "w_high", "w_low"))
    masks_made, cleared, pads_zeroed = sem("masks_made" + L), sem("cleared" + L), sem("pads_zeroed" + L)
    filled = sem("work_filled" + L)
    drained = {"A": sem("act_drained" + L), "D": sem("dve_drained" + L)}
    max_high, max_placed = sem("max_high" + L), sem("max_placed" + L)
    score_filled, exp_done, av_done = sem("score_filled" + L), sem("exp_done" + L), sem("av_done" + L)
    sums_inverted, heads_done = sem("sums_inverted" + L), sem("heads_done" + L)
    heads_t_taken, heads_turned = sem("heads_t_taken" + L), sem("heads_turned" + L)
    k_high = sem("k_high" + L)
    q_high, rotated = sem("q_high" + L), sem("rotated" + L)
    ident_cut = sem("ident_cut" + L)
    pads_made = sem("pads_made" + L)
    rows_zeroed, rows_cleared = sem("rows_zeroed" + L), sem("rows_cleared" + L)

    def key(p, r):
        return (p // 2 * 2 if window else 2 * p) + r

    def couple(u):
        g, r = u // 2, u % 2
        return slice(64 * r, 64 * r + 64), (2 * g, 2 * g + 1), (4 * g + r, 4 * g + 2 + r)

    SCORE_UNITS = [(0, [0, 1]), (1, [0, 1]), (2, [0]), (2, [1])]

    def two_blocks(bank, apart, width):
        ap = bank[:, 0:2 * width].rearrange("p (w q) -> p w q", w=2)
        return bass.AP(tensor=ap.tensor, offset=ap.offset, ap=[ap.ap[0], [apart, 2], [1, width]])

    def tiles_of(src):
        return src[:, 0:NT * PADT].rearrange("p (i t) -> p i t", i=NT)[:, :, 0:TT]

    with nc.Block() as block:

        @block.sync
        def _(sp):
            if window:
                wqT, wkT, wvT, rope_cos, rope_sin = weights
                for w, at, n in ((wqT, 0, 256), (wkT, 256, 64), (wvT, 320, 64)):
                    sp.dma_start(w_raw[:, :, at:at + n], w.rearrange("(a p) n -> p a n", p=P)).then_inc(w_loaded, 16)
                sp.dma_start(cos[:], rope_cos).then_inc(w_loaded, 16)
                sp.dma_start(sin[:], rope_sin).then_inc(w_loaded, 16)
            else:
                w_dq, w_dkv, w_uq, w_uk, w_uv = weights
                for w, at in ((w_dq, 0), (w_dkv, 64)):
                    sp.dma_start(d_raw[:, :, at:at + 64], w.rearrange("(a p) n -> p a n", p=P)).then_inc(w_loaded, 16)
                sp.wait_ge(w_zeroed, 1)
                sp.dma_start(w_raw[0:64, 0:256], w_uq).then_inc(w_loaded, 16)
                sp.dma_start(w_raw[64:P, 256:512], w_uk).then_inc(w_loaded, 16)
                sp.dma_start(w_raw[64:P, 512:768], w_uv).then_inc(w_loaded, 16)
                sp.wait_ge(rows_zeroed, 1)
                slots = table.experts * table.capacity
                sp.dma_start(table.x_rows[0:slots, :].rearrange("(t p) d -> p t d", p=TT),
                             table.zeros[:].to_broadcast([TT, slots // TT, 256])).then_inc(rows_cleared, 16)
                sp.wait_ge(rows_cleared, 16)

        @block.gpsimd
        def _(pool):
            pool.memset(ln.minus_half[:], -0.5).then_inc(ln.half_set, 1)
            if not window:
                pool.memset(table.zeros[:], 0.0).then_inc(rows_zeroed, 1)
                pool.memset(table.slots[:], 0)
            pool.memset(mask_s[:], 0.0).then_inc(masks_made, 1)
            pool.memset(mask_t[:], 0.0).then_inc(masks_made, 1)
            pool.wait_ge(masks_made, 2)
            n = 2

            def keep(m, base, cm, step):
                nonlocal n
                pool.wait_ge(masks_made, n)
                pool.affine_select(out=m, in_=m, compare_op=ALU.is_ge, fill=MASKED, base=base,
                                   pattern=[[step, m.shape[1]]], channel_multiplier=cm).then_inc(masks_made, 1)
                n += 1

            for i in range(NT if window else 1):
                keep(mask_s[:, i, :], TT * i, 1, -1)
                if window:
                    keep(mask_s[:, i, :], SPAN - 1 - TT * i, -1, 1)
            keep(mask_t[:], 0, -1, 1)
            if window:
                keep(mask_t[:], SPAN - 1, 1, -1)

            def rotate(n):
                for i in range(NT):
                    pool.wait_ge(drained["D"], ring.drained(n, ring.at[f"QK{i}"], "D"))
                    pool.tensor_tensor(qk_rot[:, i], qk_cos[:, i], qk_sin[:, i], ALU.add).then_inc(rotated, 1)

            def gather(n):
                pool.wait_ge(slots_set, n + 1)
                pool.sem_inc(slots_seen, 1)
                for i in range(NT):
                    pool.indirect_dma_start(ffn_rows[:, i, :], None, table.y_rows,
                                            bass.IndirectOffsetOnAxis(ap=slot[:, i:i + 1], axis=0)).then_inc(gathered, 16)

            def slots(n):
                ln.on_pool(pool, n)
                if window:
                    gather(n + 1)
                    rotate(n)

            if window:
                gather(0)
            slots(0)
            with pool.Fori(0, B - 1) as b:
                slots(b + 1)
            if window:
                pool.wait_ge(gathered, 16 * NT * (B + 1))

        masks_total = 2 + (2 * NT + 2 if window else 2)

        @block.tensor
        def _(pe):
            pe.wait_ge(masks_made, masks_total)
            pe.wait_ge(w_low, 1 if window else 2)
            pe.wait_ge(cleared, 1)
            pe.wait_ge(ident_cut, 1)

            def free(n, unit):
                for e, count in ring.before(n, unit):
                    pe.wait_ge(drained[e], count)
                return work[ring.bank(unit)]

            def three(out, terms, first=True, last=True):
                for k, (s_hi, s_lo, m_hi, m_lo) in enumerate(terms):
                    for j, (s, m) in enumerate(((s_hi, m_hi), (s_lo, m_hi), (s_hi, m_lo))):
                        got = pe.matmul(out, s, m, start=(first and k == 0 and j == 0),
                                        stop=(last and k == len(terms) - 1 and j == 2))
                return got

            def turn_rows(n):
                pe.wait_ge(ln.xn_ready, NT * n + NT)
                for i in range(NT):
                    out = free(n, f"X{i}")
                    for a in range(2):
                        got = pe.transpose(out[:, TT * a:TT * a + TT], xn[:, i, P * a:P * a + P], c.ident[0:TT, 0:TT])
                    got.then_inc(filled, 1)

            def latents(n):
                pe.wait_ge(drained["D"], ring.drained(n, ring.at["X2"], "D"))
                out = free(n, "C")
                three(out[:, 0:SP1], [(d_hi[:, a, :], d_lo[:, a, :], xt_hi[:, a, :], xt_lo[:, a, :])
                                      for a in range(2)]).then_inc(filled, 1)

            def queries_keys(n):
                unit = "X2" if window else "C"
                pe.wait_ge(drained["D"], ring.drained(n, ring.at[unit], "D"))
                for i in range(NT):
                    out = free(n, f"QK{i}")
                    t = slice(TT * i, TT * i + TT)
                    if window:
                        got = three(out[0:TT, 0:320], [(xt_hi[:, a, t], xt_lo[:, a, t], w_hi[:, a, 0:320], w_lo[:, a, 0:320])
                                                       for a in range(2)])
                    else:
                        got = three(out[0:TT, 0:512], [(c_hi[:, t], c_lo[:, t], w_hi[:, 0:512], w_lo[:, 0:512])])
                    got.then_inc(filled, 1)

            def values(n):
                for i in range(NT):
                    out = free(n, f"V{i}")
                    t = slice(TT * i, TT * i + TT)
                    if window:
                        got = three(out[0:TT, 0:64], [(xt_hi[:, a, t], xt_lo[:, a, t], w_hi[:, a, 320:384], w_lo[:, a, 320:384])
                                                      for a in range(2)])
                    else:
                        got = three(out[0:TT, 0:256], [(c_hi[:, t], c_lo[:, t], w_hi[:, 512:768], w_lo[:, 512:768])])
                    got.then_inc(filled, 1)

            def turn(n, unit, pad, at):
                out = free(n, unit)
                for i in range(NT):
                    got = pe.matmul(out[:, PADT * i:PADT * i + PADT],
                                    pad[:, i, at:at + 2, :].rearrange("p h c -> p (h c)").bitcast(F32R),
                                    ident_r[:, :], start=True, stop=True)
                got.then_inc(filled, 1)

            def turn_pair(n, p):
                if p == 0:
                    pe.wait_ge(pads_made, NT * n + NT)
                if p in K_TILES:
                    turn(n, f"TK{p}", kpad, key(p, 0))
                turn(n, f"TQ{p}", qpad, 2 * p)

            def first_scores(n, u):
                _, tiles, _ = couple(u)
                pe.wait_ge(drained["A"], ring.drained(n, ring.at[f"TQ{tiles[1]}"], "A"))
                for k, (i, which) in enumerate(SCORE_UNITS):
                    out = free(n, f"S{u}_{k}")
                    w = len(which)
                    for j, head in enumerate(which):
                        p = tiles[head]
                        at = NK[i] * j
                        pe.matmul(out[0:TT, at:at + NK[i]], q_first[p % 4][:, TT * i:TT * i + TT],
                                  k_t[:, key(p, u % 2), K0[i]:K0[i] + NK[i]], start=(j == 0), stop=False, skip_group_check=True)
                    both = out[0:TT, 0:w * NK[i]].rearrange("p (w k) -> p w k", w=w)
                    if window:
                        cols, mask = both, mask_s[:, i, K0[i]:K0[i] + NK[i]]
                    else:
                        m = TT if i == 1 else PADT
                        cols, mask = both[:, :, TT * i:TT * i + m], mask_s[:, 0, 0:m]
                    pe.matmul(cols, c.ident_bf[:, :], mask.unsqueeze(1).to_broadcast([TT, w, mask.shape[1]]),
                              start=False, stop=True, skip_group_check=True).then_inc(filled, 1)

            def turn_shifted(n, p):
                pe.wait_ge(max_placed, 8 * n + 2 * (p // 2) + 2)
                turn(n, f"R{p}", qpad, 2 * p)

            def scores(b, u):
                _, tiles, _ = couple(u)
                if u == 0:
                    for e in "AD":
                        pe.wait_ge(drained[e], ring.drained(b, len(ring.who) - 1, e))
                for k in range(3):
                    pe.wait_ge(exp_done, 24 * b + 3 * u + k + 1)
                    blocks = [(k, 0, 0), (k, 2, NQ[0])] if k < 2 else [(0, 1, 0), (1, 1, 2 * TT)]
                    for at_block, (w, j, at) in enumerate(blocks):
                        p = tiles[w]
                        pe.matmul(score_t[k][:, at:at + NQ[j]], k_t[:, key(p, u % 2), TT * j:TT * j + TT],
                                  q_shift[:, p, TT * j:TT * j + NQ[j]], start=(at_block == 0), stop=False,
                                  skip_group_check=True)
                    (_, _, at0), (_, _, at1) = blocks
                    if window and k < 2:
                        parts = [(score_t[k][:, at:at + n].unsqueeze(1), n) for at, n in ((at0, NQ[0]), (at1, PADT))]
                    else:
                        n = 2 * TT if window else PADT
                        parts = [(two_blocks(score_t[k], at1, n), n)]
                    for out, n in parts:
                        got = pe.matmul(out, c.ident_bf[:, :], mask_t[:, 0:n].unsqueeze(1).to_broadcast([TT, out.shape[1], n]),
                                        start=False, stop=True, skip_group_check=True)
                    got.then_inc(score_filled, 1)

            def weigh(b, u):
                pe.wait_ge(exp_done, 24 * b + 3 * u + 6)
                if u % 2 == 0:
                    pe.wait_ge(heads_t_taken, 4 * b + u // 2 + 1)
                for w, head in enumerate(couple(u)[2]):
                    rows = slice(32 * (head % 4), 32 * (head % 4) + 32)
                    for j, (k, col) in enumerate(((w, 0), (2, 2 * TT * w), (w, NQ[0]))):
                        n = min(NQ[j], S - TT * j)
                        got = pe.matmul(heads_t[rows, TT * j:TT * j + n], vaug[:, j, head * KV // H, :],
                                        probs[u % 2][:, k, col:col + n], start=(j == 0), stop=(j == 2),
                                        skip_group_check=True, tile_position=(0, 32 * (head % 4)))
                got.then_inc(av_done, 1)

            def turn_back(b, g):
                pe.wait_ge(heads_t_taken, 4 * b + g + 2)
                pe.wait_ge(heads_done, 4 * b + g + 1)
                for i in range(NT):
                    got = pe.transpose(heads[:, i].rearrange("p h c -> p (h c)"), out_t[g % 2][:, TT * i:TT * i + TT],
                                       c.ident[:, :])
                got.then_inc(heads_turned, 1)

            def slots(b, n):
                for s in range(SLOTS):
                    if b is not None:
                        for u in at(SCORES_AT, s):
                            scores(b, u)
                        for u in at(WEIGH_AT, s):
                            weigh(b, u)
                        for g in at(BACK_AT, s):
                            turn_back(b, g)
                    if n is not None:
                        if s == 1:
                            turn_rows(n)
                        if s == 2 and not window:
                            latents(n)
                        if s == 3:
                            queries_keys(n)
                        for u in at(FIRST_AT, s):
                            first_scores(n, u)
                        for p in at(PAIRS_AT, s):
                            turn_pair(n, p)
                        for p in at(SHIFT_AT, s):
                            turn_shifted(n, p)
                if n is not None:
                    values(n)

            credit(pe, av_done, 2)
            slots(None, 0)
            with pe.Fori(0, B - 1) as b:
                slots(b, b + 1)
            slots(B - 1, None)

        @block.scalar
        def _(act):
            if window:
                act.wait_ge(w_loaded, 80)
                act.copy(w_hi[:], w_raw[:]).then_inc(w_high, 1)
            else:
                act.wait_ge(w_loaded, 80)
                act.copy(d_hi[:], d_raw[:]).then_inc(w_high, 1)
                act.copy(w_hi[:], w_raw[:]).then_inc(w_high, 1)
            act.wait_ge(cleared, 1)
            act.wait_ge(c.ready, 1)
            act.copy(ident_r[:], c.ident[0:TT, 0:PADT]).then_inc(ident_cut, 1)
            credit(act, drained["A"], ring.per["A"])
            credit(act, exp_done, 3)
            credit(act, heads_t_taken, 1)

            def bank(n, unit):
                act.wait_ge(filled, ring.filled(n, unit))
                return work[ring.bank(unit)]

            def high_rows(n):
                for i in range(NT):
                    src = bank(n, f"X{i}")
                    act.copy(xt_hi[:, :, TT * i:TT * i + TT], src[:, 0:2 * TT].rearrange("p (a t) -> p a t", a=2))\
                        .then_inc(drained["A"], 1)

            def high_latents(n):
                src = bank(n, "C")
                act.copy(c_hi[:, 0:S], src[:, 0:S]).then_inc(drained["A"], 1)

            def spread(n):
                for i in range(NT):
                    if window:
                        act.wait_ge(rotated, NT * n + i + 1)
                        q = qk_rot[:, i, 0:16, :]
                    else:
                        src = bank(n, f"QK{i}")
                        q = src[0:TT, 0:256].rearrange("p (h d) -> p h d", h=H)
                        k = src[0:TT, 256:512].rearrange("p (h d) -> p h d", h=H)
                    got = act.copy(qpad[:, i, :, 0:32].rearrange("p h (s d) -> p h s d", s=2).bitcast(F32R),
                                   q.unsqueeze(2).to_broadcast([TT, H, 2, D]))
                    if window:
                        got.then_inc(q_high, 1)
                    else:
                        act.copy(kpad[:, i, :, 0:48].rearrange("p h (s d) -> p h s d", s=3)[:, :, 0:3:2, :].bitcast(F32R),
                                 k.unsqueeze(2).to_broadcast([TT, H, 2, D])).then_inc(drained["A"], 1)

            def turn_pair(n, p):
                if p in K_TILES:
                    src = bank(n, f"TK{p}")
                    for r in range(2):
                        rows = slice(64 * r, 64 * r + 64)
                        got = act.copy(k_t[rows, key(p, r), 0:S].rearrange("p (i t) -> p i t", i=NT), tiles_of(src)[rows])
                    got.then_inc(drained["A"], 1)
                src = bank(n, f"TQ{p}")
                act.copy(q_first[p % 4][:, 0:S].rearrange("p (i t) -> p i t", i=NT), tiles_of(src)).then_inc(drained["A"], 1)

            def turn_shifted(n, p):
                src = bank(n, f"R{p}")
                act.copy(q_shift[:, p, 0:S].rearrange("p (i t) -> p i t", i=NT), tiles_of(src)).then_inc(drained["A"], 1)

            def values(n):
                for i in range(NT):
                    src = bank(n, f"V{i}")
                    act.copy(vaug[:, i, :, 0:D], src[0:TT, 0:KV * D].rearrange("p (g d) -> p g d", d=D))\
                        .then_inc(drained["A"], 1)

            def exps(b, p):
                act.wait_ge(av_done, 8 * b + p + 1)
                for k in range(3):
                    act.wait_ge(score_filled, 24 * b + 3 * p + k + 1)
                    n = NQ[0] + NQ[2] if k < 2 else 2 * NQ[1]
                    act.activation(probs[p % 2][:, k, 0:n], score_t[k][:, 0:n], ACT.Exp, scale=SCALE)\
                        .then_inc(exp_done, 1)

            def take_heads(b, g):
                act.wait_ge(av_done, 8 * b + 2 * g + 4)
                act.copy(out_t[g % 2][:], heads_t[:, 0:S]).then_inc(heads_t_taken, 1)

            def slots(b, n):
                for s in range(SLOTS):
                    if b is not None:
                        for u in at(SCORES_AT, s):
                            exps(b, u)
                        for u in at(WEIGH_AT, s):
                            if u % 2:
                                take_heads(b, u // 2)
                    if n is not None:
                        if s == 1:
                            high_rows(n)
                        if s == 2 and not window:
                            high_latents(n)
                        if s == 3:
                            spread(n)
                        for p in at(PAIRS_AT, s):
                            turn_pair(n, p)
                        for p in at(SHIFT_AT, s):
                            turn_shifted(n, p)
                if n is not None:
                    values(n)

            slots(None, 0)
            with act.Fori(0, B - 1) as b:
                slots(b, b + 1)
            slots(B - 1, None)

        @block.vector
        def _(dve):
            if not window:
                dve.memset(w_raw[:], 0.0).then_inc(w_zeroed, 1)
            for z in (qpad, kpad):
                dve.memset(z[:], 0.0).then_inc(pads_zeroed, 1)
            for z in (xt_hi, xt_lo, *q_first, q_shift, k_t, *(() if window else (c_hi, c_lo))):
                dve.memset(z[:].bitcast(F32), 0.0)
            dve.memset(vaug[:, :, :, D + 1:32], 0.0)
            dve.memset(vaug[:, :, :, D:D + 1], 1.0)
            dve.wait_ge(pads_zeroed, 2)
            dve.memset(kpad[:, :, :, 48:50], 1.0).then_inc(cleared, 1)
            if not window:
                dve.wait_ge(w_high, 1)
                dve.tensor_tensor(d_lo[:], d_raw[:], d_hi[:].bitcast(F32), ALU.subtract).then_inc(w_low, 1)
            dve.wait_ge(w_high, 1 if window else 2)
            dve.tensor_tensor(w_lo[:], w_raw[:], w_hi[:].bitcast(F32), ALU.subtract).then_inc(w_low, 1)
            dve.wait_ge(ln.half_set, 1)
            credit(dve, drained["D"], ring.per["D"])
            credit(dve, heads_done, 1)

            def bank(n, unit):
                dve.wait_ge(filled, ring.filled(n, unit))
                return work[ring.bank(unit)]

            def point(n):
                dve.tensor_copy(slot[:], table.slots[:, 0, bass.ds(NT * n, NT)]).then_inc(slots_set, 1)

            def normalize(n):
                if window:
                    dve.wait_ge(gathered, 16 * NT * (n + 1))
                    rows = h[:, bass.ds(NT * n, NT), :]
                    dve.tensor_tensor(rows, rows, ffn_rows[:], ALU.add).then_inc(rows_added, 1)
                    dve.wait_ge(rows_added, n + 1)
                    point(n + 1)
                ln.on_vector_stats(dve, c.ready, n)
                ln.on_vector_apply(dve, n)

            def low_rows(n):
                for i in range(NT):
                    src = bank(n, f"X{i}")
                    dve.wait_ge(drained["A"], ring.drained(n, ring.at[f"X{i}"], "A"))
                    t = slice(TT * i, TT * i + TT)
                    dve.tensor_tensor(xt_lo[:, :, t], src[:, 0:2 * TT].rearrange("p (a t) -> p a t", a=2),
                                      xt_hi[:, :, t].bitcast(F32), ALU.subtract).then_inc(drained["D"], 1)

            def low_latents(n):
                src = bank(n, "C")
                dve.wait_ge(drained["A"], ring.drained(n, ring.at["C"], "A"))
                dve.tensor_tensor(c_lo[:, 0:S], src[:, 0:S], c_hi[:, 0:S].bitcast(F32), ALU.subtract)\
                    .then_inc(drained["D"], 1)

            def rotate(n):
                for i in range(NT):
                    src = bank(n, f"QK{i}")
                    both = src[0:TT, 0:320].rearrange("p (h d) -> p h d", d=D)
                    dve.tensor_tensor(qk_cos[:, i], both, cos[:, i:i + 1, :].to_broadcast([TT, 20, D]), ALU.mult)
                    dve.tensor_tensor(qk_sin[:, i, :, 0:8], both[:, :, 8:16],
                                      sin[:, i:i + 1, 0:8].to_broadcast([TT, 20, 8]), ALU.mult)
                    dve.tensor_tensor(qk_sin[:, i, :, 8:16], both[:, :, 0:8],
                                      sin[:, i:i + 1, 8:16].to_broadcast([TT, 20, 8]), ALU.mult)\
                        .then_inc(drained["D"], 1)

            def spread(n):
                for i in range(NT):
                    if window:
                        dve.wait_ge(rotated, NT * n + i + 1)
                        q, k = qk_rot[:, i, 0:16, :], qk_rot[:, i, 16:20, :].unsqueeze(2).to_broadcast([TT, KV, 2, D])
                    else:
                        src = bank(n, f"QK{i}")
                        q = src[0:TT, 0:256].rearrange("p (h d) -> p h d", h=H)
                        k = src[0:TT, 256:512].rearrange("p (g r d) -> p g r d", g=H // 2, r=2)
                    place = [kpad[:, i, :, slot * D:slot * D + D].rearrange("p (g r) d -> p g r d", r=2) for slot in range(3)]
                    if window:
                        for slot in (0, 2):
                            got = dve.tensor_copy(place[slot].bitcast(F32R), k)
                        got.then_inc(k_high, 1)
                        dve.wait_ge(k_high, NT * n + i + 1)
                    else:
                        dve.wait_ge(drained["A"], ring.drained(n, ring.at[f"QK{i}"], "A"))
                    dve.tensor_tensor(place[1].bitcast(F32R), k, place[0], ALU.subtract)
                    if window:
                        dve.wait_ge(q_high, NT * n + i + 1)
                    got = dve.tensor_tensor(qpad[:, i, :, 32:48].bitcast(F32R), q, qpad[:, i, :, 0:16], ALU.subtract)
                    if not window:
                        got.then_inc(drained["D"], 1)
                    dve.memset(qpad[:, i, :, 48:50], 0.0).then_inc(pads_made, 1)

            def maxima(n, u):
                m = neg_max[u % 2]
                for k, (i, which) in enumerate(SCORE_UNITS):
                    src = bank(n, f"S{u}_{k}")
                    w = len(which)
                    dve.tensor_reduce(m[:, i, which[0]:which[0] + w],
                                      src[0:TT, 0:w * NK[i]].rearrange("p (h k) -> p h k", h=w),
                                      AX.X, ALU.max, negate=True).then_inc(drained["D"], 1)
                dve.wait_ge(drained["D"], ring.drained(n, ring.at[f"S{u}_3"], "D"))
                a, z = couple(u)[2]
                dve.tensor_copy(qpad[:, :, a:z + 1:2, 48].bitcast(F32R), m[:]).then_inc(max_high, 1)
                dve.wait_ge(max_high, 8 * n + u + 1)
                dve.tensor_tensor(qpad[:, :, a:z + 1:2, 49].bitcast(F32R), m[:], qpad[:, :, a:z + 1:2, 48], ALU.subtract)\
                    .then_inc(max_placed, 1)

            def divide(b, g):
                dve.wait_ge(heads_turned, 4 * b + g + 1)
                dve.reciprocal(rsum[g % 2][:], heads[:, :, :, D]).then_inc(sums_inverted, 1)
                dve.wait_ge(sums_inverted, 4 * b + g + 1)
                dve.tensor_tensor(ao[:, bass.ds(NT * b, NT), 64 * g:64 * g + 64].rearrange("p t (h d) -> p t h d", h=4),
                                  heads[:, :, :, 0:D], rsum[g % 2][:].unsqueeze(3).to_broadcast([TT, NT, 4, D]), ALU.mult)\
                    .then_inc(heads_done, 1)

            def slots(b, n):
                for s in range(SLOTS):
                    if n is not None and s == 0:
                        normalize(n)
                    if b is not None:
                        for g in at(BACK_AT, s):
                            divide(b, g)
                    if n is not None:
                        if s == 1:
                            low_rows(n)
                        if s == 2 and not window:
                            low_latents(n)
                        if s == 3:
                            if window:
                                rotate(n)
                            spread(n)
                        for u in at(FIRST_AT, s):
                            maxima(n, u)

            if window:
                point(0)
            slots(None, 0)
            with dve.Fori(0, B - 1) as b:
                slots(b, b + 1)
            slots(B - 1, None)


def dispatch(nc, sb, ps, sem, layer, c, h, ao, B, w_out, w_gate, b_gate, table):
    L = f"_d{layer}"
    top2 = layer == 1
    E = table.experts
    G = 2
    T, B = NT * G, B // G
    out_ring = Ring(3, [(f"A{i}", "AD") for i in range(T)] + [(f"Y{k}", "D") for k in range(T // 2)])
    gate_ring = Ring(4, [(f"X{i}", "AD") for i in range(T)] + [("G", "D"), ("POS", "D")]
                     + [(f"unused{i}", "") for i in range(-(T + 2) % 4)])
    products = [(f"Y{k}", (2 * k, 2 * k + 1)) for k in range(T // 2)]

    xn = sb("xn" + L, [TT, T, 256], F32)
    xs = sb("xs" + L, [TT, T, 256], F32)
    xt_hi, xt_lo = sb("xt_hi" + L, [P, 2, T * TT], F32R), sb("xt_lo" + L, [P, 2, T * TT], F32R)
    g_raw, g_cut = sb("g_raw" + L, [P, 2, E], F32), sb("g_cut" + L, [P, 2, 2, E], F32R)
    g_hi, g_lo = g_cut[:, :, 0, :], g_cut[:, :, 1, :]
    if not top2:
        ao_now = sb("ao_now" + L, [TT, T, 256], F32)
        at_hi, at_lo = sb("at_hi" + L, [P, 2, T * TT], F32R), sb("at_lo" + L, [P, 2, T * TT], F32R)
        o_raw, o_hi, o_lo = (sb(n + L, [P, 2, 256], d) for n, d in (("o_raw", F32), ("o_hi", F32R), ("o_lo", F32R)))
    bias = sb("bias" + L, [TT, E], F32)
    upto = sb("upto" + L, [TT, TT], F32)
    ones = sb("ones" + L, [TT, TT], F32)
    order = sb("order" + L, [TT, T, E], F32)
    token = sb("token" + L, [TT, T], F32)
    logits, masked, equal, ranks, picked = (sb(n + L, [TT, T, E], F32) for n in ("logits", "masked", "equal", "ranks", "picked"))
    hot = [sb(f"hot{k}" + L, [TT, T, E], F32) for k in range(2)]
    both = sb("both" + L, [TT, T, E], F32)
    best = [sb(f"best{k}" + L, [TT, T], F32) for k in range(2)]
    first = [sb(f"first{k}" + L, [TT, T], F32) for k in range(2)]
    place = [sb(f"place{k}" + L, [TT, T], F32) for k in range(2)]
    kept, shift, expo = sb("kept" + L, [TT, T], F32), sb("shift" + L, [TT, T, E], F32), sb("expo" + L, [TT, T, E], F32)
    prob, inverse, factor = (sb(n + L, [TT, T], F32) for n in ("prob", "inverse", "factor"))
    before = sb("before" + L, [TT, T + 1, E], F32)
    slot = [sb(f"slot{k}" + L, [TT, T], I32) for k in range(2)]
    ln = LayerNorm(sb, sem, L, h, xn, T)
    for ring, name in ((out_ring, "out"), (gate_ring, "gate")):
        ring.tiles = [ps(f"{name}_bank{i}" + L, [P, 512], F32) for i in range(ring.banks)]
        ring.filled_sem = sem(f"{name}_filled" + L)
        ring.drained_sem = {"A": sem(f"{name}_act_drained" + L), "D": sem(f"{name}_dve_drained" + L)}

    def ring_of(unit):
        return out_ring if unit in out_ring.at and not unit.startswith("unused") else gate_ring

    count_ps = ps("count_ps" + L, [TT, 16], F32)

    loaded, w_high, w_low, made, cleared = (sem(n + L) for n in ("loaded", "w_high", "w_low", "made", "cleared"))
    ao_ready, step = sem("ao_ready" + L), sem("step" + L)
    logits_ready, exp_done, hot_ready = sem("logits_ready" + L), sem("exp_done" + L), sem("hot_ready" + L)
    slots_ready, scattered, copied = sem("slots_ready" + L), sem("scattered" + L), sem("copied" + L)
    total_ready, tails_ready = sem("total_ready" + L), sem("tails_ready" + L)
    rows_left = sem("rows_left" + L)
    factor_ready, xs_ready = sem("factor_ready" + L), sem("xs_ready" + L)
    slots_seen = sem("slots_seen" + L)
    plan_step = sem("plan_step" + L)
    K = 2 if top2 else 1
    MADE = 8 if top2 else 5
    if top2:
        ks = sb("ks" + L, [TT, E, B * G], F32)
        js = sb("js" + L, [TT, E, table.blocks], F32)
    with nc.Block() as block:

        @block.sync
        def _(sp):
            sp.dma_start(g_raw[:], w_gate.rearrange("(a p) n -> p a n", p=P)).then_inc(loaded, 16)
            sp.dma_start(bias[:], b_gate.partition_broadcast(TT)).then_inc(loaded, 16)
            if not top2:
                sp.dma_start(o_raw[:], w_out.rearrange("(a p) n -> p a n", p=P)).then_inc(loaded, 16)

                def load_heads(n):
                    sp.dma_start(ao_now[:], ao[:, bass.ds(T * n, T), :]).then_inc(ao_ready, 16)

                def keep_dropped(n):
                    sp.wait_ge(xs_ready, n + 1)
                    sp.dma_start(table.y_rows[bass.ds(table.own + G * S * n, G * S), :].rearrange("(t p) d -> p t d", p=TT),
                                 xs[:]).then_inc(copied, 16)

                load_heads(0)
                with sp.Fori(0, B - 1) as b:
                    sp.wait_ge(out_ring.drained_sem["D"], out_ring.drained(b, out_ring.at[f"A{T - 1}"], "D"))
                    load_heads(b + 1)
                    keep_dropped(b)
                keep_dropped(B - 1)
                sp.wait_ge(copied, 16 * (B + 1))
            else:
                sp.wait_ge(tails_ready, 1)
                sp.wait_ge(scattered, 16 * T * K * B)
                for e in range(E):
                    at = sp.value_load(table.tails[0:1, e:e + 1], min_val=e * table.region,
                                       max_val=e * table.region + S * B * G)
                    sp.dma_start(table.x_rows[bass.ds(at, S), :].rearrange("(t p) d -> p t d", p=TT),
                                 table.zeros[:].to_broadcast([TT, NT, 256])).then_inc(copied, 16)
                sp.dma_start(table.x_rows[E * table.region:E * table.region + S, :].rearrange("(t p) d -> p t d", p=TT),
                             table.zeros[:].to_broadcast([TT, NT, 256])).then_inc(copied, 16)
                sp.wait_ge(copied, 16 * (E + 1))

        @block.gpsimd
        def _(pool):
            pool.memset(ln.minus_half[:], -0.5).then_inc(ln.half_set, 1)
            pool.memset(upto[:], 1.0).then_inc(made, 1)
            pool.memset(ones[:], 1.0).then_inc(made, 1)
            pool.iota(order[:], [[0, T], [-1, E]], base=E, channel_multiplier=0,
                      allow_small_or_imprecise_dtypes=True).then_inc(made, 1)
            pool.iota(token[:], [[TT, T]], base=table.own, channel_multiplier=1,
                      allow_small_or_imprecise_dtypes=True).then_inc(made, 1)
            pool.wait_ge(made, 4)
            pool.affine_select(out=upto[:], in_=upto[:], compare_op=ALU.is_ge, fill=0.0, base=0,
                               pattern=[[1, TT]], channel_multiplier=-1).then_inc(made, 1)
            if top2:
                pool.iota(ks[:], [[0, E], [S, B * G]], base=0, channel_multiplier=0,
                          allow_small_or_imprecise_dtypes=True).then_inc(made, 1)
                pool.iota(js[:], [[0, E], [1, table.blocks]], base=0, channel_multiplier=0,
                          allow_small_or_imprecise_dtypes=True).then_inc(made, 1)
                pool.memset(table.zeros[:], 0.0).then_inc(made, 1)

            def send(n):
                pool.wait_ge(xs_ready, n + 1)
                pool.wait_ge(slots_ready, n + 1)
                pool.sem_inc(slots_seen, 1)
                for i in range(T):
                    for k in range(K):
                        pool.indirect_dma_start(table.x_rows, bass.IndirectOffsetOnAxis(ap=slot[k][:, i:i + 1], axis=0),
                                                xs[:, i, :], None).then_inc(scattered, 16)
                pool.wait_ge(scattered, 16 * T * K * (n + 1))
                pool.sem_inc(rows_left, 1)

            ln.on_pool(pool, 0)
            with pool.Fori(0, B - 1) as b:
                ln.on_pool(pool, b + 1)
                send(b)
            send(B - 1)

        @block.tensor
        def _(pe):
            pe.wait_ge(w_low, 1 if top2 else 2)
            pe.wait_ge(made, MADE)
            pe.wait_ge(cleared, 1)

            def free(n, unit):
                ring = ring_of(unit)
                for e, count in ring.before(n, unit):
                    pe.wait_ge(ring.drained_sem[e], count)
                return ring.tiles[ring.bank(unit)]

            def three(out, terms):
                for k, (s_hi, s_lo, m_hi, m_lo) in enumerate(terms):
                    for j, (s, m) in enumerate(((s_hi, m_hi), (s_lo, m_hi), (s_hi, m_lo))):
                        got = pe.matmul(out, s, m, start=(k == 0 and j == 0), stop=(k == len(terms) - 1 and j == 2))
                return got

            def turn(n, name, src):
                for i in range(T):
                    out = free(n, f"{name}{i}")
                    for a in range(2):
                        got = pe.transpose(out[:, TT * a:TT * a + TT], src[:, i, P * a:P * a + P], c.ident[0:TT, 0:TT])
                    got.then_inc(ring_of(f"{name}0").filled_sem, 1)

            def turn_heads(n):
                pe.wait_ge(ao_ready, 16 * (n + 1))
                turn(n, "A", ao_now)

            def out_product(n, which):
                pe.wait_ge(out_ring.drained_sem["D"], out_ring.drained(n, out_ring.at[f"A{T - 1}"], "D"))
                for unit, tiles in products[which]:
                    out = free(n, unit)
                    for k, i in enumerate(tiles):
                        t = slice(TT * i, TT * i + TT)
                        got = three(out[0:TT, 256 * k:256 * k + 256],
                                    [(at_hi[:, a, t], at_lo[:, a, t], o_hi[:, a, :], o_lo[:, a, :]) for a in range(2)])
                    got.then_inc(out_ring.filled_sem, 1)

            def turn_rows(n):
                pe.wait_ge(ln.xn_ready, T * n + T)
                turn(n, "X", xn)

            def gate(n):
                pe.wait_ge(gate_ring.drained_sem["D"], gate_ring.drained(n, gate_ring.at[f"X{T - 1}"], "D"))
                out = free(n, "G")
                for i in range(T):
                    t = slice(TT * i, TT * i + TT)
                    for a in range(2):
                        pe.matmul(out[0:TT, 2 * E * i:2 * E * i + 2 * E], xt_hi[:, a, t], flat(g_cut[:, a]),
                                  start=(i == 0 and a == 0), stop=False, skip_group_check=True)
                        got = pe.matmul(out[0:TT, 2 * E * i:2 * E * i + E], xt_lo[:, a, t], g_cut[:, a, 0, :],
                                        start=False, stop=(a == 1), skip_group_check=True)
                got.then_inc(gate_ring.filled_sem, 1)

            def rank(n):
                pe.wait_ge(hot_ready, n + 1)
                out = free(n, "POS")
                pe.matmul(out[0:TT, 0:T * E], upto[:, :], (both if top2 else hot[0])[:].rearrange("p t e -> p (t e)"),
                          start=True, stop=False)
                pe.matmul(out[0:TT, 0:T * E], ones[:, :], before[:, 0:T, :].rearrange("p t e -> p (t e)"),
                          start=False, stop=True).then_inc(gate_ring.filled_sem, 1)

            if not top2:
                turn_heads(0)
                out_product(0, slice(0, T // 2))
            with pe.Fori(0, B - 1) as b:
                turn_rows(b)
                if not top2:
                    turn_heads(b + 1)
                gate(b)
                if not top2:
                    out_product(b + 1, slice(0, 1))
                rank(b)
                if not top2:
                    out_product(b + 1, slice(1, T // 2))
            turn_rows(B - 1)
            gate(B - 1)
            rank(B - 1)
            if top2:
                pe.wait_ge(total_ready, 1)
                pe.matmul(count_ps[:, 0:E], ones[:, :], before[:, T, :], start=True, stop=True).then_inc(total_ready, 1)

        @block.scalar
        def _(act):
            act.wait_ge(loaded, 32 if top2 else 48)
            act.copy(g_hi, g_raw[:]).then_inc(w_high, 1)
            if not top2:
                act.copy(o_hi[:], o_raw[:]).then_inc(w_high, 1)
            act.wait_ge(cleared, 1)
            for ring in (out_ring, gate_ring):
                credit(act, ring.drained_sem["A"], ring.per["A"])

            def high(n, name, to):
                ring = ring_of(f"{name}0")
                for i in range(T):
                    act.wait_ge(ring.filled_sem, ring.filled(n, f"{name}{i}"))
                    src = ring.tiles[ring.bank(f"{name}{i}")]
                    act.copy(to[:, :, TT * i:TT * i + TT], src[:, 0:2 * TT].rearrange("p (a t) -> p a t", a=2))\
                        .then_inc(ring.drained_sem["A"], 1)

            def power(n):
                act.wait_ge(logits_ready, n + 1)
                act.activation(expo[:], shift[:], ACT.Exp).then_inc(exp_done, 1)

            def scale(n):
                act.wait_ge(rows_left, n + 1)
                if top2:
                    act.wait_ge(ln.xn_ready, T * (n + 1))
                    act.copy(xs[:], xn[:]).then_inc(xs_ready, 1)
                    return
                act.wait_ge(copied, 16 * (n + 1))
                act.wait_ge(factor_ready, n + 1)
                for i in range(T):
                    ins = act.activation(xs[:, i, :], xn[:, i, :], ACT.Copy, scale=factor[:, i:i + 1])
                ins.then_inc(xs_ready, 1)

            if not top2:
                high(0, "A", at_hi)
            with act.Fori(0, B - 1) as b:
                high(b, "X", xt_hi)
                if not top2:
                    high(b + 1, "A", at_hi)
                power(b)
                scale(b)
            high(B - 1, "X", xt_hi)
            power(B - 1)
            scale(B - 1)

        @block.vector
        def _(dve):
            for z in (xt_hi, xt_lo, *(() if top2 else (at_hi, at_lo))):
                dve.memset(z[:].bitcast(F32), 0.0)
            dve.memset(before[:], 0.0).then_inc(cleared, 1)
            dve.wait_ge(w_high, 1)
            dve.tensor_tensor(g_lo, g_raw[:], g_hi.bitcast(F32), ALU.subtract).then_inc(w_low, 1)
            if not top2:
                dve.wait_ge(w_high, 2)
                dve.tensor_tensor(o_lo[:], o_raw[:], o_hi[:].bitcast(F32), ALU.subtract).then_inc(w_low, 1)
            dve.wait_ge(ln.half_set, 1)
            dve.wait_ge(made, MADE)
            for ring in (out_ring, gate_ring):
                credit(dve, ring.drained_sem["D"], ring.per["D"])
            credit(dve, rows_left, 1)
            if not top2:
                credit(dve, copied, 16)
            STEPS = 30 if top2 else 25
            taken = [0]

            def then(n, ins):
                taken[0] += 1
                ins.then_inc(step, 1)
                dve.wait_ge(step, STEPS * n + taken[0])

            def bank(n, unit):
                ring = ring_of(unit)
                dve.wait_ge(ring.filled_sem, ring.filled(n, unit))
                return ring.tiles[ring.bank(unit)]

            def taken_by_vector(n, unit):
                ring = ring_of(unit)
                dve.wait_ge(ring.drained_sem["D"], ring.drained(n, ring.at[unit], "D"))

            def low(n, name, hi, lo):
                for i in range(T):
                    src = bank(n, f"{name}{i}")
                    ring = ring_of(f"{name}{i}")
                    dve.wait_ge(ring.drained_sem["A"], ring.drained(n, ring.at[f"{name}{i}"], "A"))
                    t = slice(TT * i, TT * i + TT)
                    dve.tensor_tensor(lo[:, :, t], src[:, 0:2 * TT].rearrange("p (a t) -> p a t", a=2),
                                      hi[:, :, t].bitcast(F32), ALU.subtract).then_inc(ring.drained_sem["D"], 1)

            def add_product(n):
                for unit, tiles in products:
                    src = bank(n, unit)
                    rows = h[:, bass.ds(T * n + tiles[0], len(tiles)), :]
                    dve.tensor_tensor(rows, rows, src[0:TT, 0:256 * len(tiles)].rearrange("p (t d) -> p t d", d=256),
                                      ALU.add).then_inc(out_ring.drained_sem["D"], 1)

            def choose(n, lg, k):
                wide = lambda t: t[:].unsqueeze(2).to_broadcast([TT, T, E])
                then(n, dve.tensor_reduce(best[k][:], lg[:], AX.X, ALU.max))
                then(n, dve.tensor_tensor(equal[:], lg[:], wide(best[k]), ALU.is_equal))
                then(n, dve.tensor_tensor(equal[:], equal[:], order[:], ALU.mult))
                then(n, dve.tensor_reduce(first[k][:], equal[:], AX.X, ALU.max))
                then(n, dve.tensor_tensor(hot[k][:], order[:], wide(first[k]), ALU.is_equal))

            def route(n):
                src = bank(n, "G")
                parts = src[0:TT, 0:2 * T * E].rearrange("p (t k e) -> p t k e", k=2, e=E)
                then(n, dve.tensor_tensor(logits[:], parts[:, :, 0, :], bias[:].unsqueeze(1).to_broadcast([TT, T, E]), ALU.add))
                dve.tensor_tensor(logits[:], parts[:, :, 1, :], logits[:], ALU.add).then_inc(gate_ring.drained_sem["D"], 1)
                taken_by_vector(n, "G")
                choose(n, logits, 0)
                if top2:
                    then(n, dve.scalar_tensor_tensor(masked[:], hot[0][:], -3.0e38, logits[:], ALU.mult, ALU.add))
                    choose(n, masked, 1)
                    then(n, dve.tensor_tensor(both[:], hot[0][:], hot[1][:], ALU.add))
                    now = both
                    dve.tensor_tensor(shift[:, :, 0], best[1][:], best[0][:], ALU.subtract)
                    dve.memset(shift[:, :, 1:E], 0.0).then_inc(logits_ready, 1)
                else:
                    now = hot[0]
                    dve.tensor_tensor(shift[:], logits[:], best[0][:].unsqueeze(2).to_broadcast([TT, T, E]),
                                      ALU.subtract).then_inc(logits_ready, 1)
                for i in range(T):
                    ins = dve.tensor_tensor(before[:, i + 1, :], before[:, i, :], now[:, i, :], ALU.add)
                    if i < T - 1:
                        then(n, ins)
                ins.then_inc(hot_ready, 1)

            def send(n):
                dve.wait_ge(exp_done, n + 1)
                if top2:
                    then(n, dve.tensor_scalar(prob[:], expo[:, :, 0], 1.0, None, ALU.add))
                    then(n, dve.reciprocal(inverse[:], prob[:]))
                    dve.tensor_copy(table.weight[:, 0, bass.ds(T * n, T)], inverse[:])
                    dve.tensor_tensor(table.weight[:, 1, bass.ds(T * n, T)], inverse[:], expo[:, :, 0], ALU.mult)
                else:
                    then(n, dve.tensor_reduce(inverse[:], expo[:], AX.X, ALU.add))
                    then(n, dve.reciprocal(prob[:], inverse[:]))
                    then(n, dve.reciprocal(inverse[:], prob[:]))
                    dve.tensor_tensor(factor[:], prob[:], inverse[:], ALU.mult).then_inc(factor_ready, 1)
                src = bank(n, "POS")
                dve.tensor_copy(ranks[:], src[0:TT, 0:T * E].rearrange("p (t e) -> p t e", e=E))\
                    .then_inc(gate_ring.drained_sem["D"], 1)
                taken_by_vector(n, "POS")
                then(n, dve.tensor_copy(before[:, 0, :], before[:, T, :]))
                dve.wait_ge(rows_left, n + 1)
                for k in range(K):
                    then(n, dve.tensor_tensor(picked[:], hot[k][:], ranks[:], ALU.mult))
                    then(n, dve.tensor_reduce(place[k][:], picked[:], AX.X, ALU.add))
                    if not top2:
                        then(n, dve.tensor_scalar(kept[:], place[k][:], float(table.capacity), None, ALU.is_le))
                    then(n, dve.tensor_scalar(first[k][:], first[k][:], -float(table.region),
                                              float(E * table.region - 1), ALU.mult, ALU.add))
                    then(n, dve.tensor_tensor(place[k][:], place[k][:], first[k][:], ALU.add))
                    if not top2:
                        then(n, dve.tensor_tensor(place[k][:], place[k][:], token[:], ALU.subtract))
                        then(n, dve.tensor_tensor(place[k][:], place[k][:], kept[:], ALU.mult))
                        then(n, dve.tensor_tensor(place[k][:], place[k][:], token[:], ALU.add))
                        then(n, dve.tensor_scalar(token[:], token[:], float(G * S), None, ALU.add))
                    dve.tensor_copy((table.place if top2 else table.slots)[:, k, bass.ds(T * n, T)], place[k][:])
                    ins = dve.tensor_copy(slot[k][:], place[k][:])
                ins.then_inc(slots_ready, 1)
                assert taken[0] <= STEPS, taken
                while taken[0] < STEPS:
                    then(n, dve.memset(kept[:], 0.0))
                taken[0] = 0

            def normalize(n):
                if not (isinstance(n, int) and n == 0):
                    dve.wait_ge(xs_ready, n)
                ln.on_vector_apply(dve, n)

            if not top2:
                low(0, "A", at_hi, at_lo)
                add_product(0)
            ln.on_vector_stats(dve, c.ready, 0)
            normalize(0)
            with dve.Fori(0, B - 1) as b:
                low(b, "X", xt_hi, xt_lo)
                if not top2:
                    low(b + 1, "A", at_hi, at_lo)
                else:
                    ln.on_vector_stats(dve, c.ready, b + 1)
                route(b)
                send(b)
                if not top2:
                    add_product(b + 1)
                    ln.on_vector_stats(dve, c.ready, b + 1)
                normalize(b + 1)
            low(B - 1, "X", xt_hi, xt_lo)
            route(B - 1)
            send(B - 1)
            if top2:
                table.plan(dve, before, total_ready, count_ps, ks, js, plan_step, tails_ready)


class Table:

    def __init__(self, nc, sb, name, experts, region, capacity, own, rows, K, tiles, blocks=0):
        self.experts, self.region, self.capacity, self.own, self.blocks = experts, region, capacity, own, blocks
        self.x_rows = nc.dram_tensor(f"{name}_x_rows", [rows, 256], F32, kind="Internal").ap()
        self.y_rows = nc.dram_tensor(f"{name}_y_rows", [blocks * S if blocks else rows, 256], F32, kind="Internal").ap()
        self.slots = sb(f"{name}_slots", [TT, K, tiles + (NT if K == 1 else 0)], I32)
        self.zeros = sb(f"{name}_zeros", [TT, 1, 256], F32)
        if K == 2:
            self.place = sb(f"{name}_place", [TT, K, tiles], F32)
            self.x_place = sb(f"{name}_x_place", [TT, K, tiles], F32)
            self.beyond = sb(f"{name}_beyond", [TT, K, tiles], F32)
            self.weight = sb(f"{name}_weight", [TT, K, tiles], F32)
            E = experts
            self.count, self.n_blocks, self.upto, self.gap = (
                sb(f"{name}_{n}", [TT, E], F32) for n in ("count", "n_blocks", "upto", "gap"))
            self.over = sb(f"{name}_over", [TT, E, tiles // NT], F32)
            self.past, self.skip = (sb(f"{name}_{n}", [TT, E, blocks], F32) for n in ("past", "skip"))
            self.row_f, self.expert_f = (sb(f"{name}_{n}", [TT, blocks], F32) for n in ("row_f", "expert_f"))
            self.row, self.expert = (sb(f"{name}_{n}", [TT, blocks], I32) for n in ("row", "expert"))
            self.tails = sb(f"{name}_tails", [TT, E], I32)
            self.at = sb(f"{name}_at", [TT, E], F32)

    def plan(self, dve, before, total_ready, count_ps, ks, js, step, tails_ready):
        E, NB = self.experts, self.blocks
        done = [0]

        def then(ins):
            done[0] += 1
            ins.then_inc(step, 1)
            dve.wait_ge(step, done[0])

        dve.sem_inc(total_ready, 1)
        dve.wait_ge(total_ready, 2)
        then(dve.tensor_copy(self.count[:], count_ps[:, 0:E]))
        then(dve.tensor_tensor(self.over[:], self.count[:].unsqueeze(2).to_broadcast(list(self.over.shape)), ks[:], ALU.is_gt))
        then(dve.tensor_reduce(self.n_blocks[:], self.over[:], AX.X, ALU.add))
        then(dve.tensor_scalar(self.gap[:], self.n_blocks[:], -float(S), float(self.region), ALU.mult, ALU.add))
        then(dve.tensor_copy(self.upto[:], self.n_blocks[:]))
        for e in range(1, E):
            then(dve.tensor_tensor(self.upto[:, e:e + 1], self.upto[:, e - 1:e], self.upto[:, e:e + 1], ALU.add))
        wide = lambda t: t[:].unsqueeze(2).to_broadcast([TT, E, NB])
        then(dve.tensor_tensor(self.past[:], js[:], wide(self.upto), ALU.is_ge))
        then(dve.tensor_tensor(self.skip[:], self.past[:], wide(self.gap), ALU.mult))
        then(dve.tensor_reduce(self.expert_f[:], self.past[:].rearrange("p e j -> p j e"), AX.X, ALU.add))
        then(dve.tensor_scalar(self.expert_f[:], self.expert_f[:], float(E - 1), None, ALU.min))
        then(dve.tensor_reduce(self.row_f[:], self.skip[:].rearrange("p e j -> p j e"), AX.X, ALU.add))
        then(dve.scalar_tensor_tensor(self.row_f[:], js[:, 0, :], float(S), self.row_f[:], ALU.mult, ALU.add))
        then(dve.tensor_scalar(self.row_f[:], self.row_f[:], float(E * self.region), None, ALU.min))
        for e in range(E):
            then(dve.tensor_scalar(self.at[:, e:e + 1], self.count[:, e:e + 1], float(e * self.region), None, ALU.add))
        then(dve.tensor_copy(self.x_place[:], self.place[:]))
        for e in range(E - 1):
            then(dve.tensor_scalar(self.beyond[:], self.x_place[:], float((e + 1) * self.region), self.gap[:, e:e + 1],
                                   ALU.is_ge, ALU.mult))
            then(dve.tensor_tensor(self.place[:], self.place[:], self.beyond[:], ALU.subtract))
        dve.tensor_copy(self.slots[:], self.place[:])
        dve.tensor_copy(self.row[:], self.row_f[:])
        dve.tensor_copy(self.expert[:], self.expert_f[:])
        dve.tensor_copy(self.tails[:], self.at[:]).then_inc(tails_ready, 1)


SPREAD = 96
BOTH = 32


def move(eng, to, source, done):
    for part in (slice(0, SPREAD), slice(SPREAD, TT)):
        eng.dma_start(to[part], source[part]).then_inc(done, BOTH // 2)


def feed_forward(nc, sb, ps, sem, tag, c, N, HC, loads, func, factor, packed, b2, source, store, h=None):
    L = "_" + tag
    W = HC * 512
    per_load = {"pair": 2, "block": 1, "once": N}[loads]
    RAWS = 2 if loads == "block" else 1
    biased = b2 is not None
    x_now = [sb(f"x_now{i}" + L, [TT, NT, 256], F32) for i in range(2)]
    xt_hi, xt_lo = ([sb(f"{n}{i}" + L, [P, 2, SP1], F32R) for i in range(2)] for n in ("xt_hi", "xt_lo"))
    raw = [sb(f"raw{i}" + L, [P, W + (HC if biased else 0)], F32) for i in range(RAWS)]
    w_hi, w_lo = ([sb(f"{n}{i}" + L, [P, HC, 512], F32R) for i in range(RAWS)] for n in ("w_hi", "w_lo"))
    g = [sb(f"g{i}" + L, [P, SP1], F32) for i in range(2)]
    g_hi, g_lo = ([sb(f"{n}{i}" + L, [P, SP1], F32R) for i in range(4)] for n in ("g_hi", "g_lo"))
    if biased:
        bias, factors, b2_now = sb("bias" + L, [P, HC], F32), sb("factors" + L, [P, HC], F32), sb("b2_now" + L, [TT, 256], F32)
        y_now = [sb(f"y_now{i}" + L, [TT, NT, 256], F32) for i in range(2)]
    turn_ps = [ps(f"turn_ps{i}" + L, [P, 512], F32) for i in range(2)]
    up_ps = [ps(f"up_ps{i}" + L, [P, 512], F32) for i in range(2)]
    y_ps = [[ps(f"y_ps{i}{k}" + L, [P, 512], F32) for k in range(2)] for i in range(2)]

    raw_loaded = [sem(f"raw_loaded{i}" + L) for i in range(RAWS)]
    x_loaded = [sem(f"x_loaded{i}" + L) for i in range(2)]
    y_stored = [sem(f"y_stored{i}" + L) for i in range(2)]
    b2_loaded, factors_set, pads_zeroed = sem("b2_loaded" + L), sem("factors_set" + L), sem("pads_zeroed" + L)
    w_high, w_low, turned, xt_high, xt_low = (sem(n + L) for n in ("w_high", "w_low", "turned", "xt_high", "xt_low"))
    up_filled, act_done, g_high, g_low = (sem(n + L) for n in ("up_filled", "act_done", "g_high", "g_low"))
    down_done, y_taken = sem("down_done" + L), sem("y_taken" + L)

    def walk(eng, step):
        def at(n, k, par):
            if loads == "pair":
                step(n, k, par, k, par == 0, par == 1)
            elif loads == "block":
                step(n, k, par, n, True, True)
            else:
                step(n, k, par, 0, isinstance(n, int) and n == 0, False)

        at(0, 0, 0)
        with eng.Fori(0, (N - 3) // 2) as i:
            at(2 * i + 1, i, 1)
            at(2 * i + 2, i + 1, 0)
        for n in range(1 + 2 * ((N - 3) // 2), N):
            at(n, n // 2, n % 2)

    turns_at = {HC - 4: (0, 1), HC - 2: (2,)}

    with nc.Block() as block:

        @block.sync
        def _(sp):
            def load_weights(e, r):
                sp.dma_start(raw[r][:], packed[bass.ds(e, 1), :, 0:W + (HC if biased else 0)]
                             .rearrange("e p w -> p (e w)")).then_inc(raw_loaded[r], 16)

            def expert_of(n):
                return sp.value_load(source.expert[0:1, bass.ds(n, 1)], min_val=0, max_val=source.experts - 1)

            def load_b2(e):
                sp.dma_start(b2_now[:], b2[bass.ds(e, 1), :].rearrange("e d -> (e d)").partition_broadcast(TT))\
                    .then_inc(b2_loaded, 16)

            def put(n, par):
                sp.wait_ge(y_taken, 6 + 2 * n + 2)
                move(sp, source.to(sp, n), y_now[par], y_stored[par])

            load_weights(expert_of(0) if loads == "block" else 0, 0)
            for n in range(2):
                move(sp, x_now[n], source.rows(sp, n), x_loaded[n])
            if loads == "block":
                load_weights(expert_of(1), 1)
            if biased:
                load_b2(expert_of(0) if loads == "block" else 0)

            def step(n, k, par, load, is_first, is_last):
                fixed = isinstance(n, int)
                if not (fixed and n + 2 >= N):
                    rows = source.rows(sp, n + 2)
                    if loads == "block":
                        e = expert_of(n + 2)
                        sp.wait_ge(w_low, HC * RAWS + HC * (n + 1))
                        load_weights(e, par)
                    sp.wait_ge(turned, 6 + NT * (n + 1))
                    move(sp, x_now[par], rows, x_loaded[par])
                if not (fixed and n == 0) and biased:
                    e = expert_of(n) if loads == "block" else load
                    put(n - 1, 1 - par)
                    if is_first:
                        load_b2(e)
                if loads == "pair" and is_first and not (fixed and load + 1 >= N // 2):
                    sp.wait_ge(w_low, HC * (load + 2))
                    load_weights(load + 1, 0)

            walk(sp, step)
            if biased:
                put(N - 1, (N - 1) % 2)
                for par in range(2):
                    sp.wait_ge(y_stored[par], BOTH + BOTH * ((N + 1 - par) // 2))

        @block.gpsimd
        def _(pool):
            if biased:
                pool.memset(factors[:], factor).then_inc(factors_set, 1)
                pool.wait_ge(factors_set, 1)
            credit(pool, w_low, HC * RAWS)

            def cut(load, m, r):
                pool.wait_ge(w_high, HC * load + m + 1)
                if biased:
                    pool.tensor_tensor(bias[:, m:m + 1], raw[r][:, W + m:W + m + 1], factors[:, m:m + 1], ALU.mult)
                pool.tensor_tensor(w_lo[r][:, m, :], raw[r][:, 512 * m:512 * m + 512], w_hi[r][:, m, :].bitcast(F32),
                                   ALU.subtract).then_inc(w_low, 1)

            if loads == "block":
                def both(k):
                    for r in range(2):
                        for m in range(HC):
                            cut(2 * k + r, m, r)
                with pool.Fori(0, N // 2) as k:
                    both(k)
                if N % 2:
                    for m in range(HC):
                        cut(N - 1, m, 0)
            elif loads == "pair":
                with pool.Fori(0, N // 2) as load:
                    for m in range(HC):
                        cut(load, m, 0)
            else:
                for m in range(HC):
                    cut(0, m, 0)

        @block.tensor
        def _(pe):
            pe.wait_ge(pads_zeroed, 1)
            credit(pe, turned, 6)

            def turn(n, k, par, tiles):
                for i in tiles:
                    if i == 0:
                        pe.wait_ge(x_loaded[par], BOTH * (k + 1))
                    pe.wait_ge(xt_low, NT * n + i + 1)
                    for a in range(2):
                        got = pe.transpose(turn_ps[(par + i) % 2][:, TT * a:TT * a + TT],
                                           x_now[par][:, i, P * a:P * a + P], c.ident[0:TT, 0:TT])
                    got.then_inc(turned, 1)

            def up(n, par, load, m):
                pe.wait_ge(w_low, HC * RAWS + HC * load + m + 1)
                if m == 0:
                    pe.wait_ge(xt_low, 2 + NT * (n + 1))
                pe.wait_ge(act_done, HC * n + m + 1)
                for a in range(2):
                    for j, (w, x) in enumerate(((w_hi, xt_hi), (w_lo, xt_hi), (w_hi, xt_lo))):
                        got = pe.matmul(up_ps[m % 2][:, 0:SP1], w[par % RAWS][:, m, P * a:P * a + P], x[par][:, a, :],
                                        start=(a == 0 and j == 0), stop=(a == 1 and j == 2))
                got.then_inc(up_filled, 1)

            def down(n, par, m):
                pe.wait_ge(g_low, 2 + HC * n + m + 1)
                if m == 0:
                    pe.wait_ge(y_taken, 2 * n + 4)
                for i in range(NT):
                    out = y_ps[par][i // 2][0:TT, 256 * (i % 2):256 * (i % 2) + 256]
                    t = slice(TT * i, TT * i + TT)
                    for j, (x, w) in enumerate(((g_hi, w_hi), (g_lo, w_hi), (g_hi, w_lo))):
                        got = pe.matmul(out, x[m % 4][:, t], w[par % RAWS][:, m, 256:512], start=(m == 0 and j == 0 and i != 1),
                                        stop=(m == HC - 1 and j == 2), skip_group_check=True)
                got.then_inc(down_done, 1)

            turn(0, 0, 0, range(NT))

            def step(n, k, par, load, is_first, is_last):
                fixed = isinstance(n, int)
                for m in range(0, HC, 2):
                    up(n, par, load, m)
                    up(n, par, load, m + 1)
                    if not (fixed and n + 1 >= N):
                        turn(n + 1, k + par, 1 - par, turns_at.get(m, ()))
                    if m > 0:
                        down(n, par, m - 2)
                        down(n, par, m - 1)
                    elif not (fixed and n == 0):
                        down(n - 1, 1 - par, HC - 2)
                        down(n - 1, 1 - par, HC - 1)

            walk(pe, step)
            down(N - 1, (N - 1) % 2, HC - 2)
            down(N - 1, (N - 1) % 2, HC - 1)

        @block.scalar
        def _(act):
            credit(act, act_done, 2)

            def high(n, par, tiles):
                for i in tiles:
                    act.wait_ge(turned, 6 + NT * n + i + 1)
                    act.copy(xt_hi[par][:, :, TT * i:TT * i + TT],
                             turn_ps[(par + i) % 2][:, 0:2 * TT].rearrange("p (a t) -> p a t", a=2)).then_inc(xt_high, 1)

            def activate(n, m):
                act.wait_ge(g_low, HC * n + m + 1)
                act.wait_ge(up_filled, HC * n + m + 1)
                act.activation(g[m % 2][:, 0:SP1], up_ps[m % 2][:, 0:SP1], func, scale=factor,
                               **({"bias": bias[:, m:m + 1]} if biased else {})).then_inc(act_done, 1)

            act.wait_ge(pads_zeroed, 1)

            def cut(m, k, r, last_block):
                if m == 0:
                    act.wait_ge(raw_loaded[r], 16 * (k + 1))
                if last_block is not None:
                    act.wait_ge(down_done, HC * last_block + m + 1)
                act.copy(w_hi[r][:, m, :], raw[r][:, 512 * m:512 * m + 512]).then_inc(w_high, 1)

            cut(0, 0, 0, None)
            high(0, 0, range(NT))
            for m in range(1, HC):
                cut(m, 0, 0, None)

            def step(n, k, par, load, is_first, is_last):
                fixed = isinstance(n, int)
                for m in range(0, HC, 2):
                    activate(n, m)
                    activate(n, m + 1)
                    if not (fixed and n + 1 >= N):
                        high(n + 1, 1 - par, turns_at.get(m, ()))
                    for c in (m, m + 1):
                        if loads == "block" and not (fixed and n + 1 >= N):
                            cut(c, k + par, 1 - par, None if fixed and n == 0 else n - 1)
                        if loads == "pair" and is_last and m >= 4 and not (fixed and n + 1 >= N):
                            cut(c - 4, load + 1, 0, n)
                        if loads == "pair" and is_first and m < 4 and not (fixed and n == 0):
                            cut(HC - 4 + c, None, 0, n - 1)

            walk(act, step)

        @block.vector
        def _(dve):
            for z in (*xt_hi, *xt_lo):
                ins = dve.memset(z[:].bitcast(F32), 0.0)
            ins.then_inc(pads_zeroed, 1)
            credit(dve, xt_low, 2)
            credit(dve, g_low, 2)
            credit(dve, y_taken, 6)
            if biased:
                for par in range(2):
                    credit(dve, y_stored[par], BOTH)

            def low(n, par, tiles):
                for i in tiles:
                    dve.wait_ge(xt_high, NT * n + i + 1)
                    t = slice(TT * i, TT * i + TT)
                    dve.tensor_tensor(xt_lo[par][:, :, t],
                                      turn_ps[(par + i) % 2][:, 0:2 * TT].rearrange("p (a t) -> p a t", a=2),
                                      xt_hi[par][:, :, t].bitcast(F32), ALU.subtract).then_inc(xt_low, 1)

            def cut(n, m):
                dve.wait_ge(act_done, 2 + HC * n + m + 1)
                dve.tensor_copy(g_hi[m % 4][:], g[m % 2][:]).then_inc(g_high, 1)
                dve.wait_ge(g_high, HC * n + m + 1)
                dve.tensor_tensor(g_lo[m % 4][:], g[m % 2][:], g_hi[m % 4][:].bitcast(F32), ALU.subtract).then_inc(g_low, 1)

            def take(n, k, par, load):
                dve.wait_ge(down_done, HC * (n + 1))
                if biased:
                    dve.wait_ge(b2_loaded, 16 * (load + 1))
                    dve.wait_ge(y_stored[par], BOTH * (k + 1))
                for b, tiles in ((0, 2), (1, 1)):
                    src = y_ps[par][b][0:TT, 0:256 * tiles].rearrange("p (t d) -> p t d", d=256)
                    if biased:
                        ins = dve.scalar_tensor_tensor(y_now[par][:, 2 * b:2 * b + tiles, :], src, 1.0 / factor,
                                                       b2_now[:].unsqueeze(1).to_broadcast([TT, tiles, 256]),
                                                       ALU.mult, ALU.add)
                    else:
                        rows = h[:, bass.ds(NT * n + 2 * b, tiles), :]
                        ins = dve.tensor_tensor(rows, rows, src, ALU.add)
                    ins.then_inc(y_taken, 1)

            low(0, 0, range(NT))

            def step(n, k, par, load, is_first, is_last):
                fixed = isinstance(n, int)
                for m in range(0, HC, 2):
                    cut(n, m)
                    cut(n, m + 1)
                    if not (fixed and n + 1 >= N):
                        low(n + 1, 1 - par, turns_at.get(m, ()))
                    if m == 0 and not (fixed and n == 0):
                        take(n - 1, k - 1 + par, 1 - par, load - 1 if is_first and loads != "once" else load)

            walk(dve, step)
            last = N - 1
            take(last, last // 2, last % 2, last // per_load)


class ExpertRows:

    def __init__(self, table):
        self.table, self.experts = table, table.experts
        self.expert = table.expert if table.blocks else None

    def rows(self, sp, n):
        at = S * n
        if self.table.blocks:
            at = sp.value_load(self.table.row[0:1, bass.ds(n, 1)], min_val=0,
                               max_val=self.table.experts * self.table.region)
        return self.table.x_rows[bass.ds(at, S), :].rearrange("(p t) d -> p t d", t=NT)

    def to(self, sp, n):
        return self.table.y_rows[bass.ds(S * n, S), :].rearrange("(p t) d -> p t d", t=NT)


class TokenRows:

    def __init__(self, tokens):
        self.tokens = tokens

    def rows(self, sp, n):
        return self.tokens[:, bass.ds(NT * n, NT), :]


def combine(nc, sb, ps, sem, h, table, B, out):
    L = "_c"
    K = 2
    slot = [sb(f"slot{i}" + L, [TT, NT, K], I32) for i in range(2)]
    weight = [sb(f"weight{i}" + L, [TT, K, NT], F32) for i in range(2)]
    y = [[sb(f"y{i}{k}" + L, [TT, NT, 256], F32) for k in range(K)] for i in range(2)]
    part, total = ([sb(f"{n}{i}" + L, [TT, NT, 256], F32) for i in range(2)] for n in ("part", "total"))
    slots_set, weight_set, slots_seen = sem("slots_set" + L), sem("weight_set" + L), sem("slots_seen" + L)
    gathered, stored = ([sem(f"{n}{i}" + L) for i in range(2)] for n in ("gathered", "stored"))
    step, summed = sem("step" + L), sem("summed" + L)

    with nc.Block() as block:

        @block.sync
        def _(sp):
            with sp.Fori(0, B // 2) as i:
                for par in range(2):
                    sp.wait_ge(summed, 2 * i + par + 1 + 2)
                    move(sp, out[bass.ds(2 * i + par, 1)].rearrange("b (t p) d -> p (b t) d", p=TT), total[par],
                         stored[par])
            for par in range(2):
                sp.wait_ge(stored[par], BOTH * (B // 2) + BOTH)

        @block.gpsimd
        def _(pool):
            with pool.Fori(0, B // 2) as i:
                for par in range(2):
                    pool.wait_ge(slots_set, 2 * i + par + 1)
                    pool.sem_inc(slots_seen, 1)
                    for t in range(NT):
                        for k in range(K):
                            pool.indirect_dma_start(y[par][k][:, t, :], None, table.y_rows,
                                                    bass.IndirectOffsetOnAxis(ap=slot[par][:, t, k:k + 1], axis=0))\
                                .then_inc(gathered[par], 16)

        @block.vector
        def _(dve):
            credit(dve, summed, 2)
            for par in range(2):
                credit(dve, stored[par], BOTH)

            def point(n, par):
                for k in range(K):
                    dve.tensor_copy(weight[par][:, k], table.weight[:, k, bass.ds(NT * n, NT)]).then_inc(weight_set, 1)
                    ins = dve.tensor_copy(slot[par][:, :, k], table.slots[:, k, bass.ds(NT * n, NT)])
                ins.then_inc(slots_set, 1)

            def add(n, i, par):
                dve.wait_ge(gathered[par], 16 * NT * K * (i + 1))
                rows = h[:, bass.ds(NT * n, NT), :]
                w = [weight[par][:, k].unsqueeze(2).to_broadcast([TT, NT, 256]) for k in range(K)]
                dve.wait_ge(weight_set, 2 * n + 2)
                dve.wait_ge(summed, n + 2)
                dve.tensor_tensor(part[0][:], y[par][0][:], w[0], ALU.mult)
                dve.tensor_tensor(part[1][:], y[par][1][:], w[1], ALU.mult).then_inc(step, 1)
                dve.wait_ge(step, 2 * n + 1)
                dve.tensor_tensor(part[0][:], part[0][:], part[1][:], ALU.add).then_inc(step, 1)
                dve.wait_ge(step, 2 * n + 2)
                dve.wait_ge(stored[par], BOTH * i + BOTH)
                dve.tensor_tensor(total[par][:], part[0][:], rows, ALU.add).then_inc(summed, 1)

            point(0, 0)
            point(1, 1)
            with dve.Fori(0, B // 2 - 1) as i:
                for par in range(2):
                    add(2 * i + par, i, par)
                    point(2 * i + par + 2, par)
            for par in range(2):
                add(B - 2 + par, B // 2 - 1, par)


class Constants:

    def __init__(self, sb, sem):
        self.ident, self.ident_bf = sb("ident", [P, P], F32), sb("ident_bf", [TT, TT], BF16)
        self.zeroed, self.made, self.ready = sem("ident_zeroed"), sem("ident_made"), sem("constants_ready")

    def make(self, nc):
        with nc.Block() as block:
            @block.gpsimd
            def _(pool):
                for m in (self.ident, self.ident_bf):
                    pool.memset(m[:], 0.0).then_inc(self.zeroed, 1)
                pool.wait_ge(self.zeroed, 2)
                for m, n in ((self.ident, P), (self.ident_bf, TT)):
                    pool.affine_select(out=m[:], in_=m[:], compare_op=ALU.not_equal, fill=1.0, base=0,
                                       pattern=[[-1, n]], channel_multiplier=1).then_inc(self.made, 1)
                pool.wait_ge(self.made, 2)
                pool.sem_inc(self.ready, 1)


def program(nc, x, txt, scharr, w_dq, w_uq, w_dkv, w_uk, w_uv, w_o, w_sw, b_sw, f_w, f_b1, f_b2,
            wqT, wkT, wvT, rope_cos, rope_sin, m_w, w_g, b_g, e_w, e_b1, e_b2, out):
    with ExitStack() as whole:
        def sem(name):
            return whole.enter_context(nc.semaphore(name))

        def stage(step, *args):
            semaphores = []

            def own_sem(name):
                semaphores.append(nc.alloc_semaphore(name))
                return semaphores[-1]

            with ExitStack() as own:
                step(nc, lambda n, s, d: own.enter_context(nc.sbuf_tensor(n, s, d)),
                     lambda n, s, d: own.enter_context(nc.psum_tensor(n, s, d)), own_sem, *args)
            nc.clear_and_free_semaphores(semaphores)
            nc.all_engine_barrier()

        whole_sb = lambda n, s, d: whole.enter_context(nc.sbuf_tensor(n, s, d))
        B = x.shape[0]
        h = whole_sb("h", [TT, NT * B, 256], F32)
        c = Constants(whole_sb, sem)
        c.make(nc)
        stage(load_and_cut_image, x, txt, scharr, h)
        cap = B * S // f_b1.shape[0]
        own = f_b1.shape[0] * cap
        switch = Table(nc, whole_sb, "switch", f_b1.shape[0], cap, cap, own, own + B * S, 1, NT * B)
        region = (B + 1) * S
        top = Table(nc, whole_sb, "top2", e_b1.shape[0], region, 0, 0, e_b1.shape[0] * region + S, 2, NT * B,
                    blocks=2 * B + e_b1.shape[0] - 1)
        with nc.sbuf_tensor("ao", [TT, NT * B, 256], F32) as ao:
            stage(attention, 0, c, h, ao, B, (w_dq, w_dkv, w_uq, w_uk, w_uv), switch)
            stage(dispatch, 0, c, h, ao, B, w_o, w_sw, b_sw, switch)
        stage(feed_forward, "e0", c, 2 * f_b1.shape[0], 8, "pair", ACT.Gelu, np.sqrt(2.0) / 1.41421, f_w, f_b2,
              ExpertRows(switch), True)
        with nc.sbuf_tensor("ao1", [TT, NT * B, 256], F32) as ao:
            stage(attention, 1, c, h, ao, B, (wqT, wkT, wvT, rope_cos, rope_sin), switch)
            stage(feed_forward, "mlp", c, B, 8, "once", ACT.Silu, 1.0, m_w, None, TokenRows(ao), False, h)
        stage(dispatch, 1, c, h, None, B, None, w_g, b_g, top)
        stage(feed_forward, "e1", c, top.blocks, 4, "block", ACT.Gelu, 1.0, e_w, e_b2, ExpertRows(top), True)
        stage(combine, h, top, B, out)


def pack(w1, w2, b1=None):
    E, D, F = w1.shape
    up = w1.reshape(E, 2, P, F // P, P).transpose(0, 2, 3, 1, 4).reshape(E, P, F // P, 2 * P)
    down = w2.reshape(E, F // P, P, D).transpose(0, 2, 1, 3)
    both = np.concatenate([up, down], axis=3).reshape(E, P, F * 4)
    return both if b1 is None else np.concatenate([both, b1.reshape(E, F // P, P).transpose(0, 2, 1)], axis=2)


def rope_tables():
    half = 8
    inv_freq = (np.float32(1.0) / np.float32(10000.0) ** (np.arange(0, 2 * half, 2, dtype=np.float32) / np.float32(2 * half)))
    freqs = (np.arange(S, dtype=np.float32)[:, None] * inv_freq[None, :].astype(np.float32)).astype(np.float32)
    cos, sin = np.cos(freqs), np.sin(freqs)
    return [np.ascontiguousarray(t.reshape(NT, TT, 2 * half).transpose(1, 0, 2).astype(np.float32))
            for t in (np.concatenate([cos, cos], 1), np.concatenate([-sin, sin], 1))]


def lay_out(v):
    v = {k: np.asarray(a) for k, a in v.items()}
    cos, sin = rope_tables()
    return {
        "x": v["x"], "txt": v["txt"], "scharr": v["L0_tok_scharr"], "w_dq": v["L0_attn_W_dq"],
        "w_uq": v["L0_attn_W_uq"], "w_dkv": v["L0_attn_W_dkv"], "w_uk": v["L0_attn_W_uk"], "w_uv": v["L0_attn_W_uv"],
        "w_o": v["L0_attn_W_o"], "w_sw": v["L0_ffn_W_sw"], "b_sw": v["L0_ffn_b_sw"],
        "f_w": pack(v["L0_ffn_W1"], v["L0_ffn_W2"], v["L0_ffn_b1"]), "f_b1": v["L0_ffn_b1"], "f_b2": v["L0_ffn_b2"],
        "wqT": v["L1_attn_Wq"].T, "wkT": v["L1_attn_Wk"].T, "wvT": v["L1_attn_Wv"].T, "rope_cos": cos, "rope_sin": sin,
        "m_w": pack(v["L1_attn_W1"].T[None], v["L1_attn_W2"].T[None]), "w_g": v["L1_ffn_Wg"], "b_g": v["L1_ffn_bg"],
        "e_w": pack(v["L1_ffn_W1"], v["L1_ffn_W2"], v["L1_ffn_b1"]), "e_b1": v["L1_ffn_b1"], "e_b2": v["L1_ffn_b2"],
    }


_OUTS = [((16, S, 256), 'float32')]


def kernel(**inputs):
    import numpy as _np
    import concourse.bacc as _bacc
    from concourse import mybir as _mybir
    from concourse.bass_utils import run_bass_kernel_spmd as _run

    nc = _bacc.Bacc("TRN2", target_bir_lowering=False, num_devices=1)
    arrays, args = {}, []
    for name, a in lay_out(inputs).items():
        a = _np.ascontiguousarray(a)
        arrays[f"in_{name}_dram"] = a
        args.append(nc.dram_tensor(f"in_{name}_dram", a.shape, _mybir.dt.from_np(a.dtype), kind="ExternalInput").ap())
    for i, (shape, dtype) in enumerate(_OUTS):
        dt = _mybir.dt.from_np(_np.dtype(dtype))
        args.append(nc.dram_tensor(f"out_{i}_dram", shape, dt, kind="ExternalOutput").ap())
    program(nc, *args)
    r = _run(nc, [arrays], core_ids=[0])
    return r.results[0]["out_0_dram"]
```
